# Optimizing a Trainium2 kernel written in Bass

```python
import numpy as np
import jax
import jax.numpy as jnp

def _softmax(x, axis=-1):
    return jax.nn.softmax(x, axis=axis)

def _gelu(x):
    return jax.nn.gelu(x, approximate=True)

def _silu(x):
    return jax.nn.silu(x)

def _sigmoid(x):
    return jax.nn.sigmoid(x)

def _layernorm(x, axis=-1, eps=1e-05):
    m = jnp.mean(x, axis=axis, keepdims=True)
    v = jnp.var(x, axis=axis, keepdims=True)
    return (x - m) / jnp.sqrt(v + eps)

def _scatter_add(tgt, idx, src, axis=0):
    return tgt.at[idx].add(src)

def _segment_sum(src, seg, n):
    return jax.ops.segment_sum(src, seg, n)
kernel_name = 'mk_gnn_resnorm_d4_gnn_r32_627f73'

def setup_inputs(seed: int=0):
    np.random.seed(seed)
    _w = jnp.asarray

    def _rec_inputs():
        import jax
        import jax.numpy as jnp
        _gk = jax.random.key(seed)
        x = -0.0005121 + 1.001 * jax.random.normal(jax.random.fold_in(_gk, 1), (50000, 160), jnp.float32)
        src = jax.random.randint(jax.random.fold_in(_gk, 2), (25000,), 0, 50000, jnp.int32)
        dst = jax.random.randint(jax.random.fold_in(_gk, 3), (25000,), 0, 50000, jnp.int32)
        _o = jnp.argsort(dst, stable=True)
        src = src[_o]
        dst = dst[_o]
        edge_attr_10 = jax.random.uniform(jax.random.fold_in(_gk, 12), (25000, 10), jnp.float32, 0.0, 1)
        edge_attr_16 = jax.random.uniform(jax.random.fold_in(_gk, 13), (25000, 16), jnp.float32, 0.0, 1)
        edge_attr_3 = 0.00047201 + 1.00023 * jax.random.normal(jax.random.fold_in(_gk, 14), (25000, 3), jnp.float32)
        edge_attr_4 = 0.000898722 + 1.00012 * jax.random.normal(jax.random.fold_in(_gk, 15), (25000, 4), jnp.float32)
        edge_attr_64 = 0.000127647 + 1.00004 * jax.random.normal(jax.random.fold_in(_gk, 16), (25000, 64), jnp.float32)
        node_vec1 = jax.random.uniform(jax.random.fold_in(_gk, 18), (50000, 1), jnp.float32, 0.0, 1)
        return (x, src, dst, edge_attr_10, edge_attr_16, edge_attr_3, edge_attr_4, edge_attr_64, node_vec1)
    x, src, dst, edge_attr_10, edge_attr_16, edge_attr_3, edge_attr_4, edge_attr_64, node_vec1 = _rec_inputs()

    def _L0_gnn_setup():
        import jax, jax.numpy as jnp
        import numpy as np
        N, E = (625, 10000)
        CS, CV = (64, 32)
        AS_, AV, H = (16, 8, 4)
        NB = 16
        SQRT3 = 1.7320508075688772
        SQRT2 = 1.4142135623730951
        EPS = 1e-05

        def _cg_tp(s, v, y0, y1, w_ss, w_sv, w_vs, w_vv0, w_vv1):
            out_s = jnp.concatenate([w_ss * s * y0[:, None], w_vv0 * (jnp.einsum('eci,ei->ec', v, y1) / SQRT3)], axis=-1)
            out_v = jnp.concatenate([(w_sv * s)[:, :, None] * y1[:, None, :], (w_vs * jnp.ones_like(v[..., 0]))[..., None] * v * y0[:, None, None], (w_vv1 * jnp.ones_like(v[..., 0]))[..., None] * (jnp.cross(v, y1[:, None, :]) / SQRT2)], axis=1)
            return (out_s, out_v)

        def _equiv_layernorm(s, v, gamma_s, beta_s, gamma_v):
            mu = jnp.mean(s, axis=-1, keepdims=True)
            var = jnp.var(s, axis=-1, keepdims=True)
            s_n = (s - mu) * jax.lax.rsqrt(var + EPS) * gamma_s + beta_s
            rms = jnp.sqrt(jnp.mean(jnp.sum(v * v, axis=-1), axis=-1, keepdims=True) + EPS)
            v_n = v / rms[..., None] * gamma_v[None, :, None]
            return (s_n, v_n)
        key = jax.random.key(seed)
        ks = jax.random.split(key, 26)

        def rn(k, shape, fan):
            return jax.random.normal(k, shape, jnp.float32) / np.sqrt(fan)
        D1S, D1V = (CS + CV, CS + 2 * CV)
        WN = 2 * CS + 3 * CV
        inp = {'node': jax.random.normal(ks[0], (N, CS + 3 * CV), jnp.float32), 'edge_index': jax.random.randint(ks[1], (2, E), 0, N, jnp.int64 if jax.config.jax_enable_x64 else jnp.int32), 'rbf': jax.random.uniform(ks[2], (E, NB), jnp.float32), 'rsh': jax.random.normal(ks[3], (E, 4), jnp.float32), 'gamma_s': jnp.ones((CS,), jnp.float32), 'beta_s': jnp.zeros((CS,), jnp.float32), 'gamma_v': jnp.ones((CV,), jnp.float32), 'Ws_src': rn(ks[4], (CS, CS), CS), 'Wv_src': rn(ks[5], (CV, CV), CV), 'Ws_dst': rn(ks[6], (CS, CS), CS), 'Wv_dst': rn(ks[7], (CV, CV), CV), 'W_rbf': rn(ks[8], (NB, WN), NB), 'W_alpha': rn(ks[9], (D1S, H * AS_), D1S), 'alpha_dot': rn(ks[10], (1, H, AS_), AS_), 'Ws_val': rn(ks[11], (D1S, CS), D1S), 'Wv_val': rn(ks[12], (D1V, CV), D1V), 'Wg': rn(ks[13], (CS, CV), CS), 'w2_ss': rn(ks[14], (CS,), 1), 'w2_sv': rn(ks[15], (CS,), 1), 'w2_vs': rn(ks[16], (CV,), 1), 'w2_vv0': rn(ks[17], (CV,), 1), 'w2_vv1': rn(ks[18], (CV,), 1), 'Ws_vlin': rn(ks[19], (D1S, H * AS_), D1S), 'Wv_vlin': rn(ks[20], (D1V, H * AV), D1V), 'Wps': rn(ks[21], (H * AS_, CS), H * AS_), 'Wpv': rn(ks[22], (H * AV, CV), H * AV)}
        return inp
    _L0_gnn_all = _L0_gnn_setup()
    _L0_gnn_in = {k: v for k, v in _L0_gnn_all.items() if k in ('gamma_s', 'beta_s', 'gamma_v', 'Ws_src', 'Wv_src', 'Ws_dst', 'Wv_dst', 'W_rbf', 'W_alpha', 'alpha_dot', 'Ws_val', 'Wv_val', 'Wg', 'w2_ss', 'w2_sv', 'w2_vs', 'w2_vv0', 'w2_vv1', 'Ws_vlin', 'Wv_vlin', 'Wps', 'Wpv')}
    del _L0_gnn_all

    def _L1_gnn_setup():
        import jax, jax.numpy as jnp
        import numpy as np
        N, E = (1250, 20000)
        S_IN, V_IN = (64, 32)
        S_MID, V_MID = (96, 128)
        S_OUT, V_OUT = (96, 32)
        R = 64
        FC_HID = 64
        W_NUMEL = 64 + 64 + 32 + 32 + 32
        NUM_NEIGHBORS = 16.0

        def _inv(d):
            return 1.0 / jnp.sqrt(jnp.float32(d))

        def _forward(node_features, node_attr, edge_attr, edge_scalars, lin1_ws, lin1_wv, fc_w1, fc_w2, sc_ws, sc_wv, lin2_ws, lin2_wv, edge_src, edge_dst):
            n = node_features.shape[0]
            s = node_features[:, :S_IN]
            v = node_features[:, S_IN:].reshape(n, V_IN, 3)
            a = node_attr
            sc_s = s @ sc_ws * a * _inv(S_IN)
            sc_v = jnp.einsum('nci,cd->ndi', v, sc_wv) * a[:, :, None] * _inv(V_IN)
            h_s = s @ lin1_ws * a * _inv(S_IN)
            h_v = jnp.einsum('nci,cd->ndi', v, lin1_wv) * a[:, :, None] * _inv(V_IN)
            hid = jax.nn.silu(edge_scalars @ fc_w1 * _inv(R))
            w = hid @ fc_w2 * _inv(FC_HID)
            w1, w2, w3, w4, w5 = jnp.split(w, [64, 128, 160, 192], axis=-1)
            es = h_s[edge_src]
            ev = h_v[edge_src]
            e0 = edge_attr[:, :1]
            e1 = edge_attr[:, 1:4]
            m_s1 = w1 * es * e0
            m_s2 = w4 * jnp.einsum('eci,ei->ec', ev, e1) * _inv(3)
            m_v1 = (w2 * es)[:, :, None] * e1[:, None, :]
            m_v2 = w3[:, :, None] * ev * e0[:, :, None]
            m_v3 = w5[:, :, None] * jnp.cross(ev, e1[:, None, :]) * _inv(2)
            mid_s = jnp.concatenate([m_s1, m_s2], axis=-1)
            mid_v = jnp.concatenate([m_v1, m_v2, m_v3], axis=1)
            inv_nn = 1.0 / jnp.sqrt(jnp.float32(NUM_NEIGHBORS))
            agg_s = jax.ops.segment_sum(mid_s, edge_dst, num_segments=n) * inv_nn
            agg_v = jax.ops.segment_sum(mid_v, edge_dst, num_segments=n) * inv_nn
            o_s = agg_s @ lin2_ws * a * _inv(S_MID)
            o_v = jnp.einsum('nci,cd->ndi', agg_v, lin2_wv) * a[:, :, None] * _inv(V_MID)
            pre_s = sc_s + o_s
            pre_v = sc_v + o_v
            scalars = jax.nn.silu(pre_s[:, :64])
            gates = jax.nn.sigmoid(pre_s[:, 64:96])
            gated = gates[:, :, None] * pre_v
            return jnp.concatenate([scalars, gated.reshape(n, 3 * V_OUT)], axis=-1)
        key = jax.random.key(seed)
        ks = jax.random.split(key, 13)
        return {'node_features': jax.random.normal(ks[0], (N, S_IN + 3 * V_IN), jnp.float32), 'node_attr': jnp.ones((N, 1), jnp.float32), 'edge_src': jax.random.randint(ks[1], (E,), 0, N), 'edge_dst': jax.random.randint(ks[2], (E,), 0, N), 'edge_attr': jax.random.normal(ks[3], (E, 4), jnp.float32), 'edge_scalars': jax.random.normal(ks[4], (E, R), jnp.float32), 'lin1_ws': jax.random.normal(ks[5], (S_IN, S_IN), jnp.float32), 'lin1_wv': jax.random.normal(ks[6], (V_IN, V_IN), jnp.float32), 'fc_w1': jax.random.normal(ks[7], (R, FC_HID), jnp.float32), 'fc_w2': jax.random.normal(ks[8], (FC_HID, W_NUMEL), jnp.float32), 'sc_ws': jax.random.normal(ks[9], (S_IN, S_OUT), jnp.float32), 'sc_wv': jax.random.normal(ks[10], (V_IN, V_OUT), jnp.float32), 'lin2_ws': jax.random.normal(ks[11], (S_MID, S_OUT), jnp.float32), 'lin2_wv': jax.random.normal(ks[12], (V_MID, V_OUT), jnp.float32)}
    _L1_gnn_all = _L1_gnn_setup()
    _L1_gnn_in = {k: v for k, v in _L1_gnn_all.items() if k in ('lin1_ws', 'lin1_wv', 'fc_w1', 'fc_w2', 'sc_ws', 'sc_wv', 'lin2_ws', 'lin2_wv')}
    del _L1_gnn_all

    def _L2_gnn_setup():
        import jax, jax.numpy as jnp
        import numpy as np
        N_NODES = 50000
        N_EDGES = 25000
        MUL0, MUL1 = (64, 32)
        N_BASIS, N_RADIAL = (10, 100)
        W_NUMEL = 192
        NUM_NEIGHBORS = 16.0
        INV_SQRT3 = np.float32(1.0 / np.sqrt(3.0))
        RELU_GAIN = np.float32(np.sqrt(2.0))
        FAN_L2 = np.float32(np.sqrt(MUL0 + MUL1))

        def _fctp_scalar_attr(x0, x1, a, W0, W1):
            o0 = x0 @ W0 * a * (1.0 / np.sqrt(W0.shape[0]))
            o1 = jnp.einsum('nud,uw->nwd', x1, W1) * a[..., None] * (1.0 / np.sqrt(W1.shape[0]))
            return (o0, o1)
        key = jax.random.key(seed)
        ks = jax.random.split(key, 16)
        return {'node_input': jax.random.normal(ks[0], (N_NODES, MUL0 + 3 * MUL1), jnp.float32), 'node_attr': jnp.ones((N_NODES, 1), jnp.float32), 'edge_attr': jax.random.normal(ks[1], (N_EDGES, 4), jnp.float32), 'edge_length_embedded': jax.random.uniform(ks[2], (N_EDGES, N_BASIS), dtype=jnp.float32), 'W_si0': jax.random.normal(ks[3], (MUL0, MUL0), jnp.float32), 'W_si1': jax.random.normal(ks[4], (MUL1, MUL1), jnp.float32), 'W_l1_0': jax.random.normal(ks[5], (MUL0, MUL0), jnp.float32), 'W_l1_1': jax.random.normal(ks[6], (MUL1, MUL1), jnp.float32), 'W_l2_00': jax.random.normal(ks[7], (MUL0, MUL0), jnp.float32), 'W_l2_10': jax.random.normal(ks[8], (MUL1, MUL0), jnp.float32), 'W_l2_01': jax.random.normal(ks[9], (MUL0, MUL1), jnp.float32), 'W_l2_11': jax.random.normal(ks[10], (MUL1, MUL1), jnp.float32), 'W_fc1': jax.random.normal(ks[11], (N_BASIS, N_RADIAL), jnp.float32), 'W_fc2': jax.random.normal(ks[12], (N_RADIAL, W_NUMEL), jnp.float32), 'edge_src': jax.random.randint(ks[13], (N_EDGES,), 0, N_NODES), 'edge_dst': jax.random.randint(ks[14], (N_EDGES,), 0, N_NODES)}
    _L2_gnn_all = _L2_gnn_setup()
    _L2_gnn_in = {k: v for k, v in _L2_gnn_all.items() if k in ('W_si0', 'W_si1', 'W_l1_0', 'W_l1_1', 'W_l2_00', 'W_l2_10', 'W_l2_01', 'W_l2_11', 'W_fc1', 'W_fc2')}
    del _L2_gnn_all

    def _L3_gnn_setup():
        import jax, jax.numpy as jnp
        import numpy as np
        N_NODES = 10000
        N_EDGES = 10000
        MUL0, MUL1 = (64, 32)
        EDGE_DIM = 64
        W_NUMEL = 224
        DENOM = 32.0
        SQRT3 = 3.0 ** 0.5
        INV_SQRT3 = 1.0 / SQRT3
        INV_SQRT2 = 2.0 ** (-0.5)

        def _forward(node_feature, edge_attr, edge_feature, W_skip0, W_skip1, W_nl0, W_nl1, W_fc1, W_fc2, W_out_s, W_out_v, edge_index):
            N = node_feature.shape[0]
            E = edge_attr.shape[0]
            s = node_feature[:, :MUL0]
            v = node_feature[:, MUL0:].reshape(N, MUL1, 3)
            skip_s = s @ W_skip0
            skip_v = jnp.einsum('nmi,mk->nki', v, W_skip1)
            s = s @ W_nl0
            v = jnp.einsum('nmi,mk->nki', v, W_nl1)
            rhat = edge_attr / jnp.linalg.norm(edge_attr, axis=-1, keepdims=True)
            sh1 = SQRT3 * rhat
            w = jax.nn.relu(edge_feature @ W_fc1) @ W_fc2
            w0, w1, w2, w3, w4 = jnp.split(w, [64, 128, 160, 192], axis=-1)
            src, dst = (edge_index[0], edge_index[1])
            xs = s[dst]
            xv = v[dst]
            out0a = w0 * xs
            out0b = w3 * (jnp.einsum('emi,ei->em', xv, sh1) * INV_SQRT3)
            out1a = (w1 * xs)[:, :, None] * sh1[:, None, :]
            out1b = w2[:, :, None] * xv
            out1c = w4[:, :, None] * (jnp.cross(xv, sh1[:, None, :]) * INV_SQRT2)
            tp = jnp.concatenate([out0a, out0b, out1a.reshape(E, -1), out1b.reshape(E, -1), out1c.reshape(E, -1)], axis=-1)
            agg = jax.ops.segment_sum(tp, src, num_segments=N) / DENOM
            agg_s = agg[:, :96]
            agg_v = agg[:, 96:].reshape(N, 128, 3)
            out_s = agg_s @ W_out_s + skip_s
            out_v = jnp.einsum('nmi,mk->nki', agg_v, W_out_v) + skip_v
            fs = jax.nn.silu(out_s[:, :MUL0])
            gate = jax.nn.sigmoid(out_s[:, MUL0:MUL0 + 32])
            gv = gate[:, :, None] * out_v
            return jnp.concatenate([fs, gv.reshape(N, -1)], axis=-1)
        key = jax.random.key(seed)
        ks = jax.random.split(key, 12)

        def lin(k, fi, fo):
            return jax.random.normal(k, (fi, fo), jnp.float32) / np.float32(np.sqrt(fi))
        return {'node_feature': jax.random.normal(ks[0], (N_NODES, MUL0 + 3 * MUL1), jnp.float32), 'edge_attr': jax.random.normal(ks[1], (N_EDGES, 3), jnp.float32), 'edge_feature': jax.random.normal(ks[2], (N_EDGES, EDGE_DIM), jnp.float32), 'W_skip0': lin(ks[3], MUL0, 96), 'W_skip1': lin(ks[4], MUL1, 32), 'W_nl0': lin(ks[5], MUL0, MUL0), 'W_nl1': lin(ks[6], MUL1, MUL1), 'W_fc1': lin(ks[7], EDGE_DIM, 64), 'W_fc2': lin(ks[8], 64, W_NUMEL), 'W_out_s': lin(ks[9], 96, 96), 'W_out_v': lin(ks[10], 128, 32), 'edge_index': jax.random.randint(ks[11], (2, N_EDGES), 0, N_NODES)}
    _L3_gnn_all = _L3_gnn_setup()
    _L3_gnn_in = {k: v for k, v in _L3_gnn_all.items() if k in ('W_skip0', 'W_skip1', 'W_nl0', 'W_nl1', 'W_fc1', 'W_fc2', 'W_out_s', 'W_out_v')}
    del _L3_gnn_all
    return {'x': x, 'src': src, 'dst': dst, 'edge_attr_10': edge_attr_10, 'edge_attr_16': edge_attr_16, 'edge_attr_3': edge_attr_3, 'edge_attr_4': edge_attr_4, 'edge_attr_64': edge_attr_64, 'node_vec1': node_vec1, 'L0_gnn_gamma_s': _L0_gnn_in['gamma_s'], 'L0_gnn_beta_s': _L0_gnn_in['beta_s'], 'L0_gnn_gamma_v': _L0_gnn_in['gamma_v'], 'L0_gnn_Ws_src': _L0_gnn_in['Ws_src'], 'L0_gnn_Wv_src': _L0_gnn_in['Wv_src'], 'L0_gnn_Ws_dst': _L0_gnn_in['Ws_dst'], 'L0_gnn_Wv_dst': _L0_gnn_in['Wv_dst'], 'L0_gnn_W_rbf': _L0_gnn_in['W_rbf'], 'L0_gnn_W_alpha': _L0_gnn_in['W_alpha'], 'L0_gnn_alpha_dot': _L0_gnn_in['alpha_dot'], 'L0_gnn_Ws_val': _L0_gnn_in['Ws_val'], 'L0_gnn_Wv_val': _L0_gnn_in['Wv_val'], 'L0_gnn_Wg': _L0_gnn_in['Wg'], 'L0_gnn_w2_ss': _L0_gnn_in['w2_ss'], 'L0_gnn_w2_sv': _L0_gnn_in['w2_sv'], 'L0_gnn_w2_vs': _L0_gnn_in['w2_vs'], 'L0_gnn_w2_vv0': _L0_gnn_in['w2_vv0'], 'L0_gnn_w2_vv1': _L0_gnn_in['w2_vv1'], 'L0_gnn_Ws_vlin': _L0_gnn_in['Ws_vlin'], 'L0_gnn_Wv_vlin': _L0_gnn_in['Wv_vlin'], 'L0_gnn_Wps': _L0_gnn_in['Wps'], 'L0_gnn_Wpv': _L0_gnn_in['Wpv'], 'L1_gnn_lin1_ws': _L1_gnn_in['lin1_ws'], 'L1_gnn_lin1_wv': _L1_gnn_in['lin1_wv'], 'L1_gnn_fc_w1': _L1_gnn_in['fc_w1'], 'L1_gnn_fc_w2': _L1_gnn_in['fc_w2'], 'L1_gnn_sc_ws': _L1_gnn_in['sc_ws'], 'L1_gnn_sc_wv': _L1_gnn_in['sc_wv'], 'L1_gnn_lin2_ws': _L1_gnn_in['lin2_ws'], 'L1_gnn_lin2_wv': _L1_gnn_in['lin2_wv'], 'L2_gnn_W_si0': _L2_gnn_in['W_si0'], 'L2_gnn_W_si1': _L2_gnn_in['W_si1'], 'L2_gnn_W_l1_0': _L2_gnn_in['W_l1_0'], 'L2_gnn_W_l1_1': _L2_gnn_in['W_l1_1'], 'L2_gnn_W_l2_00': _L2_gnn_in['W_l2_00'], 'L2_gnn_W_l2_10': _L2_gnn_in['W_l2_10'], 'L2_gnn_W_l2_01': _L2_gnn_in['W_l2_01'], 'L2_gnn_W_l2_11': _L2_gnn_in['W_l2_11'], 'L2_gnn_W_fc1': _L2_gnn_in['W_fc1'], 'L2_gnn_W_fc2': _L2_gnn_in['W_fc2'], 'L3_gnn_W_skip0': _L3_gnn_in['W_skip0'], 'L3_gnn_W_skip1': _L3_gnn_in['W_skip1'], 'L3_gnn_W_nl0': _L3_gnn_in['W_nl0'], 'L3_gnn_W_nl1': _L3_gnn_in['W_nl1'], 'L3_gnn_W_fc1': _L3_gnn_in['W_fc1'], 'L3_gnn_W_fc2': _L3_gnn_in['W_fc2'], 'L3_gnn_W_out_s': _L3_gnn_in['W_out_s'], 'L3_gnn_W_out_v': _L3_gnn_in['W_out_v']}

def reference(x, src, dst, edge_attr_10, edge_attr_16, edge_attr_3, edge_attr_4, edge_attr_64, node_vec1, L0_gnn_gamma_s, L0_gnn_beta_s, L0_gnn_gamma_v, L0_gnn_Ws_src, L0_gnn_Wv_src, L0_gnn_Ws_dst, L0_gnn_Wv_dst, L0_gnn_W_rbf, L0_gnn_W_alpha, L0_gnn_alpha_dot, L0_gnn_Ws_val, L0_gnn_Wv_val, L0_gnn_Wg, L0_gnn_w2_ss, L0_gnn_w2_sv, L0_gnn_w2_vs, L0_gnn_w2_vv0, L0_gnn_w2_vv1, L0_gnn_Ws_vlin, L0_gnn_Wv_vlin, L0_gnn_Wps, L0_gnn_Wpv, L1_gnn_lin1_ws, L1_gnn_lin1_wv, L1_gnn_fc_w1, L1_gnn_fc_w2, L1_gnn_sc_ws, L1_gnn_sc_wv, L1_gnn_lin2_ws, L1_gnn_lin2_wv, L2_gnn_W_si0, L2_gnn_W_si1, L2_gnn_W_l1_0, L2_gnn_W_l1_1, L2_gnn_W_l2_00, L2_gnn_W_l2_10, L2_gnn_W_l2_01, L2_gnn_W_l2_11, L2_gnn_W_fc1, L2_gnn_W_fc2, L3_gnn_W_skip0, L3_gnn_W_skip1, L3_gnn_W_nl0, L3_gnn_W_nl1, L3_gnn_W_fc1, L3_gnn_W_fc2, L3_gnn_W_out_s, L3_gnn_W_out_v):
    import jax
    import jax.numpy as jnp

    def _L0_gnn_ref(node, rbf, rsh, gamma_s, beta_s, gamma_v, Ws_src, Wv_src, Ws_dst, Wv_dst, W_rbf, W_alpha, alpha_dot, Ws_val, Wv_val, Wg, w2_ss, w2_sv, w2_vs, w2_vv0, w2_vv1, Ws_vlin, Wv_vlin, Wps, Wpv, edge_index):
        import jax, jax.numpy as jnp
        import numpy as np
        N, E = (625, 10000)
        CS, CV = (64, 32)
        AS_, AV, H = (16, 8, 4)
        NB = 16
        SQRT3 = 1.7320508075688772
        SQRT2 = 1.4142135623730951
        EPS = 1e-05

        def _cg_tp(s, v, y0, y1, w_ss, w_sv, w_vs, w_vv0, w_vv1):
            out_s = jnp.concatenate([w_ss * s * y0[:, None], w_vv0 * (jnp.einsum('eci,ei->ec', v, y1) / SQRT3)], axis=-1)
            out_v = jnp.concatenate([(w_sv * s)[:, :, None] * y1[:, None, :], (w_vs * jnp.ones_like(v[..., 0]))[..., None] * v * y0[:, None, None], (w_vv1 * jnp.ones_like(v[..., 0]))[..., None] * (jnp.cross(v, y1[:, None, :]) / SQRT2)], axis=1)
            return (out_s, out_v)

        def _equiv_layernorm(s, v, gamma_s, beta_s, gamma_v):
            mu = jnp.mean(s, axis=-1, keepdims=True)
            var = jnp.var(s, axis=-1, keepdims=True)
            s_n = (s - mu) * jax.lax.rsqrt(var + EPS) * gamma_s + beta_s
            rms = jnp.sqrt(jnp.mean(jnp.sum(v * v, axis=-1), axis=-1, keepdims=True) + EPS)
            v_n = v / rms[..., None] * gamma_v[None, :, None]
            return (s_n, v_n)
        n = node.shape[0]
        e = rsh.shape[0]
        s = node[:, :CS]
        v = node[:, CS:].reshape(n, CV, 3)
        s_n, v_n = _equiv_layernorm(s, v, gamma_s, beta_s, gamma_v)
        src, dst = (edge_index[0], edge_index[1])
        msg_s = (s_n @ Ws_src)[src] + (s_n @ Ws_dst)[dst]
        msg_v = jnp.einsum('ncx,cd->ndx', v_n, Wv_src)[src] + jnp.einsum('ncx,cd->ndx', v_n, Wv_dst)[dst]
        y0, y1 = (rsh[:, 0], rsh[:, 1:4])
        w1 = rbf @ W_rbf
        m1_s, m1_v = _cg_tp(msg_s, msg_v, y0, y1, w1[:, :CS], w1[:, CS:2 * CS], w1[:, 2 * CS:2 * CS + CV], w1[:, 2 * CS + CV:2 * CS + 2 * CV], w1[:, 2 * CS + 2 * CV:])
        a = (m1_s @ W_alpha).reshape(e, H, AS_)
        a = jnp.where(a > 0, a, 0.2 * a)
        a = jnp.sum(a * alpha_dot, axis=-1, keepdims=True)
        amax = jax.ops.segment_max(a, dst, num_segments=n)
        amax = jnp.where(jnp.isfinite(amax), amax, 0.0)
        ex = jnp.exp(a - amax[dst])
        den = jax.ops.segment_sum(ex, dst, num_segments=n)
        alpha = ex / (den[dst] + 1e-16)
        val_s = m1_s @ Ws_val
        val_v = jnp.einsum('ecx,cd->edx', m1_v, Wv_val)
        val_v = val_v * jax.nn.sigmoid(val_s @ Wg)[..., None]
        val_s = jax.nn.sigmoid(val_s)
        m2_s, m2_v = _cg_tp(val_s, val_v, y0, y1, w2_ss, w2_sv, w2_vs, w2_vv0, w2_vv1)
        hs = (m2_s @ Ws_vlin).reshape(e, H, AS_)
        hv = jnp.einsum('ecx,cd->edx', m2_v, Wv_vlin).reshape(e, H, AV, 3)
        h = jnp.concatenate([hs, hv.reshape(e, H, AV * 3)], axis=-1)
        agg = jax.ops.segment_sum(alpha * h, dst, num_segments=n)
        agg_s = agg[:, :, :AS_].reshape(n, H * AS_)
        agg_v = agg[:, :, AS_:].reshape(n, H * AV, 3)
        out = node + jnp.concatenate([agg_s @ Wps, jnp.einsum('ncx,cd->ndx', agg_v, Wpv).reshape(n, CV * 3)], axis=-1)
        return out

    def _L1_gnn_ref(node_features, node_attr, edge_src, edge_dst, edge_attr, edge_scalars, lin1_ws, lin1_wv, fc_w1, fc_w2, sc_ws, sc_wv, lin2_ws, lin2_wv):
        import jax, jax.numpy as jnp
        import numpy as np
        N, E = (1250, 20000)
        S_IN, V_IN = (64, 32)
        S_MID, V_MID = (96, 128)
        S_OUT, V_OUT = (96, 32)
        R = 64
        FC_HID = 64
        W_NUMEL = 64 + 64 + 32 + 32 + 32
        NUM_NEIGHBORS = 16.0

        def _inv(d):
            return 1.0 / jnp.sqrt(jnp.float32(d))

        def _forward(node_features, node_attr, edge_attr, edge_scalars, lin1_ws, lin1_wv, fc_w1, fc_w2, sc_ws, sc_wv, lin2_ws, lin2_wv, edge_src, edge_dst):
            n = node_features.shape[0]
            s = node_features[:, :S_IN]
            v = node_features[:, S_IN:].reshape(n, V_IN, 3)
            a = node_attr
            sc_s = s @ sc_ws * a * _inv(S_IN)
            sc_v = jnp.einsum('nci,cd->ndi', v, sc_wv) * a[:, :, None] * _inv(V_IN)
            h_s = s @ lin1_ws * a * _inv(S_IN)
            h_v = jnp.einsum('nci,cd->ndi', v, lin1_wv) * a[:, :, None] * _inv(V_IN)
            hid = jax.nn.silu(edge_scalars @ fc_w1 * _inv(R))
            w = hid @ fc_w2 * _inv(FC_HID)
            w1, w2, w3, w4, w5 = jnp.split(w, [64, 128, 160, 192], axis=-1)
            es = h_s[edge_src]
            ev = h_v[edge_src]
            e0 = edge_attr[:, :1]
            e1 = edge_attr[:, 1:4]
            m_s1 = w1 * es * e0
            m_s2 = w4 * jnp.einsum('eci,ei->ec', ev, e1) * _inv(3)
            m_v1 = (w2 * es)[:, :, None] * e1[:, None, :]
            m_v2 = w3[:, :, None] * ev * e0[:, :, None]
            m_v3 = w5[:, :, None] * jnp.cross(ev, e1[:, None, :]) * _inv(2)
            mid_s = jnp.concatenate([m_s1, m_s2], axis=-1)
            mid_v = jnp.concatenate([m_v1, m_v2, m_v3], axis=1)
            inv_nn = 1.0 / jnp.sqrt(jnp.float32(NUM_NEIGHBORS))
            agg_s = jax.ops.segment_sum(mid_s, edge_dst, num_segments=n) * inv_nn
            agg_v = jax.ops.segment_sum(mid_v, edge_dst, num_segments=n) * inv_nn
            o_s = agg_s @ lin2_ws * a * _inv(S_MID)
            o_v = jnp.einsum('nci,cd->ndi', agg_v, lin2_wv) * a[:, :, None] * _inv(V_MID)
            pre_s = sc_s + o_s
            pre_v = sc_v + o_v
            scalars = jax.nn.silu(pre_s[:, :64])
            gates = jax.nn.sigmoid(pre_s[:, 64:96])
            gated = gates[:, :, None] * pre_v
            return jnp.concatenate([scalars, gated.reshape(n, 3 * V_OUT)], axis=-1)
        return _forward(node_features, node_attr, edge_attr, edge_scalars, lin1_ws, lin1_wv, fc_w1, fc_w2, sc_ws, sc_wv, lin2_ws, lin2_wv, edge_src, edge_dst)

    def _L2_gnn_ref(node_input, node_attr, edge_src, edge_dst, edge_attr, edge_length_embedded, W_si0, W_si1, W_l1_0, W_l1_1, W_l2_00, W_l2_10, W_l2_01, W_l2_11, W_fc1, W_fc2):
        import jax, jax.numpy as jnp
        import numpy as np
        N_NODES = 50000
        N_EDGES = 25000
        MUL0, MUL1 = (64, 32)
        N_BASIS, N_RADIAL = (10, 100)
        W_NUMEL = 192
        NUM_NEIGHBORS = 16.0
        INV_SQRT3 = np.float32(1.0 / np.sqrt(3.0))
        RELU_GAIN = np.float32(np.sqrt(2.0))
        FAN_L2 = np.float32(np.sqrt(MUL0 + MUL1))

        def _fctp_scalar_attr(x0, x1, a, W0, W1):
            o0 = x0 @ W0 * a * (1.0 / np.sqrt(W0.shape[0]))
            o1 = jnp.einsum('nud,uw->nwd', x1, W1) * a[..., None] * (1.0 / np.sqrt(W1.shape[0]))
            return (o0, o1)
        N = node_input.shape[0]
        x0 = node_input[:, :MUL0]
        x1 = node_input[:, MUL0:].reshape(N, MUL1, 3)
        a = node_attr
        h = jax.nn.relu(edge_length_embedded @ W_fc1 * (1.0 / np.sqrt(N_BASIS))) * RELU_GAIN
        w = h @ W_fc2 * (1.0 / np.sqrt(N_RADIAL))
        w0, w1, w2, w3 = (w[:, :64], w[:, 64:128], w[:, 128:160], w[:, 160:192])
        si0, si1 = _fctp_scalar_attr(x0, x1, a, W_si0, W_si1)
        l0, l1 = _fctp_scalar_attr(x0, x1, a, W_l1_0, W_l1_1)
        y0 = l0[edge_src]
        y1 = l1[edge_src]
        e0 = edge_attr[:, :1]
        e1 = edge_attr[:, 1:4]
        m0 = w0 * y0 * e0
        m1 = (w1 * y0)[:, :, None] * e1[:, None, :]
        m2 = (w2 * e0)[:, :, None] * y1
        m3 = w3 * jnp.einsum('eud,ed->eu', y1, e1) * INV_SQRT3
        inv = np.float32(1.0 / np.sqrt(NUM_NEIGHBORS))
        s0 = jax.ops.segment_sum(m0, edge_dst, num_segments=N) * inv
        s1 = jax.ops.segment_sum(m1, edge_dst, num_segments=N) * inv
        s2 = jax.ops.segment_sum(m2, edge_dst, num_segments=N) * inv
        s3 = jax.ops.segment_sum(m3, edge_dst, num_segments=N) * inv
        o0 = (s0 @ W_l2_00 + s3 @ W_l2_10) * a / FAN_L2
        o1 = (jnp.einsum('nud,uw->nwd', s1, W_l2_01) + jnp.einsum('nud,uw->nwd', s2, W_l2_11)) * a[..., None] / FAN_L2
        out0 = si0 + 0.5 * o0
        out1 = si1 + 0.5 * o1
        return jnp.concatenate([out0, out1.reshape(N, 3 * MUL1)], axis=1)

    def _L3_gnn_ref(node_feature, edge_attr, edge_feature, W_skip0, W_skip1, W_nl0, W_nl1, W_fc1, W_fc2, W_out_s, W_out_v, edge_index):
        import jax, jax.numpy as jnp
        import numpy as np
        N_NODES = 10000
        N_EDGES = 10000
        MUL0, MUL1 = (64, 32)
        EDGE_DIM = 64
        W_NUMEL = 224
        DENOM = 32.0
        SQRT3 = 3.0 ** 0.5
        INV_SQRT3 = 1.0 / SQRT3
        INV_SQRT2 = 2.0 ** (-0.5)

        def _forward(node_feature, edge_attr, edge_feature, W_skip0, W_skip1, W_nl0, W_nl1, W_fc1, W_fc2, W_out_s, W_out_v, edge_index):
            N = node_feature.shape[0]
            E = edge_attr.shape[0]
            s = node_feature[:, :MUL0]
            v = node_feature[:, MUL0:].reshape(N, MUL1, 3)
            skip_s = s @ W_skip0
            skip_v = jnp.einsum('nmi,mk->nki', v, W_skip1)
            s = s @ W_nl0
            v = jnp.einsum('nmi,mk->nki', v, W_nl1)
            rhat = edge_attr / jnp.linalg.norm(edge_attr, axis=-1, keepdims=True)
            sh1 = SQRT3 * rhat
            w = jax.nn.relu(edge_feature @ W_fc1) @ W_fc2
            w0, w1, w2, w3, w4 = jnp.split(w, [64, 128, 160, 192], axis=-1)
            src, dst = (edge_index[0], edge_index[1])
            xs = s[dst]
            xv = v[dst]
            out0a = w0 * xs
            out0b = w3 * (jnp.einsum('emi,ei->em', xv, sh1) * INV_SQRT3)
            out1a = (w1 * xs)[:, :, None] * sh1[:, None, :]
            out1b = w2[:, :, None] * xv
            out1c = w4[:, :, None] * (jnp.cross(xv, sh1[:, None, :]) * INV_SQRT2)
            tp = jnp.concatenate([out0a, out0b, out1a.reshape(E, -1), out1b.reshape(E, -1), out1c.reshape(E, -1)], axis=-1)
            agg = jax.ops.segment_sum(tp, src, num_segments=N) / DENOM
            agg_s = agg[:, :96]
            agg_v = agg[:, 96:].reshape(N, 128, 3)
            out_s = agg_s @ W_out_s + skip_s
            out_v = jnp.einsum('nmi,mk->nki', agg_v, W_out_v) + skip_v
            fs = jax.nn.silu(out_s[:, :MUL0])
            gate = jax.nn.sigmoid(out_s[:, MUL0:MUL0 + 32])
            gv = gate[:, :, None] * out_v
            return jnp.concatenate([fs, gv.reshape(N, -1)], axis=-1)
        return _forward(node_feature, edge_attr, edge_feature, W_skip0, W_skip1, W_nl0, W_nl1, W_fc1, W_fc2, W_out_s, W_out_v, edge_index)
    edge_index = jnp.stack([src, dst])
    x = _layernorm(x + _L0_gnn_ref(x, edge_attr_16, edge_attr_4, L0_gnn_gamma_s, L0_gnn_beta_s, L0_gnn_gamma_v, L0_gnn_Ws_src, L0_gnn_Wv_src, L0_gnn_Ws_dst, L0_gnn_Wv_dst, L0_gnn_W_rbf, L0_gnn_W_alpha, L0_gnn_alpha_dot, L0_gnn_Ws_val, L0_gnn_Wv_val, L0_gnn_Wg, L0_gnn_w2_ss, L0_gnn_w2_sv, L0_gnn_w2_vs, L0_gnn_w2_vv0, L0_gnn_w2_vv1, L0_gnn_Ws_vlin, L0_gnn_Wv_vlin, L0_gnn_Wps, L0_gnn_Wpv, edge_index), axis=-1)
    x = _layernorm(x + _L1_gnn_ref(x, node_vec1, src, dst, edge_attr_4, edge_attr_64, L1_gnn_lin1_ws, L1_gnn_lin1_wv, L1_gnn_fc_w1, L1_gnn_fc_w2, L1_gnn_sc_ws, L1_gnn_sc_wv, L1_gnn_lin2_ws, L1_gnn_lin2_wv), axis=-1)
    x = _layernorm(x + _L2_gnn_ref(x, node_vec1, src, dst, edge_attr_4, edge_attr_10, L2_gnn_W_si0, L2_gnn_W_si1, L2_gnn_W_l1_0, L2_gnn_W_l1_1, L2_gnn_W_l2_00, L2_gnn_W_l2_10, L2_gnn_W_l2_01, L2_gnn_W_l2_11, L2_gnn_W_fc1, L2_gnn_W_fc2), axis=-1)
    x = _layernorm(x + _L3_gnn_ref(x, edge_attr_3, edge_attr_64, L3_gnn_W_skip0, L3_gnn_W_skip1, L3_gnn_W_nl0, L3_gnn_W_nl1, L3_gnn_W_fc1, L3_gnn_W_fc2, L3_gnn_W_out_s, L3_gnn_W_out_v, edge_index), axis=-1)
    return x

_drawn_inputs = setup_inputs


def setup_inputs(seed=0):
    import zlib

    import numpy as np

    out = dict(_drawn_inputs(seed))
    spreads = {'L0_gnn_gamma_s': (1.0, 0.6), 'L0_gnn_beta_s': (0.0, 0.8), 'L0_gnn_gamma_v': (1.0, 0.6)}
    factors = {'edge_attr_10': 8.0,
     'edge_attr_3': 8.0,
     'edge_attr_64': 3.164,
     'L0_gnn_W_alpha': 3.352,
     'L0_gnn_alpha_dot': 3.29,
     'L1_gnn_lin1_ws': 4.101,
     'L1_gnn_lin1_wv': 4.706,
     'L1_gnn_fc_w1': 3.357,
     'L1_gnn_fc_w2': 3.182,
     'L1_gnn_lin2_ws': 4.906,
     'L1_gnn_lin2_wv': 4.155,
     'L2_gnn_W_l1_0': 5.652,
     'L2_gnn_W_l1_1': 7.761,
     'L2_gnn_W_l2_00': 8.0,
     'L2_gnn_W_l2_10': 8.0,
     'L2_gnn_W_l2_01': 7.068,
     'L2_gnn_W_l2_11': 8.0,
     'L2_gnn_W_fc1': 5.723,
     'L2_gnn_W_fc2': 4.972,
     'L3_gnn_W_nl0': 8.0,
     'L3_gnn_W_nl1': 8.0,
     'L3_gnn_W_fc1': 8.0,
     'L3_gnn_W_fc2': 7.65,
     'L3_gnn_W_out_s': 8.0,
     'L3_gnn_W_out_v': 8.0}
    for name, (base, spread) in spreads.items():
        noise = np.random.default_rng([zlib.crc32(name.encode()), seed]).standard_normal(out[name].shape)
        drawn = base * np.exp(spread * noise) if base else spread * noise
        out[name] = jnp.asarray(drawn.astype(out[name].dtype))
    for name, factor in factors.items():
        out[name] = (out[name] * factor).astype(out[name].dtype)
    return out
```

```python
from contextlib import ExitStack

import concourse.bass as bass
from concourse import mybir

F32 = mybir.dt.float32
BF16 = mybir.dt.bfloat16
I32 = mybir.dt.int32
ALU = mybir.AluOpType
ACT = mybir.ActivationFunctionType
AX = mybir.AxisListType

P = 128
N, E = 50000, 25000
S, V, H = 64, 32, 4
V3, C = 3 * V, S + 3 * V
HS, HV = S // H, V // H
Q = 4
GRP = Q * P
NJ = 392
NP = P * NJ
NG = NJ // Q
EG = 50
EP = EG * GRP
ET = EP // P
XW = 164
TW = 192
EPS = 1e-5
BIG = float(1 << 20)
NEG = -1.0e30

A64, A4, A10, A16, A3, ASRC, ADST, AW = 0, 64, 68, 78, 94, 97, 98, 100

K_ID, K_TRI, K_TRIU, K_ONE, K_IOTA = 0, 128, 256, 384, 512
K_PIDX = K_IOTA + NJ
K_LAST = K_PIDX + 1
K_HALF = K_LAST + 1
KW = K_HALF + 16


def weight_plan():
    plan, at = {}, 0
    def put(name, rows, cols):
        nonlocal at
        plan[name] = (rows, at, cols)
        at += cols
    for L, (hs, at_rows, hid, sw) in enumerate(((128, 36, 0, 160), (128, 68, 64, 96), (128, 14, 100, 64), (64, 68, 64, 96))):
        put(f"hs{L}", hs, P)
        put(f"hv{L}", V3, V3)
        if L == 0:
            put("hvd0", V3, V3)
        else:
            put(f"fc{L}", at_rows, hid)
        put(f"eb{L}", at_rows, V3)
        k = hid or at_rows
        put(f"wab{L}", k, P)
        put(f"w3{L}", k, V3)
        put(f"w4{L}", k, V3)
        if L != 2:
            put(f"w5{L}", k, V3)
            put(f"od{L}", V3, V3)
        put(f"oab{L}", P, sw + V)
        put(f"of{L}", V3, sw)
        put(f"oc{L}", V3, V3)
        if L:
            put(f"ns{L}", S, 64 if L == 2 else 96)
            put(f"nv{L}", V3, V3)
    put("o2s", V3, 160)
    put("o2v", V3, 192)
    put("fs", S, S)
    put("fv", V3, V3)
    put("vst", S, S)
    put("vst2", S, V3)
    put("wg", S, V)
    put("adot", P, S)
    put("cols", P, 8)
    return plan, at


PLAN, WW = weight_plan()


def build(nc, x_in, attr_in, keys_in, w_in, wscale_in, const_in, out, stop_after=4):
    with ExitStack() as ctx:
        def sb(name, shape, dt=F32):
            return ctx.enter_context(nc.sbuf_tensor("sb_" + name, shape, dt))

        sems = {}

        def sem(name):
            sems[name] = ctx.enter_context(nc.semaphore(name))
            return sems[name]

        x_a = nc.dram_tensor("x_a", (NP, XW), F32).ap()
        x_b = nc.dram_tensor("x_b", (NP, XW), F32).ap()
        agg_dst = nc.dram_tensor("agg_dst", (NP, TW), F32).ap()
        agg_src = nc.dram_tensor("agg_src", (NP, TW), F32).ap()
        by_dst = nc.dram_tensor("by_dst", (EP + GRP, AW), F32).ap()
        by_src = nc.dram_tensor("by_src", (EP + GRP, AW), F32).ap()

        w = sb("w", [P, WW])
        con = sb("con", [P, KW])
        ident = con[:, K_ID:K_ID + P]
        ones = con[:, K_ONE:K_ONE + P]
        iota = con[:, K_IOTA:K_IOTA + NJ]
        ident_b = sb("ident_b", [P, P], BF16)

        def W(name, r0=0, r1=None, c0=0, c1=None):
            rows, at, cols = PLAN[name]
            return w[r0:(rows if r1 is None else r1), at + c0:at + (cols if c1 is None else c1)]

        def col(k, rows=P):
            at = PLAN["cols"][1] + k
            return w[0:rows, at:at + 1]

        F = [ctx.enter_context(nc.psum_tensor(f"ps_f{k}", [P, 512], F32)) for k in range(4)]
        O = ctx.enter_context(nc.psum_tensor("ps_o", [P, Q, 512], F32))

        M = sb("M", [P, 2, Q, TW])
        G = sb("G", [P, 2, Q, TW])
        KC = sb("KC", [P, 2, Q])
        MC = sb("MC", [P, 2, Q, H])
        MF = sb("MF", [H, 2, GRP])
        KR = sb("KR", [H, 2, GRP + 1])
        MK = sb("MK", [H, GRP + 1])
        YO = sb("YO", [P, 2, Q, XW])

        room = ExitStack()

        def tmp(name, shape, dt=F32):
            return room.enter_context(nc.sbuf_tensor("sb_" + name, shape, dt))

        keys_i = tmp("keys_i", [P, 2, ET], I32)
        part_i = tmp("part_i", [P, 2, 2, ET], I32)
        key_f = tmp("key_f", [P, 2, ET])
        lo_f = tmp("lo_f", [P, 2, ET])
        hi_f = tmp("hi_f", [P, 2, ET])
        oh_hi = tmp("oh_hi", [P, 2, 2, NJ], BF16)
        oh_lo = tmp("oh_lo", [P, 2, 2, P], BF16)
        cnt = tmp("cnt", [P, 2, NJ])
        inc = tmp("inc", [P, 2, NJ])
        onesj = tmp("onesj", [P, NJ])
        bcol = tmp("bcol", [P, 2])
        off = tmp("off", [P, 2, 2, NJ])
        offi = tmp("offi", [P, 2, NJ])
        dg = tmp("dg", [P, 2, 2, 2, P])
        oht = tmp("oht", [P, 2, 2, P])
        gj = tmp("gj", [P, NJ])
        gt = tmp("gt", [P, P])
        pos = tmp("pos", [P, 2, 2, 2])
        pos_i = tmp("pos_i", [P, 2, 2], I32)
        rowt = tmp("rowt", [P, 2, AW])
        XG_w = tmp("wscale", [P, WW])[:, :]
        cnt_m1_t = tmp("cnt_m1", [1, AW])
        cnt_m1 = cnt_m1_t[0:1, :]
        zeros = tmp("zeros", [P, 14 * TW])
        room.close()

        A = sb("A", [P, 2, Q, AW])
        knext = sb("knext", [P, 2, Q])
        XG = sb("XG", [P, 2, Q, S + XW])
        XD = sb("XD", [P, 2, Q, XW])
        XN = sb("XN", [P, Q, 2 * C])
        XSQ = sb("XSQ", [P, Q, 2, C])
        STAT = sb("STAT", [P, 2, 2, Q, 2])
        RST = sb("RST", [P, 2, 2, Q, 2])
        RB = sb("RB", [P, 2, Q, 36])
        XTs = sb("XTs", [P, 2, GRP])
        XTv = sb("XTv", [P, 2, GRP])
        XTd = sb("XTd", [P, GRP])
        AT = sb("AT", [P, 2, GRP])
        HID = sb("HID", [P, 2, GRP])
        HSG = sb("HSG", [P, GRP])
        S2 = sb("S2", [P, 2, GRP])
        VT = sb("VT", [P, 2, GRP])
        VE = sb("VE", [P, 2, GRP])
        P1 = sb("P1", [P, 2, GRP])
        P3 = sb("P3", [P, 2, GRP])
        P4 = sb("P4", [P, 2, GRP])
        P5 = sb("P5", [P, 2, GRP])
        ER = sb("ER", [P, 2, Q, 5])
        DX = sb("DX", [P, 2, Q, 160])
        C1 = sb("C1", [P, 2, Q, V3])
        C2 = sb("C2", [P, 2, Q, V3])
        U = sb("U", [P, 2, Q, V3])
        MSG = sb("MSG", [P, 2, Q, TW])
        SEL = sb("SEL", [P, 2, Q, P])
        CAR = sb("CAR", [P, 2, Q, P])
        KP = sb("KP", [P, 2, Q])
        KN = sb("KN", [P, 2, Q])
        IDX = sb("IDX", [P, 2, Q], I32)
        SM3 = sb("SM3", [P, 2, Q, 3])
        LA = sb("LA", [P, Q, S])
        SG = sb("SG", [P, Q, V3])
        VV = sb("VV", [P, Q, V3])
        AE = sb("AE", [P, Q, H])
        AET = sb("AET", [H, GRP])
        MB = sb("MB", [H, GRP])
        RES = sb("RES", [P, H])
        MPS = sb("MPS", [P, TW])
        HS1 = sb("HS1", [P, Q, S])
        DEN = sb("DEN", [P, Q, H])
        MN = sb("MN", [P, Q, C])
        TA = sb("TA", [P, GRP])
        TV = sb("TV", [P, GRP])
        XN_in = sb("XN_in", [P, 2, Q, XW])
        GN = sb("GN", [P, 2, Q, TW])
        T1 = sb("T1", [P, 2, Q, TW])
        SIG = sb("SIG", [P, 2, Q, V3])
        Y = sb("Y", [P, 2, Q, C])
        BN = sb("BN", [P, 2, Q, 6])
        MV = sb("MV", [P, 2, Q, 2])
        RS = sb("RS", [P, 2, Q])
        NM = sb("NM", [P, 2, Q])

        def wait(eng, semaphore, value):
            if not isinstance(value, int) or value > 0:
                eng.wait_ge(semaphore, value)

        loaded = sem("loaded")
        zeroed = sem("zeroed")
        setup_done = {n: sem("setup_" + n) for n in ("dve", "pe")}
        tables_zero = sem("tables_zero")
        row_ready = [sem("row_ready0"), sem("row_ready1")]
        next_ready = [sem("next_ready0"), sem("next_ready1")]
        gathered = [sem("gathered0"), sem("gathered1")]
        scattered = [sem("scattered0"), sem("scattered1")]
        node_in = [sem("node_in0"), sem("node_in1")]
        stored = [sem("stored0"), sem("stored1")]
        gate = sem("gate")

        ALL, CONV, CROSS, ZERO, L12 = (0, 1, 2, 3), (1, 2, 3), (0, 1, 3), (0,), (1, 2)
        USES = {}

        def events(layers, *names):
            for name in names:
                USES[name] = layers
                sem(name)

        events(ALL, "p_xts", "p_xtv", "p_at", "p_hs", "p_hv", "p_eb", "p_wab", "p_w3", "p_w4", "p_key",
               "p_out", "p_sum", "a_xts", "a_xtv", "a_at", "a_s2", "a_v", "a_sum", "d_ve", "d_p1",
               "d_p3", "d_p4", "d_keys", "d_kp", "d_car", "d_idx", "d_er", "d_tb1", "d_v1", "d_kc")
        events(CONV, "p_hid", "a_hid", "a_msg_s")
        events(L12, "l_se")
        events((1,), "a_sig")
        events((3,), "d_sq", "l_rn")
        events(CROSS, "p_w5", "d_p5", "a_dx1", "l_c1", "d_w1")
        events(ZERO, "p_xtd", "a_xtd", "d_mean", "d_cent", "a_sq", "d_var", "l_rstd", "d_xn", "l_rb",
               "a_tanh", "l_sg", "a_la", "d_la", "l_la", "d_ae", "d_gate", "d_dot",
               "p_ta", "p_tv", "p_ae", "a_ta", "a_tv", "a_ae", "a_kr", "d_mk", "d_mf", "d_mb", "p_mc",
               "a_mc", "d_sub", "a_exp", "d_res", "a_res", "d_mps", "p_out2", "a_hs", "d_hs", "a_dx2",
               "l_c2", "d_tb2", "d_w2", "d_v2", "d_msg", "d_rden", "d_mn",
               "p_fs", "p_fv", "a_fs", "a_fv", "p_g")
        def base(name, L):
            return EG * sum(1 for k in USES[name] if k < L)

        def on(eng, name, L, i, u, per=1, k=0):
            wait(eng, sems[name], i * (2 * per) + (base(name, L) * per + u * per + k + 1))

        def before(eng, name, L, i, u, per=1):
            wait(eng, sems[name], i * (2 * per) + (base(name, L) * per + u * per))

        for name in ("n_xts", "n_xtv", "n_exts", "n_extv", "n_lin", "n_t", "n_ta", "n_sig", "n_sg2",
                     "n_yv", "n_y", "n_bn", "n_mv", "n_rs", "n_nm", "n_out"):
            sem(name)

        def onn(eng, name, k, i, u, back=0):
            wait(eng, sems[name], i * 2 + (NG * k + u + 1 - back))

        X_OF = (x_in, x_a, x_b, x_a)
        X_TO = (x_a, x_b, x_a, out)
        A_OF = (by_dst, by_dst, by_dst, by_src)
        KEY = (ADST, ADST, ADST, ASRC)
        OTHER = (ASRC, ASRC, ASRC, ADST)
        TABLE = (agg_dst, agg_dst, agg_dst, agg_src)
        SW = (96, 96, 64, 96)
        MW = (164, 192, 160, 192)
        MAT = (0, 320, 256, 320)
        HIDK = (0, 64, 100, 64)
        ATR = (36, 68, 14, 68)
        ATC = (0, A64, A4, A64)
        HSK = (128, 128, 128, 64)

        def stores_before(eng, L):
            for u in range(2):
                if L:
                    eng.wait_ge(stored[u], 16 * (NG // 2) * L)
                else:
                    eng.wait_ge(row_out[u], 32 * HT)
            if not L:
                eng.wait_ge(c_upd, ET)

        def scatters_before(eng, L):
            for u in range(2):
                eng.wait_ge(scattered[u], 16 * Q * (EG // 2) * (L + 1))

        def loop(eng, count, body):
            for u in range(2):
                body(0, u)
            with eng.Fori(1, count) as i:
                for u in range(2):
                    body(i, u)

        def loop_ahead(eng, count, body):
            for u in range(2):
                body(0, u, True)
            with eng.Fori(1, count - 1) as i:
                for u in range(2):
                    body(i, u, True)
            for u in range(2):
                body(count - 1, u, u == 0)

        def bx(ap):
            return ap.unsqueeze(2).broadcast_to([ap.shape[0], ap.shape[1], 3, ap.shape[2]])

        def bd(ap, n=V):
            return ap.unsqueeze(3).broadcast_to([ap.shape[0], ap.shape[1], ap.shape[2], n])

        def xd(ap, n=3):
            return ap.rearrange("p q (x d) -> p q x d", x=n)

        count_step = sem("count_step")
        CAST, COPY, SCAN, BASE, EXCL, FIRST_PLACE = 2, 6, 8, 9, 11, 13
        c_hot, c_cnt, c_base, c_seed, c_dg, c_row, c_oht, c_offs, c_g, c_upd, c_hot2, c_posi, c_chk = (
            sem(k) for k in ("one_hots", "counted", "key_base", "places_seeded", "diagonals", "key_rows", "one_hots_turned",
                             "places_copied", "places_read", "places_moved", "one_hots_again", "positions", "position_parts"))
        row_in = [sem("row_in0"), sem("row_in1")]
        row_out = [sem("row_out0"), sem("row_out1")]
        HT = ET // 2

        def prep_sync(sp):
            sp.dma_start(w[:, :], w_in).then_inc(loaded, 16)
            sp.dma_start(con[:, :], const_in).then_inc(loaded, 16)
            sp.dma_start(XG_w, wscale_in).then_inc(loaded, 16)
            sp.dma_start(keys_i[:, :, :], keys_in).then_inc(loaded, 16)
            sp.wait_ge(zeroed, 1)
            for table in (agg_dst, agg_src):
                flat = table.rearrange("(p j) c -> p (j c)", p=P)
                for k in range(NJ // 14):
                    sp.dma_start(flat[:, k * 14 * TW:(k + 1) * 14 * TW], zeros[:, :]).then_inc(tables_zero, 16)
            for table in (by_dst, by_src):
                sp.dma_start(table[EP:EP + 1, :], cnt_m1).then_inc(tables_zero, 16)

            def load_row(i, u):
                wait(sp, row_out[u], i * 32)
                sp.dma_start(rowt[:, u, :], attr_in.rearrange("(t p) c -> t p c", p=P)[i * 2 + u]).then_inc(row_in[u], 16)
            loop(sp, HT, load_row)


        def prep_vector(dve):
            dve.memset(cnt_m1, -1.0)
            dve.memset(zeros[:, :], 0.0).then_inc(zeroed, 1)
            dve.memset(onesj[:, :], 1.0)
            dve.memset(M[:, :, :, :], 0.0)
            dve.memset(G[:, :, :, :], 0.0)
            dve.memset(KC[:, :, :], -1.0)
            dve.memset(MC[:, :, :, :], 0.0)
            dve.memset(MF[:, :, :], 0.0)
            dve.memset(KR[:, :, :], -1.0)
            dve.memset(MK[:, :], 0.0)
            dve.memset(YO[:, :, :, :], 0.0)
            dve.wait_ge(loaded, 64)
            dve.tensor_tensor(w[:, :], w[:, :], XG_w, ALU.mult).then_inc(setup_done["dve"], 1)
            dve.tensor_copy(ident_b[:, :], ident).then_inc(setup_done["dve"], 1)
            dve.wait_ge(setup_done["dve"], 2)
            for name, c0, c1, factor in (("o2s", 0, S, 3), ("o2s", S, S + V, 6), ("o2s", S + V, 160, 3), ("o2v", 0, V3, 4), ("o2v", V3, 192, 5)):
                dve.tensor_scalar(W(name, c0=c0, c1=c1), W(name, c0=c0, c1=c1), col(factor, V3), None, ALU.mult).then_inc(setup_done["dve"], 1)
            dve.wait_ge(setup_done["pe"], 1)
            dve.tensor_copy(W("oab0", r1=S, c0=P, c1=P + V), F[0][0:S, 0:V]).then_inc(setup_done["dve"], 1)
            dve.tensor_copy(W("of0", c0=P, c1=P + V), F[0][0:V3, V:2 * V]).then_inc(setup_done["dve"], 1)
            for r in range(2):
                dve.tensor_scalar(part_i[:, r, 0, :], keys_i[:, r, :], 7, None, ALU.arith_shift_right)
                dve.tensor_scalar(part_i[:, r, 1, :], keys_i[:, r, :], 127, None, ALU.bitwise_and).then_inc(count_step, 1)
            dve.wait_ge(count_step, CAST)
            for r in range(2):
                dve.tensor_copy(key_f[:, r, :], keys_i[:, r, :])
                dve.tensor_copy(hi_f[:, r, :], part_i[:, r, 0, :])
                dve.tensor_copy(lo_f[:, r, :], part_i[:, r, 1, :]).then_inc(count_step, 1)
            dve.wait_ge(count_step, 4)
            def count(i, u):
                wait(dve, c_cnt, i * 2 + (u - 1))
                for r in range(2):
                    dve.tensor_scalar(oh_hi[:, u, r, :], iota, hi_f[:, r, bass.ds(i * 2 + u, 1)], None, ALU.is_equal)
                    ins = dve.tensor_scalar(oh_lo[:, u, r, :], con[:, K_IOTA:K_IOTA + P], lo_f[:, r, bass.ds(i * 2 + u, 1)], None, ALU.is_equal)
                ins.then_inc(c_hot, 1)
            loop(dve, HT, count)

            dve.wait_ge(c_cnt, ET)
            for r in range(2):
                dve.tensor_copy(cnt[:, r, :], F[r][:, 0:NJ]).then_inc(count_step, 1)
            dve.wait_ge(count_step, COPY)
            for r in range(2):
                dve.tensor_tensor_scan(inc[:, r, :], onesj[:, :], cnt[:, r, :], 0.0, ALU.mult, ALU.add).then_inc(count_step, 1)
            dve.wait_ge(c_base, 1)
            dve.tensor_copy(bcol[:, :], F[2][:, 0:2]).then_inc(count_step, 1)
            dve.wait_ge(count_step, SCAN)
            for r in range(2):
                dve.tensor_tensor(offi[:, r, :], inc[:, r, :], cnt[:, r, :], ALU.subtract).then_inc(count_step, 1)
            dve.wait_ge(count_step, EXCL)
            for r in range(2):
                dve.tensor_scalar(off[:, 1, r, :], offi[:, r, :], bcol[:, r:r + 1], None, ALU.add).then_inc(count_step, 1)

            def place(i, u):
                t = i * 2 + u
                wait(dve, c_upd, t - 1)
                for r in range(2):
                    dve.tensor_scalar(dg[:, u, r, 0, :], ident, key_f[:, r, bass.ds(t, 1)], None, ALU.mult)
                    ins = dve.tensor_scalar(dg[:, u, r, 1, :], ident, lo_f[:, r, bass.ds(t, 1)], None, ALU.mult)
                ins.then_inc(c_dg, 1)
                for r in range(2):
                    dve.tensor_scalar(oh_hi[:, u, r, :], iota, hi_f[:, r, bass.ds(t, 1)], None, ALU.is_equal)
                    ins = dve.tensor_scalar(oh_lo[:, u, r, :], con[:, K_IOTA:K_IOTA + P], lo_f[:, r, bass.ds(t, 1)], None, ALU.is_equal)
                ins.then_inc(c_hot2, 1)
                dve.wait_ge(c_row, t + 1)
                for r in range(2):
                    ins = dve.tensor_scalar(oht[:, u, r, :], F[2][:, r * 256 + P:r * 256 + 256], con[:, K_PIDX:K_PIDX + 1], None, ALU.is_equal)
                ins.then_inc(c_oht, 1)
                for r in range(2):
                    dve.scalar_tensor_tensor(gt[:, :], F[2][:, r * 256:r * 256 + P], key_f[:, r, bass.ds(t, 1)],
                                             con[:, K_TRI:K_TRI + P], ALU.is_equal, ALU.mult,
                                             accum_out=pos[:, u, r, 0:1]).then_inc(c_chk, 1)
                    dve.wait_ge(c_chk, i * 8 + (u * 4 + r + 1))
                dve.wait_ge(c_hot2, t + 1)
                dve.wait_ge(c_g, t + 1)
                for r in range(2):
                    dve.scalar_tensor_tensor(gj[:, :], O[:, 2 + r, 0:NJ], 1.0, oh_hi[:, u, r, :], ALU.mult, ALU.mult,
                                             accum_out=pos[:, u, r, 1:2]).then_inc(c_chk, 1)
                    dve.wait_ge(c_chk, i * 8 + (u * 4 + r + 3))
                wait(dve, row_out[u], i * 32)
                dve.tensor_tensor(pos_i[:, u, :], pos[:, u, :, 0], pos[:, u, :, 1], ALU.add).then_inc(c_posi, 1)
            loop(dve, HT, place)

        def prep_tensor(pe):
            pe.wait_ge(setup_done["dve"], 2)
            pe.matmul(F[0][0:S, 0:V], W("vst"), W("wg"), start=True, stop=True)
            pe.matmul(F[0][0:V3, V:2 * V], W("vst2"), W("wg"), start=True, stop=True).then_inc(setup_done["pe"], 1)
            pe.wait_ge(setup_done["dve"], 9)
            pe.wait_ge(zeroed, 1)
            for r in range(2):
                pe.matmul(F[r][:, 0:NJ], ident_b[:, :], zeros_b[:, 0:NJ], start=True, stop=False, skip_group_check=True)

            def count(i, u):
                pe.wait_ge(c_hot, i * 2 + (u + 1))
                for r in range(2):
                    ins = pe.matmul(F[r][:, 0:NJ], oh_lo[:, u, r, :], oh_hi[:, u, r, :], start=False, stop=False, skip_group_check=True)
                ins.then_inc(c_cnt, 1)
            loop(pe, HT, count)

            pe.wait_ge(count_step, SCAN)
            for r in range(2):
                ins = pe.matmul(F[2][:, r:r + 1], con[:, K_TRIU:K_TRIU + P], inc[:, r, NJ - 1:NJ], start=True, stop=True)
            ins.then_inc(c_base, 1)
            pe.wait_ge(count_step, FIRST_PLACE)
            for r in range(2):
                ins = pe.matmul(O[:, r, 0:NJ], ident, off[:, 1, r, :], start=True, stop=False, skip_group_check=True)
            ins.then_inc(c_seed, 1)

            def place(i, u):
                t = i * 2 + u
                pe.wait_ge(c_dg, t + 1)
                wait(pe, c_chk, i * 8 + u * 4)
                pe.matmul(F[2][:, :], ones, dg[:, u, :, :, :].rearrange("p r k n -> p (r k n)"), start=True, stop=True).then_inc(c_row, 1)
                pe.wait_ge(c_oht, t + 1)
                pe.wait_ge(c_offs, t + 1)
                for r in range(2):
                    ins = pe.matmul(O[:, 2 + r, 0:NJ], oht[:, u, r, :], off[:, u, r, :], start=True, stop=True)
                ins.then_inc(c_g, 1)
                pe.wait_ge(c_hot2, t + 1)
                for r in range(2):
                    ins = pe.matmul(O[:, r, 0:NJ], oh_lo[:, u, r, :], oh_hi[:, u, r, :], start=False, stop=False, skip_group_check=True)
                ins.then_inc(c_upd, 1)
            loop(pe, HT, place)

        zeros_b = zeros[:, 0:NJ].bitcast(BF16)

        def prep_scalar(act):
            act.wait_ge(c_seed, 1)

            def offsets(i, u):
                wait(act, c_upd, i * 2 + u)
                for r in range(2):
                    ins = act.copy(off[:, u, r, :], O[:, r, 0:NJ])
                ins.then_inc(c_offs, 1)
            loop(act, HT, offsets)

        def prep_pool(pool):
            pool.wait_ge(tables_zero, 16 * (2 * (NJ // 14) + 2))

            def scatter(i, u):
                pool.wait_ge(row_in[u], i * 16 + 16)
                pool.wait_ge(c_posi, i * 2 + (u + 1))
                pool.sem_inc(gate, 1)
                for r, table in enumerate((by_dst, by_src)):
                    pool.indirect_dma_start(out=table[0:EP, :], out_offset=bass.IndirectOffsetOnAxis(ap=pos_i[:, u, r:r + 1], axis=0),
                                            in_=rowt[:, u, :], in_offset=None).then_inc(row_out[u], 16)
            loop(pool, HT, scatter)
            for u in range(2):
                pool.wait_ge(row_out[u], 32 * HT)

        def edge_sync(sp, L):
            if L == 0:
                stores_before(sp, 0)
            rows = A_OF[L][0:EP, :].rearrange("(g q p) c -> g p q c", q=Q, p=P)
            nxt = A_OF[L][1:EP + 1, KEY[L]:KEY[L] + 1].rearrange("(g q p) c -> g p q c", q=Q, p=P)

            def load(i, u):
                last = ("d_mn" if L == 0 else "d_v1")
                if not isinstance(i, int) or i > 0:
                    on(sp, last, L, i - 1, u)
                sp.dma_start(A[:, u, :, :], rows[i * 2 + u]).then_inc(row_ready[u], 16)
                sp.dma_start(knext[:, u, :].unsqueeze(2), nxt[i * 2 + u], allow_slow_non_contiguous=True).then_inc(next_ready[u], 16)
            if L:
                on(sp, "d_mn" if L == 1 else "d_v1", L - 1, EG // 2 - 1, 1)
            loop(sp, EG // 2, load)

        def edge_pool(pool, L):
            stores_before(pool, L)
            HALF = EG // 2

            def gather(i, u, L=L):
                pool.wait_ge(row_ready[u], i * 16 + 16 * (HALF * L + 1))
                pool.sem_inc(gate, 1)
                for q in range(Q):
                    idx = A[:, u, q, OTHER[L]:OTHER[L] + 1].bitcast(I32)
                    pool.indirect_dma_start(out=XG[:, u, q, S:S + XW], out_offset=None, in_=X_OF[L],
                                            in_offset=bass.IndirectOffsetOnAxis(ap=idx, axis=0)).then_inc(gathered[u], 16)
                    if L == 0:
                        idx = A[:, u, q, KEY[L]:KEY[L] + 1].bitcast(I32)
                        pool.indirect_dma_start(out=XD[:, u, q, :], out_offset=None, in_=X_OF[L],
                                                in_offset=bass.IndirectOffsetOnAxis(ap=idx, axis=0)).then_inc(gathered[u], 16)

            def cross(i, u, k):
                on(pool, f"a_dx{k}", L, i, u)
                if k == 1:
                    on(pool, "d_er", L, i, u)
                pool.tensor_tensor(xd(C1[:, u, :, :]), xd(DX[:, u, :, V:4 * V]), bd(ER[:, u, :, 2:5]), ALU.mult)
                pool.tensor_tensor(xd(C2[:, u, :, :]), xd(DX[:, u, :, 2 * V:5 * V]), bd(ER[:, u, :, 1:4]), ALU.mult).then_inc(sems[f"l_c{k}"], 1)

            def body(i, u, more):
                if L == 0:
                    on(pool, "d_er", L, i, u)
                    pool.tensor_tensor(RB[:, u, :, 0:16], A[:, u, :, A16:A16 + 16],
                                       A[:, u, :, A4:A4 + 1].to_broadcast([P, Q, 16]), ALU.mult)
                    pool.tensor_copy(RB[:, u, :, 16:32], A[:, u, :, A16:A16 + 16])
                    pool.tensor_copy(RB[:, u, :, 32:36], A[:, u, :, A4:A4 + 4]).then_inc(sems["l_rb"], 1)
                    on(pool, "d_var", L, i, u)
                    pool.tensor_tensor(RST[:, u, :, :, :].rearrange("p a q r -> p (a q r)"),
                                       STAT[:, u, :, :, :].rearrange("p a q r -> p (a q r)"),
                                       con[:, K_HALF:K_HALF + 16], ALU.pow).then_inc(sems["l_rstd"], 1)
                if L in L12:
                    on(pool, "d_er", L, i, u)
                    pool.tensor_tensor(XG[:, u, :, 0:S], XG[:, u, :, S:2 * S],
                                       A[:, u, :, A4:A4 + 1].to_broadcast([P, Q, S]), ALU.mult).then_inc(sems["l_se"], 1)
                if L == 3:
                    on(pool, "d_sq", L, i, u)
                    pool.tensor_tensor(KN[:, u, :], SM3[:, u, :, 0], con[:, K_HALF:K_HALF + Q], ALU.pow).then_inc(sems["l_rn"], 1)
                if more:
                    gather(i + u, 1 - u)
                if L in CROSS:
                    cross(i, u, 1)
                if L == 0:
                    on(pool, "a_tanh", L, i, u)
                    pool.sem_inc(gate, 1)
                    pool.tensor_scalar(SG[:, :, :], SG[:, :, :], 0.5, 0.5, ALU.mult, ALU.add).then_inc(sems["l_sg"], 1)
                    on(pool, "d_la", L, i, u)
                    pool.tensor_tensor(LA[:, :, :], LA[:, :, :], W("adot").unsqueeze(1).broadcast_to([P, Q, S]), ALU.mult).then_inc(sems["l_la"], 1)
                    cross(i, u, 2)
                on(pool, "d_idx", L, i, u)
                on(pool, "a_sum", L, i, u, per=Q, k=Q - 1)
                if L == 0:
                    on(pool, "a_g", L, i, u)
                pool.sem_inc(gate, 1)
                for q in range(Q):
                    src = (M if L else G)[:, u, q, :]
                    pool.indirect_dma_start(out=TABLE[L], out_offset=bass.IndirectOffsetOnAxis(ap=IDX[:, u, q:q + 1], axis=0),
                                            in_=src, in_offset=None, bounds_check=NP - 1, oob_is_err=False).then_inc(scattered[u], 16)
            gather(0, 0)
            loop_ahead(pool, HALF, body)

        events(ZERO, "a_g")

        def edge_tensor(pe, L):
            stores_before(pe, L)
            k_at = ATR[L]

            def flip(bank, rows, src, name):
                pe.sem_inc(gate, 1)
                for q in range(Q):
                    ins = pe.transpose(bank[0:rows, q * P:(q + 1) * P], src(q), ident)
                ins.then_inc(sems[name], 1)

            def product(bank, name, lhsT, rhs, u):
                pe.matmul(bank[0:lhsT.shape[1], :], lhsT, rhs, start=True, stop=True).then_inc(sems[name], 1)

            def body(i, u):
                xs = XG[:, u, :, :]
                if L == 0:
                    on(pe, "d_xn", L, i, u)
                    before(pe, "a_fs", L, i, u)
                    flip(F[0], P, lambda q: XN[:, q, 0:P], "p_xts")
                    before(pe, "a_fv", L, i, u)
                    flip(F[1], V3, lambda q: XN[:, q, P:P + V3], "p_xtv")
                    before(pe, "a_ae", L, i, u)
                    flip(F[2], V3, lambda q: XN[:, q, P + V3:P + 2 * V3], "p_xtd")
                    on(pe, "l_rb", L, i, u)
                    before(pe, "a_mc", L, i, u)
                    flip(F[3], k_at, lambda q: RB[:, u, q, :], "p_at")
                else:
                    pe.wait_ge(gathered[u], i * (16 * Q) + (gathered_base(L) + 16 * Q))
                    on(pe, "d_er", L, i, u)
                    if L in L12:
                        on(pe, "l_se", L, i, u)
                    before(pe, "d_p3", L, i, u)
                    flip(F[0], HSK[L], (lambda q: xs[:, q, 0:P]) if L < 3 else (lambda q: xs[:, q, S:2 * S]), "p_xts")
                    before(pe, "d_p5" if L != 2 else "a_v", L, i, u)
                    flip(F[1], V3, lambda q: xs[:, q, 2 * S:2 * S + V3], "p_xtv")
                    before(pe, "d_p4", L, i, u)
                    flip(F[2], k_at, lambda q: A[:, u, q, ATC[L]:ATC[L] + k_at], "p_at")
                    on(pe, "a_at", L, i, u)
                    before(pe, "d_car", L, i, u)
                    product(F[3], "p_hid", W(f"fc{L}"), AT[0:k_at, u, :], u)
                on(pe, "a_xts", L, i, u)
                product(F[0], "p_hs", W(f"hs{L}"), XTs[0:HSK[L], u, :], u)
                on(pe, "a_xtv", L, i, u)
                if L:
                    product(F[1], "p_hv", W(f"hv{L}"), XTv[0:V3, u, :], u)
                else:
                    on(pe, "a_xtd", L, i, u)
                    pe.matmul(F[1][0:V3, :], W("hv0"), XTv[0:V3, u, :], start=True, stop=False)
                    pe.matmul(F[1][0:V3, :], W("hvd0"), XTd[0:V3, :], start=False, stop=True).then_inc(sems["p_hv"], 1)
                    on(pe, "a_at", L, i, u)
                product(F[2], "p_eb", W(f"eb{L}"), AT[0:k_at, u, :], u)
                if L:
                    on(pe, "d_hid" if L == 1 else "a_hid", L, i, u)
                hid = HID[0:HIDK[L], u, :] if L else AT[0:k_at, u, :]
                product(F[3], "p_wab", W(f"wab{L}"), hid, u)
                on(pe, "a_s2", L, i, u)
                product(F[0], "p_w3", W(f"w3{L}"), hid, u)
                on(pe, "a_v", L, i, u)
                if L in CROSS:
                    product(F[1], "p_w5", W(f"w5{L}"), hid, u)
                on(pe, "d_ve", L, i, u)
                product(F[2], "p_w4", W(f"w4{L}"), hid, u)
                on(pe, "d_p1", L, i, u)
                on(pe, "d_keys", L, i, u)
                product(F[3], "p_key", ones, DG[:, :, :].rearrange("p q n -> p (q n)"), u)
                on(pe, "d_p3", L, i, u)
                on(pe, "d_p4", L, i, u)
                if L in CROSS:
                    on(pe, "d_p5", L, i, u)
                before(pe, "d_v1", L, i, u)
                if L:
                    before(pe, "a_msg_s", L, i, u)
                before(pe, "a_sum", L, i, u, per=Q)
                if L == 0:
                    before_g(pe, i, u)
                sw = PLAN[f"of{L}"][2]
                for q in range(Q):
                    e = slice(q * P, (q + 1) * P)
                    pe.matmul(O[:, q, 0:sw + V], P1[:, u, e], W(f"oab{L}"), start=True, stop=False, skip_group_check=True)
                    pe.matmul(O[:, q, 0:sw], P4[0:V3, u, e], W(f"of{L}"), start=False, stop=True, skip_group_check=True)
                    ins = pe.matmul(O[:, q, sw + V:sw + V + V3], P3[0:V3, u, e], W(f"oc{L}"), start=True, stop=True, skip_group_check=True)
                    if L in CROSS:
                        ins = pe.matmul(O[:, q, sw + V + V3:sw + V + 2 * V3], P5[0:V3, u, e], W(f"od{L}"), start=True, stop=True, skip_group_check=True)
                ins.then_inc(sems["p_out"], 1)
                if L == 0:
                    second_product(i, u)
                on(pe, "d_car", L, i, u)
                if L:
                    on(pe, "d_v1", L, i, u)
                    on(pe, "a_msg_s", L, i, u)
                else:
                    on(pe, "d_msg", L, i, u)
                    on(pe, "d_mps", L, i, u)
                for q in range(Q):
                    to = O[:, q, MAT[L]:MAT[L] + MW[L]]
                    pe.matmul(to, SEL[:, u, q, :], MSG[:, u, q, 0:MW[L]], start=True, stop=False, skip_group_check=True)
                    if q:
                        on(pe, "a_sum", L, i, u, per=Q, k=q - 1)
                        prev = M[:, u, q - 1, 0:MW[L]]
                    else:
                        if L:
                            before(pe, "a_sum", L, i, u, per=Q)
                        prev = M[:, 1 - u, Q - 1, 0:MW[L]] if L else MPS[:, 0:MW[L]]
                    pe.matmul(to, CAR[:, u, q, :], prev, start=False, stop=True, skip_group_check=True).then_inc(sems["p_sum"], 1)
                if L == 0:
                    last_product(i, u)

            def second_product(i, u):
                on(pe, "d_dot", 0, i, u)
                flip(F[0], V3, lambda q: SG[:, q, :], "p_ta")
                flip(F[1], V3, lambda q: VV[:, q, :], "p_tv")
                on(pe, "d_ae", 0, i, u)
                flip(F[2], H, lambda q: AE[:, q, :], "p_ae")
                on(pe, "d_mb", 0, i, u)
                on(pe, "d_car", 0, i, u)
                pe.sem_inc(gate, 1)
                for q in range(Q):
                    pe.matmul(F[3][:, q * H:(q + 1) * H], MB[:, q * P:(q + 1) * P], con[0:H, K_ID:K_ID + H], start=True, stop=True)
                pe.matmul(F[3][:, 16:16 + H], MB[:, 0:1].to_broadcast([H, P]), con[0:H, K_ID:K_ID + H], start=True, stop=True).then_inc(sems["p_mc"], 1)
                on(pe, "a_ta", 0, i, u)
                on(pe, "a_tv", 0, i, u)
                for q in range(Q):
                    e = slice(q * P, (q + 1) * P)
                    pe.matmul(O[:, q, 0:160], TA[0:V3, e], W("o2s"), start=True, stop=True, skip_group_check=True)
                    ins = pe.matmul(O[:, q, 160:352], TV[0:V3, e], W("o2v"), start=True, stop=True, skip_group_check=True)
                ins.then_inc(sems["p_out2"], 1)

            def last_product(i, u):
                on(pe, "d_mn", 0, i, u)
                flip(F[0], S, lambda q: MN[:, q, 0:S], "p_fs")
                flip(F[1], V3, lambda q: MN[:, q, S:C], "p_fv")
                on(pe, "a_fs", 0, i, u)
                on(pe, "a_fv", 0, i, u)
                for q in range(Q):
                    e = slice(q * P, (q + 1) * P)
                    pe.matmul(O[:, q, 176:176 + S], TA[0:S, e], W("fs"), start=True, stop=True, skip_group_check=True)
                    ins = pe.matmul(O[:, q, 176 + S:176 + C], TV[0:V3, e], W("fv"), start=True, stop=True, skip_group_check=True)
                ins.then_inc(sems["p_g"], 1)
            loop(pe, EG // 2, body)

        events((1,), "d_hid")
        DG = sb("DG", [P, Q, P])

        def gathered_base(L):
            return 16 * Q * (EG // 2) * (L + 1 if L else 0)

        def before_g(eng, i, u):
            wait(eng, sems["a_g"], i * 2 + u)

        def edge_scalar(act, L):
            stores_before(act, L)

            def move(dst, src, name, wait, i, u, **kw):
                on(act, wait, L, i, u)
                if kw:
                    act.activation(dst, src, **kw).then_inc(sems[name], 1)
                else:
                    act.copy(dst, src).then_inc(sems[name], 1)

            def spread_d(i, u, k, at):
                act.copy(DX[:, u, :, 0:V3], O[:, :, at:at + V3])
                act.copy(DX[:, u, :, V3:160], O[:, :, at:at + 2 * V]).then_inc(sems[f"a_dx{k}"], 1)

            def body(i, u):
                if L == 0:
                    on(act, "d_cent", L, i, u)
                    act.activation(XSQ[:, :, :, 0:S], XN[:, :, 0:P].rearrange("p q (r c) -> p q r c", r=2), ACT.Square)
                    act.activation(XSQ[:, :, 0, S:C], XG[:, u, :, 2 * S:2 * S + V3], ACT.Square)
                    act.activation(XSQ[:, :, 1, S:C], XD[:, u, :, S:C], ACT.Square).then_inc(sems["a_sq"], 1)
                    move(XTs[:, u, :], F[0][:, :], "a_xts", "p_xts", i, u, func=ACT.Identity, scale=col(0), bias=col(1))
                    move(XTv[0:V3, u, :], F[1][0:V3, :], "a_xtv", "p_xtv", i, u, func=ACT.Identity, scale=col(2, V3))
                    move(XTd[0:V3, :], F[2][0:V3, :], "a_xtd", "p_xtd", i, u, func=ACT.Identity, scale=col(2, V3))
                    move(AT[0:36, u, :], F[3][0:36, :], "a_at", "p_at", i, u)
                else:
                    move(XTs[0:HSK[L], u, :], F[0][0:HSK[L], :], "a_xts", "p_xts", i, u)
                    move(XTv[0:V3, u, :], F[1][0:V3, :], "a_xtv", "p_xtv", i, u)
                    move(AT[0:ATR[L], u, :], F[2][0:ATR[L], :], "a_at", "p_at", i, u)
                    if L == 1:
                        move(HSG[0:S, :], F[3][0:S, :], "a_sig", "p_hid", i, u, func=ACT.Tanh, scale=0.5)
                        act.copy(HID[0:S, u, :], F[3][0:S, :]).then_inc(sems["a_hid"], 1)
                    else:
                        move(HID[0:HIDK[L], u, :], F[3][0:HIDK[L], :], "a_hid", "p_hid", i, u, func=ACT.Relu)
                move(S2[:, u, :], F[0][:, :], "a_s2", "p_hs", i, u)
                move(VT[0:V3, u, :], F[1][0:V3, :], "a_v", "p_hv", i, u)
                if L == 0:
                    on(act, "d_car", L, i, u)
                    act.copy(KR[:, u, 1:GRP + 1], F[3][0:H, :])
                    before(act, "a_kr", L, i, u)
                    act.copy(KR[:, u, 0:1], KR[:, 1 - u, GRP:GRP + 1]).then_inc(sems["a_kr"], 1)
                    on(act, "p_out", L, i, u)
                    act.activation(SG[:, :, :], O[:, :, S:160], ACT.Tanh, scale=0.5).then_inc(sems["a_tanh"], 1)
                    act.activation(LA[:, :, :], O[:, :, 0:S], ACT.Copy, scale=0.2).then_inc(sems["a_la"], 1)
                    spread_d(i, u, 1, 288)
                    move(TA[0:V3, :], F[0][0:V3, :], "a_ta", "p_ta", i, u)
                    move(TV[0:V3, :], F[1][0:V3, :], "a_tv", "p_tv", i, u)
                    move(AET[:, :], F[2][0:H, :], "a_ae", "p_ae", i, u)
                    on(act, "p_mc", L, i, u)
                    act.copy(MC[:, u, :, :].rearrange("p q h -> p (q h)"), F[3][:, 0:16]).then_inc(sems["a_mc"], 1)
                    on(act, "d_sub", L, i, u)
                    act.activation(MSG[:, u, :, C:C + H], AE[:, :, :], ACT.Exp).then_inc(sems["a_exp"], 1)
                    on(act, "d_res", L, i, u)
                    act.activation(RES[:, :], RES[:, :], ACT.Exp).then_inc(sems["a_res"], 1)
                    on(act, "p_out2", L, i, u)
                    act.copy(HS1[:, :, :], O[:, :, V3:160]).then_inc(sems["a_hs"], 1)
                    spread_d(i, u, 2, 256)
                else:
                    on(act, "p_out", L, i, u)
                    act.copy(MSG[:, u, :, 0:SW[L]], O[:, :, 0:SW[L]]).then_inc(sems["a_msg_s"], 1)
                    if L in CROSS:
                        spread_d(i, u, 1, 224)
                if L:
                    wait(act, scattered[u], i * (16 * Q) + 16 * Q * ((EG // 2) * L))
                for q in range(Q):
                    on(act, "p_sum", L, i, u, per=Q, k=q)
                    act.copy(M[:, u, q, 0:MW[L]], O[:, q, MAT[L]:MAT[L] + MW[L]]).then_inc(sems["a_sum"], 1)
                if L == 0:
                    move(TA[0:S, :], F[0][0:S, :], "a_fs", "p_fs", i, u)
                    move(TV[0:V3, :], F[1][0:V3, :], "a_fv", "p_fv", i, u)
                    on(act, "p_g", L, i, u)
                    wait(act, scattered[u], i * (16 * Q))
                    act.copy(G[:, u, :, 0:C], O[:, :, 176:176 + C]).then_inc(sems["a_g"], 1)
            loop(act, EG // 2, body)

        def edge_vector(dve, L):
            stores_before(dve, L)
            DVE_GATHER = 16 * Q * (2 if L == 0 else 1)

            def direction(i, u):
                dve.wait_ge(gathered[u], i * DVE_GATHER + gathered_base(L) + DVE_GATHER)
                e4 = A[:, u, :, A4:A4 + 4]
                if L in L12:
                    dve.tensor_tensor(e4, e4, XG[:, u, :, S + C:S + C + 1].to_broadcast([P, Q, 4]), ALU.mult).then_inc(sems["d_kc"], 1)
                    on(dve, "d_kc", L, i, u)
                    at = A4 + 1
                elif L == 3:
                    a3 = A[:, u, :, A3:A3 + 3]
                    dve.tensor_tensor(U[:, u, :, 0:3], a3, a3, ALU.mult).then_inc(sems["d_kc"], 1)
                    on(dve, "d_kc", L, i, u)
                    dve.tensor_reduce(SM3[:, u, :, 0:1], U[:, u, :, 0:3], AX.X, ALU.add).then_inc(sems["d_sq"], 1)
                    on(dve, "l_rn", L, i, u)
                    dve.tensor_tensor(A[:, u, :, A4:A4 + 3], a3, KN[:, u, :].unsqueeze(2).broadcast_to([P, Q, 3]), ALU.mult).then_inc(sems["d_rhat"], 1)
                    on(dve, "d_rhat", L, i, u)
                    at = A4
                else:
                    at = A4 + 1
                    dve.tensor_copy(U[:, u, :, 0:1], e4[:, :, 0:1]).then_inc(sems["d_kc"], 1)
                dve.tensor_copy(ER[:, u, :, 0:3], A[:, u, :, at:at + 3])
                dve.tensor_copy(ER[:, u, :, 3:5], A[:, u, :, at:at + 2]).then_inc(sems["d_er"], 1)

            def keys(i, u):
                dve.wait_ge(next_ready[u], i * 16 + 16 * ((EG // 2) * L + 1))
                before(dve, "p_sum", L, i, u, per=Q)
                key = A[:, u, :, KEY[L]:KEY[L] + 1].bitcast(I32)
                dve.tensor_copy(KC[:, u, :].unsqueeze(2), key)
                dve.tensor_copy(KN[:, u, :], knext[:, u, :].bitcast(I32)).then_inc(sems["d_kn"], 1)
                on(dve, "d_kn", L, i, u)
                dve.tensor_tensor(KN[:, u, :], KN[:, u, :], KC[:, u, :], ALU.is_equal).then_inc(sems["d_eq"], 1)
                on(dve, "d_eq", L, i, u)
                wait(dve, scattered[u], i * (16 * Q) + 16 * Q * ((EG // 2) * L))
                dve.scalar_tensor_tensor(IDX[:, u, :], KN[:, u, :], BIG, KC[:, u, :], ALU.mult, ALU.add).then_inc(sems["d_idx"], 1)
                dve.tensor_scalar(KP[:, u, 0:1], KC[:, 1 - u, Q - 1:Q], 1.0, con[:, K_LAST:K_LAST + 1], ALU.add, ALU.mult)
                dve.tensor_scalar(KP[:, u, 1:Q], KC[:, u, 0:Q - 1], 1.0, con[:, K_LAST:K_LAST + 1], ALU.add, ALU.mult).then_inc(sems["d_kp"], 1)
                on(dve, "d_kp", L, i, u)
                dve.tensor_scalar(KP[:, u, :], KP[:, u, :], 1.0, None, ALU.subtract)
                dve.tensor_tensor(DG[:, :, :], ident.unsqueeze(1).broadcast_to([P, Q, P]),
                                  KC[:, u, :].unsqueeze(2).broadcast_to([P, Q, P]), ALU.mult).then_inc(sems["d_keys"], 1)

            def mult(dst, bank, src, rows, wait, name, i, u):
                on(dve, wait, L, i, u)
                dve.tensor_tensor(dst[0:rows, u, :], bank[0:rows, :], src[0:rows, u, :], ALU.mult).then_inc(sems[name], 1)

            def vectors(dst, i, u, k, b, c, e0, cross):
                last = f"d_v{k}"
                out4 = xd(dst)
                ins = dve.tensor_tensor(out4, bx(O[:, :, b:b + V]), bd(ER[:, u, :, 0:3]), ALU.mult)
                if not e0:
                    ins.then_inc(sems[f"d_tb{k}"], 1)
                if e0:
                    dve.tensor_tensor(U[:, u, :, :], O[:, :, c:c + V3], A[:, u, :, A4:A4 + 1].to_broadcast([P, Q, V3]), ALU.mult).then_inc(sems[f"d_tb{k}"], 1)
                    add = U[:, u, :, :]
                else:
                    add = O[:, :, c:c + V3]
                on(dve, f"d_tb{k}", L, i, u)
                ins = dve.tensor_tensor(dst, dst, add, ALU.add)
                if not cross:
                    ins.then_inc(sems[last], 1)
                if cross:
                    on(dve, f"l_c{k}", L, i, u)
                    dve.tensor_tensor(C1[:, u, :, :], C1[:, u, :, :], C2[:, u, :, :], ALU.subtract).then_inc(sems[f"d_w{k}"], 1)
                    on(dve, f"d_w{k}", L, i, u)
                    dve.tensor_tensor(dst, dst, C1[:, u, :, :], ALU.add).then_inc(sems[last], 1)

            def normalise(i, u):
                both = (XG[:, u, :, S:S + C], XD[:, u, :, 0:C])
                for r in range(2):
                    ins = dve.tensor_reduce(STAT[:, u, 0, :, r:r + 1], both[r][:, :, 0:S], AX.X, ALU.add)
                ins.then_inc(sems["d_mean"], 1)
                on(dve, "d_mean", L, i, u)
                for r in range(2):
                    mean = STAT[:, u, 0, :, r:r + 1].to_broadcast([P, Q, S])
                    ins = dve.scalar_tensor_tensor(XN[:, :, r * S:(r + 1) * S], both[r][:, :, 0:S], float(S), mean, ALU.mult, ALU.subtract)
                ins.then_inc(sems["d_cent"], 1)
                on(dve, "a_sq", L, i, u)
                dve.tensor_reduce(STAT[:, u, 0, :, :].unsqueeze(3), XSQ[:, :, :, 0:S], AX.X, ALU.add)
                dve.tensor_reduce(STAT[:, u, 1, :, :].unsqueeze(3), XSQ[:, :, :, S:C], AX.X, ALU.add).then_inc(sems["d_st"], 1)
                on(dve, "d_st", L, i, u)
                dve.tensor_scalar(STAT[:, u, 0, :, :], STAT[:, u, 0, :, :], 1.0 / S, float(S * S) * EPS, ALU.mult, ALU.add)
                dve.tensor_scalar(STAT[:, u, 1, :, :], STAT[:, u, 1, :, :], 1.0 / V, EPS, ALU.mult, ALU.add).then_inc(sems["d_var"], 1)
                on(dve, "l_rstd", L, i, u)
                before(dve, "p_out", L, i, u)
                for r in range(2):
                    sc = slice(r * S, (r + 1) * S)
                    dve.tensor_tensor(XN[:, :, sc], XN[:, :, sc], RST[:, u, 0, :, r:r + 1].to_broadcast([P, Q, S]), ALU.mult)
                    vc = slice(P + r * V3, P + (r + 1) * V3)
                    ins = dve.tensor_tensor(XN[:, :, vc], both[r][:, :, S:C], RST[:, u, 1, :, r:r + 1].to_broadcast([P, Q, V3]), ALU.mult)
                ins.then_inc(sems["d_xn"], 1)

            def body(i, u):
                direction(i, u)
                if L == 0:
                    normalise(i, u)
                keys(i, u)
                if L == 1:
                    on(dve, "a_sig", L, i, u)
                    dve.tensor_scalar(HSG[0:S, :], HSG[0:S, :], 0.5, 0.5, ALU.mult, ALU.add).then_inc(sems["d_hsg"], 1)
                    on(dve, "d_hsg", L, i, u)
                    on(dve, "a_hid", L, i, u)
                    dve.tensor_tensor(HID[0:S, u, :], HID[0:S, u, :], HSG[0:S, :], ALU.mult).then_inc(sems["d_hid"], 1)
                on(dve, "a_v", L, i, u)
                mult(VE, F[2], VT, V3, "p_eb", "d_ve", i, u)
                on(dve, "a_s2", L, i, u)
                mult(P1, F[3], S2, P, "p_wab", "d_p1", i, u)
                mult(P3, F[0], VT, V3, "p_w3", "d_p3", i, u)
                if L in CROSS:
                    mult(P5, F[1], VT, V3, "p_w5", "d_p5", i, u)
                on(dve, "d_ve", L, i, u)
                mult(P4, F[2], VE, V3, "p_w4", "d_p4", i, u)
                on(dve, "p_key", L, i, u)
                rows = F[3][:, :].rearrange("p (q n) -> p q n", q=Q)
                dve.tensor_tensor(SEL[:, u, :, :], rows, KC[:, u, :].unsqueeze(2).broadcast_to([P, Q, P]), ALU.is_equal)
                dve.tensor_tensor(CAR[:, u, :, :], rows, KP[:, u, :].unsqueeze(2).broadcast_to([P, Q, P]), ALU.is_equal).then_inc(sems["d_car"], 1)
                if L:
                    on(dve, "a_msg_s" if L == 2 else "a_dx1", L, i, u)
                    sw = SW[L]
                    vectors(MSG[:, u, :, sw:sw + V3], i, u, 1, sw, sw + V, L in L12, L in CROSS)
                    return
                on(dve, "a_kr", L, i, u)
                dve.tensor_tensor(MK[:, 0:GRP], KR[:, u, 0:GRP], KR[:, u, 1:GRP + 1], ALU.is_equal).then_inc(sems["d_link"], 1)
                on(dve, "d_link", L, i, u, per=5, k=LINK["mk"])
                dve.tensor_scalar(MK[:, 0:GRP], MK[:, 0:GRP], 1.0, -NEG, ALU.subtract, ALU.mult).then_inc(sems["d_mk"], 1)
                on(dve, "a_dx1", L, i, u)
                dve.tensor_tensor(LA[:, :, :], LA[:, :, :], O[:, :, 0:S], ALU.max).then_inc(sems["d_la"], 1)
                vectors(VV[:, :, :], i, u, 1, 160, 192, False, True)
                on(dve, "l_la", L, i, u)
                dve.tensor_reduce(AE[:, :, :].unsqueeze(3), LA[:, :, :].rearrange("p q (h c) -> p q h c", h=H), AX.X, ALU.add).then_inc(sems["d_ae"], 1)
                on(dve, "l_sg", L, i, u)
                on(dve, "d_v1", L, i, u)
                dve.tensor_tensor(xd(VV[:, :, :]), xd(VV[:, :, :]), bx(SG[:, :, S:V3]), ALU.mult).then_inc(sems["d_gate"], 1)
                on(dve, "d_gate", L, i, u)
                dve.tensor_tensor(xd(U[:, u, :, :]), xd(VV[:, :, :]), bd(ER[:, u, :, 0:3]), ALU.mult).then_inc(sems["d_link"], 1)
                on(dve, "d_link", L, i, u, per=5, k=LINK["vy"])
                dve.tensor_reduce(SG[:, :, S:V3].unsqueeze(3), U[:, u, :, :].rearrange("p q (x d) -> p q d x", x=3), AX.X, ALU.add).then_inc(sems["d_dot"], 1)
                on(dve, "a_ae", L, i, u)
                on(dve, "d_mk", L, i, u)
                before(dve, "d_mf", L, i, u)
                dve.tensor_tensor_scan(MF[:, u, :], MK[:, 0:GRP], AET[:, :], MF[:, 1 - u, GRP - 1:GRP], ALU.add, ALU.max).then_inc(sems["d_mf"], 1)
                on(dve, "d_mf", L, i, u)
                dve.tensor_tensor_scan(MB[:, GRP - 1::-1], MK[:, GRP:0:-1], MF[:, u, GRP - 1::-1], NEG, ALU.add, ALU.max).then_inc(sems["d_mb"], 1)
                on(dve, "a_mc", L, i, u)
                on(dve, "p_ae", L, i, u)
                dve.tensor_tensor(AE[:, :, :].rearrange("p q h -> p (q h)"), AE[:, :, :].rearrange("p q h -> p (q h)"), F[3][:, 0:16], ALU.subtract).then_inc(sems["d_sub"], 1)
                before(dve, "a_mc", L, i, u)
                dve.tensor_tensor(RES[:, :], MC[:, 1 - u, Q - 1, :], F[3][:, 16:16 + H], ALU.subtract).then_inc(sems["d_link"], 1)
                on(dve, "d_link", L, i, u, per=5, k=LINK["res"])
                dve.tensor_scalar(RES[:, :], RES[:, :], 0.0, None, ALU.min).then_inc(sems["d_res"], 1)
                on(dve, "a_res", L, i, u)
                before(dve, "a_sum", L, i, u, per=Q)
                old = M[:, 1 - u, Q - 1, :]
                heads(MPS[:, 0:S], old[:, 0:S], RES[:, :], HS)
                for k in range(3):
                    heads(MPS[:, S + k * V:S + (k + 1) * V], old[:, S + k * V:S + (k + 1) * V], RES[:, :], HV)
                dve.tensor_tensor(MPS[:, C:C + H], old[:, C:C + H], RES[:, :], ALU.mult).then_inc(sems["d_mps"], 1)
                on(dve, "a_dx2", L, i, u)
                on(dve, "a_exp", L, i, u)
                dve.tensor_tensor(U[:, u, :, 0:S], O[:, :, 0:S], A[:, u, :, A4:A4 + 1].to_broadcast([P, Q, S]), ALU.mult).then_inc(sems["d_link"], 1)
                on(dve, "d_link", L, i, u, per=5, k=LINK["hs"])
                dve.tensor_tensor(HS1[:, :, :], HS1[:, :, :], U[:, u, :, 0:S], ALU.add).then_inc(sems["d_hs"], 1)
                on(dve, "d_hs", L, i, u)
                ex = MSG[:, u, :, C:C + H]
                dve.tensor_tensor(MSG[:, u, :, 0:S].rearrange("p q (h c) -> p q h c", h=H), HS1[:, :, :].rearrange("p q (h c) -> p q h c", h=H),
                                  bd(ex, HS), ALU.mult)
                vectors(VV[:, :, :], i, u, 2, 64, 160, True, True)
                on(dve, "d_v2", L, i, u)
                for k in range(3):
                    c = slice(S + k * V, S + (k + 1) * V)
                    ins = dve.tensor_tensor(MSG[:, u, :, c].rearrange("p q (h c) -> p q h c", h=H),
                                            VV[:, :, k * V:(k + 1) * V].rearrange("p q (h c) -> p q h c", h=H), bd(ex, HV), ALU.mult)
                ins.then_inc(sems["d_msg"], 1)
                on(dve, "a_sum", L, i, u, per=Q, k=Q - 1)
                dve.tensor_scalar(DEN[:, :, :], M[:, u, :, C:C + H], 1e-16, None, ALU.add).then_inc(sems["d_link"], 1)
                on(dve, "d_link", L, i, u, per=5, k=LINK["den"])
                dve.reciprocal(DEN[:, :, :], DEN[:, :, :]).then_inc(sems["d_rden"], 1)
                on(dve, "d_rden", L, i, u)
                dve.tensor_tensor(MN[:, :, 0:S].rearrange("p q (h c) -> p q h c", h=H), M[:, u, :, 0:S].rearrange("p q (h c) -> p q h c", h=H),
                                  bd(DEN[:, :, :], HS), ALU.mult)
                for k in range(3):
                    c = slice(S + k * V, S + (k + 1) * V)
                    ins = dve.tensor_tensor(MN[:, :, c].rearrange("p q (h c) -> p q h c", h=H), M[:, u, :, c].rearrange("p q (h c) -> p q h c", h=H),
                                            bd(DEN[:, :, :], HV), ALU.mult)
                ins.then_inc(sems["d_mn"], 1)

            def heads(dst, src, factor, n):
                dve.tensor_tensor(dst.rearrange("p (h c) -> p h c", h=H), src.rearrange("p (h c) -> p h c", h=H),
                                  factor.unsqueeze(2).broadcast_to([P, H, n]), ALU.mult)

            loop(dve, EG // 2, body)

        events(ALL, "d_kn", "d_eq")
        events((3,), "d_rhat")
        events((1,), "d_hsg")
        events(ZERO, "d_st", "d_link")
        LINK = {"mk": 0, "vy": 1, "res": 2, "hs": 3, "den": 4}

        def node_sync(sp, L):
            scatters_before(sp, L)
            stores_before(sp, L)
            xv = X_OF[L].rearrange("(p g q) c -> g p q c", g=NG, q=Q)
            tv = TABLE[L].rearrange("(p g q) c -> g p q c", g=NG, q=Q)
            ov = X_TO[L].rearrange("(p g q) c -> g p q c", g=NG, q=Q)
            gw = MW[L] if L else C

            def load(i, u):
                sp.dma_start(XN_in[:, u, :, :], xv[i * 2 + u]).then_inc(node_in[u], 16)
                sp.dma_start(GN[:, u, :, 0:gw], tv[i * 2 + u][:, :, 0:gw]).then_inc(node_in[u], 16)

            def body(i, u, more):
                if more:
                    onn(sp, "n_out", L, i, u, back=1)
                    load(i + u, 1 - u)
                onn(sp, "n_out", L, i, u)
                if L < 3:
                    sp.dma_start(ov[i * 2 + u], YO[:, u, :, :]).then_inc(stored[u], 16)
                else:
                    sp.dma_start(ov[i * 2 + u], YO[:, u, :, 0:C]).then_inc(stored[u], 16)
            load(0, 0)
            loop_ahead(sp, NG // 2, body)

        def node_tensor(pe, L):
            scatters_before(pe, L)
            if L == 0:
                return
            sw = PLAN[f"ns{L}"][2]

            def body(i, u):
                pe.wait_ge(node_in[u], i * 32 + 32 * ((NG // 2) * L + 1))
                onn(pe, "n_extv", L - 1, i, u, back=1)
                pe.sem_inc(gate, 1)
                for q in range(Q):
                    ins = pe.transpose(F[0][0:S, q * P:(q + 1) * P], XN_in[:, u, q, 0:S], ident)
                ins.then_inc(sems["n_xts"], 1)
                for q in range(Q):
                    ins = pe.transpose(F[1][0:V3, q * P:(q + 1) * P], XN_in[:, u, q, S:C], ident)
                ins.then_inc(sems["n_xtv"], 1)
                onn(pe, "n_t", L - 1, i, u, back=1)
                onn(pe, "n_exts", L - 1, i, u)
                onn(pe, "n_extv", L - 1, i, u)
                for q in range(Q):
                    e = slice(q * P, (q + 1) * P)
                    pe.matmul(O[:, q, 0:sw], XTs[0:S, u, e], W(f"ns{L}"), start=True, stop=True, skip_group_check=True)
                    ins = pe.matmul(O[:, q, sw:sw + V3], XTv[0:V3, u, e], W(f"nv{L}"), start=True, stop=True, skip_group_check=True)
                ins.then_inc(sems["n_lin"], 1)
            loop(pe, NG // 2, body)

        def node_scalar(act, L):
            scatters_before(act, L)

            def body(i, u):
                if L:
                    onn(act, "n_xts", L - 1, i, u)
                    act.copy(XTs[0:S, u, :], F[0][0:S, :]).then_inc(sems["n_exts"], 1)
                    onn(act, "n_xtv", L - 1, i, u)
                    act.copy(XTv[0:V3, u, :], F[1][0:V3, :]).then_inc(sems["n_extv"], 1)
                if L in (1, 3):
                    k = 0 if L == 1 else 1
                    onn(act, "n_ta" if L == 1 else "n_t", 0 if L == 1 else 2, i, u)
                    act.activation(SIG[:, u, :, :], T1[:, u, :, 0:V3], ACT.Tanh, scale=0.5).then_inc(sems["n_sig"], 1)
                onn(act, "n_nm", L, i, u)
                wait(act, stored[u], i * 16 + 16 * (NG // 2) * L)
                for q in range(Q):
                    ins = act.activation(YO[:, u, q, 0:C], Y[:, u, q, :], ACT.Identity, scale=RS[:, u, q:q + 1], bias=NM[:, u, q:q + 1])
                if L < 3:
                    ins = act.copy(YO[:, u, :, C:C + 1], XN_in[:, u, :, C:C + 1])
                ins.then_inc(sems["n_out"], 1)
            loop(act, NG // 2, body)

        def node_pool(pool, L):
            scatters_before(pool, L)

            def body(i, u):
                if L in (1, 2):
                    onn(pool, "n_t", L - 1, i, u)
                    pool.tensor_tensor(T1[:, u, :, 0:MW[L]], T1[:, u, :, 0:MW[L]], XN_in[:, u, :, C:C + 1].to_broadcast([P, Q, MW[L]]), ALU.mult).then_inc(sems["n_ta"], 1)
                if L in (1, 3):
                    onn(pool, "n_sig", 0 if L == 1 else 1, i, u)
                    pool.sem_inc(gate, 1)
                    pool.tensor_scalar(SIG[:, u, :, :], SIG[:, u, :, :], 0.5, 0.5, ALU.mult, ALU.add).then_inc(sems["n_sg2"], 1)
                onn(pool, "n_mv", L, i, u)
                pool.sem_inc(gate, 1)
                pool.tensor_scalar(RS[:, u, :].unsqueeze(2), MV[:, u, :, 1:2], 1.0, EPS, ALU.mult, ALU.add).then_inc(sems["n_rs0"], 1)
                onn(pool, "n_rs0", L, i, u)
                pool.tensor_tensor(RS[:, u, :], RS[:, u, :], con[:, K_HALF:K_HALF + Q], ALU.pow).then_inc(sems["n_rs"], 1)
            loop(pool, NG // 2, body)

        sem("n_rs0")
        sem("n_nm0")

        def node_vector(dve, L):
            scatters_before(dve, L)

            def perm(ap):
                return ap.rearrange("p q (x d) -> p q d x", x=3)

            def chan(ap):
                return ap.rearrange("p q (d x) -> p q d x", x=3)

            def body(i, u):
                xin = XN_in[:, u, :, :]
                y = Y[:, u, :, :]
                dve.wait_ge(node_in[u], i * 32 + 32 * ((NG // 2) * L + 1))
                if L == 0:
                    g = GN[:, u, :, :]
                    dve.tensor_scalar(T1[:, u, :, 0:C], xin[:, :, 0:C], 2.0, None, ALU.mult).then_inc(sems["n_t0"], 1)
                    onn(dve, "n_t0", 0, i, u)
                    dve.tensor_tensor(y[:, :, 0:S], T1[:, u, :, 0:S], g[:, :, 0:S], ALU.add)
                    dve.tensor_tensor(chan(y[:, :, S:C]), chan(T1[:, u, :, S:C]), perm(g[:, :, S:C]), ALU.add).then_inc(sems["n_y"], 1)
                else:
                    sw = PLAN[f"ns{L}"][2]
                    onn(dve, "n_lin", L - 1, i, u)
                    dve.tensor_tensor(T1[:, u, :, 0:sw + V3], O[:, :, 0:sw + V3], GN[:, u, :, 0:sw + V3], ALU.add).then_inc(sems["n_t"], 1)
                    t = T1[:, u, :, :]
                    if L == 2:
                        onn(dve, "n_ta", 1, i, u)
                        dve.tensor_tensor(y[:, :, 0:S], t[:, :, 0:S], xin[:, :, 0:S], ALU.add)
                        dve.tensor_tensor(chan(y[:, :, S:C]), perm(t[:, :, S:C]), chan(xin[:, :, S:C]), ALU.add).then_inc(sems["n_y"], 1)
                    else:
                        k = 0 if L == 1 else 1
                        onn(dve, "n_sg2", k, i, u)
                        if L == 1:
                            onn(dve, "n_ta", 0, i, u)
                        dve.tensor_tensor(y[:, :, 0:S], t[:, :, 0:S], SIG[:, u, :, 0:S], ALU.mult)
                        dve.tensor_tensor(chan(y[:, :, S:C]), perm(t[:, :, V3:2 * V3]), bd(SIG[:, u, :, S:V3], 3), ALU.mult).then_inc(sems["n_yv"], 1)
                        onn(dve, "n_yv", k, i, u)
                        dve.tensor_tensor(y, y, xin[:, :, 0:C], ALU.add).then_inc(sems["n_y"], 1)
                onn(dve, "n_y", L, i, u)
                for q in range(Q):
                    ins = dve.bn_stats(BN[:, u, q, :], Y[:, u, q, :])
                ins.then_inc(sems["n_bn"], 1)
                onn(dve, "n_bn", L, i, u)
                dve.sem_inc(gate, 1)
                for q in range(Q):
                    ins = dve.bn_aggr(MV[:, u, q, :], BN[:, u, q, :])
                ins.then_inc(sems["n_mv"], 1)
                onn(dve, "n_rs", L, i, u)
                dve.tensor_tensor(NM[:, u, :], MV[:, u, :, 0], RS[:, u, :], ALU.mult).then_inc(sems["n_nm0"], 1)
                onn(dve, "n_nm0", L, i, u)
                dve.tensor_scalar(NM[:, u, :], NM[:, u, :], -1.0, None, ALU.mult).then_inc(sems["n_nm"], 1)
            loop(dve, NG // 2, body)

        sem("n_t0")

        block = ctx.enter_context(nc.Block())
        LAYERS = range(stop_after)

        @block.sync
        def _(sp):
            prep_sync(sp)
            for L in LAYERS:
                edge_sync(sp, L)
                node_sync(sp, L)
            for u in range(2):
                sp.wait_ge(stored[u], 16 * (NG // 2) * len(LAYERS))

        @block.gpsimd
        def _(pool):
            prep_pool(pool)
            for L in LAYERS:
                edge_pool(pool, L)
                node_pool(pool, L)

        @block.tensor
        def _(pe):
            prep_tensor(pe)
            for L in LAYERS:
                edge_tensor(pe, L)
                node_tensor(pe, L)

        @block.scalar
        def _(act):
            prep_scalar(act)
            for L in LAYERS:
                edge_scalar(act, L)
                node_scalar(act, L)

        @block.vector
        def _(dve):
            prep_vector(dve)
            for L in LAYERS:
                edge_vector(dve, L)
                node_vector(dve, L)


def pack(inputs):
    import numpy as np
    get = {k: np.asarray(v) for k, v in inputs.items()}
    wt, sc = np.zeros((P, WW), np.float32), np.ones((P, WW), np.float32)

    def put(name, r0, c0, matrix, scale=1.0):
        at = PLAN[name][1] + c0
        wt[r0:r0 + matrix.shape[0], at:at + matrix.shape[1]] = matrix
        sc[r0:r0 + matrix.shape[0], at:at + matrix.shape[1]] = scale

    def put3(name, matrix, scale=1.0, c0=0, inner=False):
        at = PLAN[name][1] + c0
        for x in range(3):
            rows = slice(x, V3, 3) if inner else slice(x * V, (x + 1) * V)
            wt[rows, at + x * V:at + (x + 1) * V] = matrix
            sc[rows, at + x * V:at + (x + 1) * V] = scale

    def rep(matrix):
        return np.concatenate([matrix] * 3, axis=1)

    def rows3(matrix):
        return np.concatenate([matrix] * 3, axis=0)

    def direction_rows(name, first):
        for x in range(3):
            wt[first + x, PLAN[name][1] + x * V:PLAN[name][1] + (x + 1) * V] = 1.0

    r2, r3 = 2.0 ** 0.5, 3.0 ** 0.5
    g = {k[7:]: v for k, v in get.items() if k.startswith("L0_gnn_")}
    for c0 in (0, S):
        put("hs0", 0, c0, g["Ws_src"])
        put("hs0", S, c0, g["Ws_dst"])
    put3("hv0", g["Wv_src"], inner=True)
    put3("hvd0", g["Wv_dst"], inner=True)
    direction_rows("eb0", 33)
    rbf = g["W_rbf"]
    put("wab0", 0, 0, rbf[:, 0:S])
    put("wab0", 16, S, rbf[:, S:2 * S])
    put("w30", 0, 0, rep(rbf[:, 2 * S:2 * S + V]))
    put("w40", 16, 0, rep(rbf[:, 2 * S + V:2 * S + 2 * V]))
    put("w50", 16, 0, rep(rbf[:, 2 * S + 2 * V:]))
    put("oab0", 0, 0, g["W_alpha"][0:S])
    put("oab0", 0, S, g["Ws_val"][0:S])
    put("oab0", S, 160, g["Wv_val"][0:S])
    put("of0", 0, 0, rows3(g["W_alpha"][S:]), 1 / r3)
    put("of0", 0, S, rows3(g["Ws_val"][S:]), 1 / r3)
    put3("oc0", g["Wv_val"][S:S + V])
    put3("od0", g["Wv_val"][S + V:], 1 / r2)
    put("vst", 0, 0, g["Ws_val"][0:S].T)
    put("vst2", 0, 0, rep(g["Ws_val"][S:].T), 1 / r3)
    put("wg", 0, 0, g["Wg"])
    put("o2s", 0, 0, g["Ws_vlin"][0:S])
    put("o2s", 0, S, g["Wv_vlin"][0:S])
    put("o2s", S, S + V, g["Ws_vlin"][S:], 1 / r3)
    put3("o2v", g["Wv_vlin"][S:S + V])
    put3("o2v", g["Wv_vlin"][S + V:], 1 / r2, c0=V3)
    put("fs", 0, 0, g["Wps"])
    put3("fv", g["Wpv"])
    put("adot", 0, 0, np.broadcast_to(g["alpha_dot"].reshape(1, S), (P, S)))
    for r0 in (0, S):
        put("cols", r0, 0, g["gamma_s"][:, None])
        put("cols", r0, 1, g["beta_s"][:, None])
    put("cols", 0, 2, np.repeat(g["gamma_v"], 3)[:, None])
    put("cols", 0, 3, np.concatenate([g["w2_ss"], g["w2_vv0"]])[:, None])
    put("cols", 0, 4, np.concatenate([g["w2_vs"]] * 3)[:, None])
    put("cols", 0, 5, np.concatenate([g["w2_vv1"]] * 3)[:, None])
    put("cols", 0, 6, g["w2_sv"][:, None])

    def conv(L, ls, lv, fc1, fc2, os_, ov, ns, nv, c_h, c_hv, c_fc1, c_fc2, fc_row, e_row, c_s, c_dot, c_b, c_v, c_x, c_ns, c_nv):
        if L == 3:
            put("hs3", 0, 0, ls, c_h)
            put("hs3", 0, S, ls, c_h)
        else:
            put(f"hs{L}", 0, 0, ls, c_h)
            put(f"hs{L}", S, S, ls, c_h)
        put3(f"hv{L}", lv, c_hv, inner=True)
        put(f"fc{L}", fc_row, 0, fc1, c_fc1)
        direction_rows(f"eb{L}", e_row)
        put(f"wab{L}", 0, 0, fc2[:, 0:2 * S], c_fc2)
        for k, name in enumerate(("w3", "w4", "w5")[:2 if L == 2 else 3]):
            put(f"{name}{L}", 0, 0, rep(fc2[:, 2 * S + k * V:2 * S + (k + 1) * V]), c_fc2)
        put(f"oab{L}", 0, 0, os_[0], c_s)
        put(f"oab{L}", S, os_[0].shape[1], ov[0], c_b)
        put(f"of{L}", 0, 0, rows3(os_[1]), c_dot)
        put3(f"oc{L}", ov[1], c_v)
        if L != 2:
            put3(f"od{L}", ov[2], c_x)
        put(f"ns{L}", 0, 0, ns, c_ns)
        put3(f"nv{L}", nv, c_nv, inner=True)

    g = {k[7:]: v for k, v in get.items() if k.startswith("L1_gnn_")}
    s96, s128 = 96.0 ** -0.5 / 4, 128.0 ** -0.5 / 4
    conv(1, g["lin1_ws"], g["lin1_wv"], g["fc_w1"], g["fc_w2"], (g["lin2_ws"][0:S], g["lin2_ws"][S:]),
         (g["lin2_wv"][0:S], g["lin2_wv"][S:S + V], g["lin2_wv"][S + V:]), g["sc_ws"], g["sc_wv"],
         1 / 8, 32.0 ** -0.5, 1 / 8, 1 / 8, 0, 65, s96, s96 / r3, s128, s128, s128 / r2, 1 / 8, 32.0 ** -0.5)
    g = {k[7:]: v for k, v in get.items() if k.startswith("L2_gnn_")}
    o = 0.5 / 4 * 96.0 ** -0.5
    conv(2, g["W_l1_0"], g["W_l1_1"], g["W_fc1"], g["W_fc2"], (g["W_l2_00"], g["W_l2_10"]), (g["W_l2_01"], g["W_l2_11"]),
         g["W_si0"], g["W_si1"], 1 / 8, 32.0 ** -0.5, 10.0 ** -0.5, r2 / 10, 4, 1, o, o / r3, o, o, o, 1 / 8, 32.0 ** -0.5)
    g = {k[7:]: v for k, v in get.items() if k.startswith("L3_gnn_")}
    conv(3, g["W_nl0"], g["W_nl1"], g["W_fc1"], g["W_fc2"], (g["W_out_s"][0:S], g["W_out_s"][S:]),
         (g["W_out_v"][0:S], g["W_out_v"][S:S + V], g["W_out_v"][S + V:]), g["W_skip0"], g["W_skip1"],
         1.0, 1.0, 1.0, 1.0, 0, 64, 1 / 32, 1 / 32, r3 / 32, 1 / 32, r3 / r2 / 32, 1.0, 1.0)
    return wt, sc


def constants():
    import numpy as np
    k = np.zeros((P, KW), np.float32)
    k[:, K_ID:K_ID + P] = np.eye(P)
    k[:, K_TRI:K_TRI + P] = np.tri(P, P, -1)
    k[:, K_TRIU:K_TRIU + P] = np.tri(P, P, -1).T
    k[:, K_ONE:K_ONE + P] = 1.0
    k[:, K_IOTA:K_IOTA + NJ] = np.arange(NJ)
    k[:, K_PIDX] = np.arange(P)
    k[P - 1, K_LAST] = 1.0
    k[:, K_HALF:K_HALF + 16] = -0.5
    return k


def kernel(**inputs):
    import numpy as np
    import concourse.bacc as bacc
    from concourse.bass_utils import run_bass_kernel_spmd

    get = {k: np.asarray(inputs[k]) for k in ("x", "src", "dst", "edge_attr_10", "edge_attr_16", "edge_attr_3",
                                              "edge_attr_4", "edge_attr_64", "node_vec1")}
    x = np.zeros((NP, XW), np.float32)
    x[0:N, 0:C] = get["x"]
    x[0:N, C:C + 1] = get["node_vec1"]
    attr = np.zeros((EP, AW), np.float32)
    attr[:, A3:A3 + 3] = 1.0
    for at, name in ((A64, "edge_attr_64"), (A4, "edge_attr_4"), (A10, "edge_attr_10"), (A16, "edge_attr_16"), (A3, "edge_attr_3")):
        attr[0:E, at:at + get[name].shape[1]] = get[name]
    ends = attr.view(np.int32)
    ends[:, ASRC] = ends[:, ADST] = N
    ends[0:E, ASRC], ends[0:E, ADST] = get["src"], get["dst"]
    keys = np.full((2, EP), N, np.int32)
    keys[0, 0:E], keys[1, 0:E] = get["dst"], get["src"]
    keys = np.ascontiguousarray(keys.reshape(2, ET, P).transpose(2, 0, 1))
    wt, sc = pack(inputs)

    nc = bacc.Bacc("TRN2", target_bir_lowering=False, num_devices=1)
    arrays = {"x_in": x, "attr_in": attr, "keys_in": keys, "w_in": wt, "wscale_in": sc, "const_in": constants()}
    args = [nc.dram_tensor(k, a.shape, mybir.dt.from_np(a.dtype), kind="ExternalInput").ap() for k, a in arrays.items()]
    out = nc.dram_tensor("out", (NP, C), F32, kind="ExternalOutput").ap()
    build(nc, *args, out)
    r = run_bass_kernel_spmd(nc, [arrays], core_ids=[0])
    return r.results[0]["out"][0:N]
```

```python
from contextlib import ExitStack

import concourse.bass as bass
from concourse import mybir

F32 = mybir.dt.float32
BF16 = mybir.dt.bfloat16
I32 = mybir.dt.int32
ALU = mybir.AluOpType
ACT = mybir.ActivationFunctionType
AX = mybir.AxisListType

P = 128
N, E = 50000, 25000
S, V, H = 64, 32, 4
V3, C = 3 * V, S + 3 * V
HS, HV = S // H, V // H
Q = 4
GRP = Q * P
NJ = 400
NP = P * NJ
NG = NJ // Q
DEPTH = 10
BUFS = 5
EG = 50
EP = EG * GRP
ET = EP // P
ZJ = 16
XW = 164
TW = 192
EPS = 1e-5
BIG = float(1 << 20)
NEG = -1.0e30

A64, A4, A10, A16, A3, ASRC, ADST, AW = 0, 64, 68, 78, 94, 97, 98, 100

K_ID, K_TRI, K_TRIU, K_ONE, K_IOTA = 0, 128, 256, 384, 512
K_PIDX = K_IOTA + NJ
K_LAST = K_PIDX + 1
K_HALF = K_LAST + 1
KW = K_HALF + 16


def weight_plan():
    plan, at = {}, 0
    def put(name, rows, cols):
        nonlocal at
        plan[name] = (rows, at, cols)
        at += cols
    for L, (hs, at_rows, hid, sw) in enumerate(((128, 32, 0, 160), (128, 64, 64, 96), (128, 10, 100, 64), (64, 64, 64, 96))):
        put(f"hs{L}", hs, P)
        put(f"hv{L}", P, P)
        if L == 0:
            put("hvd0", P, P)
        else:
            put(f"fc{L}", at_rows, hid)
        k = hid or at_rows
        put(f"wab{L}", k, P)
        put(f"w34{L}", k, P)
        if L != 2:
            put(f"w5{L}", k, V3)
            put(f"od{L}", V3, V3)
        put(f"oab{L}", P, sw + V)
        put(f"of{L}", P, sw)
        put(f"oc{L}", P, V3)
        if L:
            put(f"ns{L}", S, 64 if L == 2 else 96)
            put(f"nv{L}", V3, V3)
    put("o2s", V3, 160)
    put("o2v", V3, 192)
    put("fs", S, S)
    put("fv", V3, V3)
    put("vst", S, S)
    put("vst2", S, P)
    put("wg", S, V)
    put("adot", P, S)
    put("cols", P, 8)
    return plan, at


PLAN, WW = weight_plan()


def build(nc, x_in, attr_in, keys_in, w_in, wscale_in, const_in, out, stop_after=4):
    with ExitStack() as ctx:
        def sb(name, shape, dt=F32):
            return ctx.enter_context(nc.sbuf_tensor("sb_" + name, shape, dt))

        sems = {}

        def sem(name):
            sems[name] = ctx.enter_context(nc.semaphore(name))
            return sems[name]

        x_a = nc.dram_tensor("x_a", (NP, XW), F32).ap()
        x_b = nc.dram_tensor("x_b", (NP, XW), F32).ap()
        agg_dst = nc.dram_tensor("agg_dst", (NP, TW), F32).ap()
        agg_src = nc.dram_tensor("agg_src", (NP, TW), F32).ap()
        by_dst = nc.dram_tensor("by_dst", (EP + GRP, AW), F32).ap()
        new_key = nc.dram_tensor("new_key", (EP,), F32).ap()
        by_src = nc.dram_tensor("by_src", (EP + GRP, AW), F32).ap()

        w = sb("w", [P, WW])
        con = sb("con", [P, KW])
        ident = con[:, K_ID:K_ID + P]
        ones = con[:, K_ONE:K_ONE + P]
        iota = con[:, K_IOTA:K_IOTA + NJ]
        ident_b = sb("ident_b", [P, P], BF16)
        ones_b = sb("ones_b", [P, P], BF16)

        def W(name, r0=0, r1=None, c0=0, c1=None):
            rows, at, cols = PLAN[name]
            return w[r0:(rows if r1 is None else r1), at + c0:at + (cols if c1 is None else c1)]

        def col(k, rows=P):
            at = PLAN["cols"][1] + k
            return w[0:rows, at:at + 1]

        F = [ctx.enter_context(nc.psum_tensor(f"ps_f{k}", [P, 512], F32)) for k in range(4)]
        O = ctx.enter_context(nc.psum_tensor("ps_o", [P, Q, 512], F32))

        M = sb("M", [P, 2, Q, TW])
        G = sb("G", [P, 2, Q, TW])
        MC = sb("MC", [P, 2, Q, H])
        MF = sb("MF", [H, 2, GRP])
        MK = sb("MK", [H, 2, GRP + 1])
        LAST = sb("LAST", [P, 2, ET])
        CARRY = sb("CARRY", [P, 2, ET])
        ROW_TO = sb("ROW_TO", [P, 2, ET], I32)
        YO = sb("YO", [P, 2, Q, XW])

        room = ExitStack()

        def tmp(name, shape, dt=F32):
            return room.enter_context(nc.sbuf_tensor("sb_" + name, shape, dt))

        keys_i = tmp("keys_i", [P, 2, ET], I32)
        part_i = tmp("part_i", [P, 5, 2, ET], I32)
        key_f = tmp("key_f", [P, 2, ET])
        lo_f = tmp("lo_f", [P, 2, ET])
        hi_f = tmp("hi_f", [P, 2, ET])
        oh_hi = tmp("oh_hi", [P, 2, 2, NJ], BF16)
        oh_lo = tmp("oh_lo", [P, 2, 2, P], BF16)
        cnt = tmp("cnt", [P, 2, NJ])
        inc = tmp("inc", [P, 2, NJ])
        onesj = tmp("onesj", [P, NJ])
        bcol = tmp("bcol", [P, 2])
        off = tmp("off", [P, 2, 2, NJ])
        offi = tmp("offi", [P, 2, NJ])
        byte_f = tmp("byte_f", [P, 3, 2, ET])
        dg = tmp("dg", [P, 2, 3, 2, P], BF16)
        oht = tmp("oht", [P, 2, 2, P])
        gj = tmp("gj", [P, 2, NJ])
        gt = tmp("gt", [P, 2, P])
        pos = tmp("pos", [P, 2, 2, 2])
        pos_i = tmp("pos_i", [P, 2, 2], I32)
        rowt = tmp("rowt", [P, 2, AW])
        XG_w = tmp("wscale", [P, WW])[:, :]
        cnt_m1_t = tmp("cnt_m1", [1, AW])
        cnt_m1 = cnt_m1_t[0:1, :]
        zeros = tmp("zeros", [P, ZJ * TW])
        HP = ET // 2
        keys2 = tmp("keys2", [HP, 2, 2 * P + 2])
        key2 = tmp("key2", [HP, 2, 2 * P + 2])
        next_eq = tmp("next_eq", [HP, 2, 2 * P])
        same_tile = tmp("same_tile", [HP, 2, 2 * P])
        prev_eq = tmp("prev_eq", [HP, 2, 2 * P])
        row_to2 = tmp("row_to2", [HP, 2, 2 * P])
        place2 = tmp("place2", [HP, 2, 2 * P])
        last2 = tmp("last2", [HP, 2, 2 * P])
        carry2 = tmp("carry2", [HP, 2, 2 * P])
        link2 = tmp("link2", [HP, 2 * P])
        room.close()

        A = tmp("A", [P, 2, Q, AW])
        XG = tmp("XG", [P, 2, Q, S + C + V])
        XD = tmp("XD", [P, 2, Q, XW])
        XN = tmp("XN", [P, Q, 3 * P])
        DOT = tmp("DOT", [P, Q, 2 * V3])
        XSQ = tmp("XSQ", [P, Q, 2, C])
        STAT = tmp("STAT", [P, 2, 2, Q, 2])
        RST = tmp("RST", [P, 2, 2, Q, 2])
        RB = tmp("RB", [P, 2, Q, 32])
        XTs = tmp("XTs", [P, 2, GRP])
        XTv = tmp("XTv", [P, 2, GRP])
        XTd = tmp("XTd", [P, GRP])
        AT = tmp("AT", [P, 2, GRP])
        HID = tmp("HID", [P, 2, GRP])
        HSG = tmp("HSG", [P, GRP])
        S2 = tmp("S2", [P, 2, GRP])
        VT = tmp("VT", [P, 2, GRP])
        P1 = tmp("P1", [P, 2, GRP])
        P3 = tmp("P3", [P, 2, GRP])
        P5 = tmp("P5", [P, 2, GRP])
        ER = tmp("ER", [P, 2, Q, 6])
        DX = tmp("DX", [P, 2, Q, 160])
        C1 = tmp("C1", [P, 2, Q, V3])
        C2 = tmp("C2", [P, 2, Q, V3])
        U = tmp("U", [P, 2, Q, V3])
        MSG = tmp("MSG", [P, 2, Q, TW])
        SEL = tmp("SEL", [P, 2, Q, P])
        CAR = tmp("CAR", [P, 2, Q, P])
        KN = tmp("KN", [P, 2, Q])
        IDX = tmp("IDX", [P, 2, Q], I32)
        SM3 = tmp("SM3", [P, 2, Q, 3])
        LA = tmp("LA", [P, Q, S])
        SG = tmp("SG", [P, Q, V3])
        VV = tmp("VV", [P, Q, V3])
        AE = tmp("AE", [P, Q, H])
        AET = tmp("AET", [H, GRP])
        MB = tmp("MB", [H, GRP])
        RES = tmp("RES", [P, H])
        MPS = tmp("MPS", [P, TW])
        HS1 = tmp("HS1", [P, Q, S])
        DEN = tmp("DEN", [P, Q, H])
        MN = tmp("MN", [P, Q, C])
        TA = tmp("TA", [P, GRP])
        TV = tmp("TV", [P, GRP])
        room.close()
        XI = tmp("XI", [P, BUFS, Q, XW])
        GN = tmp("GN", [P, BUFS, Q, TW])
        NTs = tmp("NTs", [S, 2, GRP])
        NTv = tmp("NTv", [V3, 2, GRP])
        T1 = tmp("T1", [P, 2, Q, TW])
        SIG = tmp("SIG", [P, 2, Q, V3])
        Y = tmp("Y", [P, 2, Q, C + 1])
        BN = tmp("BN", [P, 2, Q, 6])
        MV = tmp("MV", [P, 2, Q, 2])
        RS = tmp("RS", [P, 2, Q])
        NM = tmp("NM", [P, 2, Q])
        room.close()

        def wait(eng, semaphore, value):
            if not isinstance(value, int) or value > 0:
                eng.wait_ge(semaphore, value)

        loaded = sem("loaded")
        zeroed = sem("zeroed")
        setup_done = {n: sem("setup_" + n) for n in ("dve", "pe")}
        tables_zero = sem("tables_zero")
        row_ready = [sem("row_ready0"), sem("row_ready1")]
        link_ready = [sem("link_ready0"), sem("link_ready1")]
        gathered = [sem("gathered0"), sem("gathered1")]
        scattered = [sem("scattered0"), sem("scattered1")]
        node_in = [sem(f"node_in{v}") for v in range(BUFS)]
        stored = [sem("stored0"), sem("stored1")]
        gate = sem("gate")

        ALL, CONV, CROSS, ZERO, L12 = (0, 1, 2, 3), (1, 2, 3), (0, 1, 3), (0,), (1, 2)
        USES = {}

        def events(layers, *names):
            for name in names:
                USES[name] = layers
                sem(name)

        events(ALL, "p_xts", "p_xtv", "p_at", "p_hs", "p_hv", "p_wab", "p_w3", "p_out", "p_sum",
               "a_xts", "a_xtv", "a_at", "a_s2", "a_v", "a_sum", "d_p1", "d_p3", "d_car", "d_er",
               "d_tb1", "d_v1", "l_dot", "d_dt")
        events(CONV, "p_hid", "a_hid", "a_msg_s", "d_kc")
        events(L12, "l_se")
        events((1,), "a_sig", "d_hid", "d_hsg")
        events((3,), "d_sq", "l_rn", "d_rhat")
        events(CROSS, "p_w5", "d_p5", "a_dx1", "l_c1", "d_w1")
        events(ZERO, "p_xtd", "a_xtd", "d_mean", "d_cent", "a_sq", "d_st", "d_var", "l_rstd", "d_xn", "l_rb",
               "a_tanh", "l_sg", "a_la", "d_la", "l_la", "d_ae", "d_gate", "d_dot", "d_link", "l_dot2",
               "p_ta", "p_tv", "p_ae", "a_ta", "a_tv", "a_ae", "d_mf", "d_mb", "p_mc",
               "a_mc", "d_sub", "a_exp", "d_res", "a_res", "d_mps", "p_out2", "a_hs", "d_hs", "a_dx2",
               "l_c2", "d_tb2", "d_w2", "d_v2", "d_msg", "d_rden", "d_mn",
               "p_fs", "p_fv", "a_fs", "a_fv", "p_g", "a_g")

        def base(name, L):
            return EG * sum(1 for k in USES[name] if k < L)

        def on(eng, name, L, i, u, per=1, k=0):
            wait(eng, sems[name], i * (2 * per) + (base(name, L) * per + u * per + k + 1))

        def before(eng, name, L, i, u, per=1):
            wait(eng, sems[name], i * (2 * per) + (base(name, L) * per + u * per))

        for name in ("n_xts", "n_xtv", "n_exts", "n_extv", "n_lin", "n_t", "n_ta", "n_sig", "n_sg2",
                     "n_yv", "n_y", "n_bn", "n_mv", "n_rs0", "n_rs", "n_nm", "n_out"):
            sem(name)

        def onn(eng, name, k, i, v, back=0):
            wait(eng, sems[name], i * DEPTH + (NG * k + v + 1 - back))

        X_OF = (x_in, x_a, x_b, x_a)
        X_TO = (x_a, x_b, x_a, out)
        A_OF = (by_dst, by_dst, by_dst, by_src)
        KEY = (ADST, ADST, ADST, ASRC)
        OTHER = (ASRC, ASRC, ASRC, ADST)
        TABLE = (agg_dst, agg_dst, agg_dst, agg_src)
        SW = (96, 96, 64, 96)
        MW = (164, 192, 160, 192)
        MAT = (0, 320, 256, 320)
        HIDK = (0, 64, 100, 64)
        ATR = (32, 64, 10, 64)
        ATC = (0, A64, A10, A64)
        HSK = (128, 128, 128, 64)

        def stores_before(eng, L):
            for u in range(2):
                if L:
                    eng.wait_ge(stored[u], 16 * (NG // 2) * L)
                else:
                    eng.wait_ge(row_out[u], 32 * HT)
            if not L:
                eng.wait_ge(c_upd, ET)
                eng.wait_ge(tables_ready, 4)
                eng.wait_ge(links_stored, 16)

        def scatters_before(eng, L):
            for u in range(2):
                eng.wait_ge(scattered[u], 16 * Q * (EG // 2) * (L + 1))

        def loop(eng, count, body):
            for u in range(2):
                body(0, u)
            with eng.Fori(1, count) as i:
                for u in range(2):
                    body(i, u)

        def bx(ap):
            return ap.unsqueeze(2).broadcast_to([ap.shape[0], ap.shape[1], 3, ap.shape[2]])

        def bd(ap, n=V):
            return ap.unsqueeze(3).broadcast_to([ap.shape[0], ap.shape[1], ap.shape[2], n])

        def xd(ap, n=3):
            return ap.rearrange("p q (x d) -> p q x d", x=n)

        count_step = sem("count_step")
        SPLIT, CAST, COPY, SCAN, BASE, EXCL, FIRST_PLACE = 1, 2, 4, 6, 7, 9, 11
        c_hot, c_cnt, c_base, c_seed, c_dg, c_row, c_oht, c_offs, c_g, c_upd, c_hot2, c_posi, c_rank, c_pick = (
            sem(k) for k in ("one_hots", "counted", "key_base", "places_seeded", "diagonals", "key_rows", "one_hots_turned",
                             "places_copied", "places_read", "places_moved", "one_hots_again", "positions", "ranked", "picked"))
        row_in = [sem("row_in0"), sem("row_in1")]
        row_out = [sem("row_out0"), sem("row_out1")]
        HT = ET // 2

        def reached(u, r):
            return F[r][:, 0:NJ] if u else O[:, 2 + r, 0:NJ]

        def loop_tiles(eng, body):
            for u in range(2):
                body(0, u, u == 0, False)
            with eng.Fori(1, HT - 1) as i:
                for u in range(2):
                    body(i, u, False, False)
            for u in range(2):
                body(HT - 1, u, False, u == 1)

        TABLES_ZERO = 16 * (2 * (NJ // ZJ) + 2)
        KEY_OF = (ADST, ASRC)
        keys_in_rows, run_step, turned, tables_ready, links_stored = (
            sem(k) for k in ("keys_in_rows", "run_step", "tables_turned", "tables_ready", "links_stored"))
        ROW_STEPS = {"cast": 1, "equal": 4, "parts": 8, "scan": 10, "carry": 11, "link": 12}

        def prep_sync(sp):
            sp.dma_start(w[:, :], w_in).then_inc(loaded, 16)
            sp.dma_start(con[:, :], const_in).then_inc(loaded, 16)
            sp.dma_start(XG_w, wscale_in).then_inc(loaded, 16)
            sp.dma_start(keys_i[:, :, :], keys_in).then_inc(loaded, 16)
            sp.wait_ge(zeroed, 1)
            for table in (agg_dst, agg_src):
                flat = table.rearrange("(p j) c -> p (j c)", p=P)
                for k in range(NJ // ZJ):
                    sp.dma_start(flat[:, k * ZJ * TW:(k + 1) * ZJ * TW], zeros[:, :]).then_inc(tables_zero, 16)
            for table in (by_dst, by_src):
                sp.dma_start(table[EP:EP + 1, :], cnt_m1).then_inc(tables_zero, 16)

            def load_row(i, u):
                wait(sp, row_out[u], i * 32)
                sp.dma_start(rowt[:, u, :], attr_in.rearrange("(t p) c -> t p c", p=P)[i * 2 + u]).then_inc(row_in[u], 16)
            loop(sp, HT, load_row)
            for u in range(2):
                sp.wait_ge(row_out[u], 32 * HT)
            sp.wait_ge(tables_zero, TABLES_ZERO)
            for r, table in enumerate((by_dst, by_src)):
                key = table[:, KEY_OF[r]:KEY_OF[r] + 1]
                sp.dma_start(keys2[:, r, 1:2 * P + 1].unsqueeze(2), key[0:EP, :].rearrange("(p n) c -> p n c", p=HP), allow_slow_non_contiguous=True).then_inc(keys_in_rows, 16)
                sp.dma_start(keys2[:, r, 2 * P + 1:2 * P + 2].unsqueeze(2), key[1:EP + 1, :].rearrange("(p n) c -> p n c", p=HP)[:, 2 * P - 1:2 * P, :], allow_slow_non_contiguous=True).then_inc(keys_in_rows, 16)
                sp.wait_ge(zeroed, 2)
                sp.dma_start(keys2[1:HP, r, 0:1].unsqueeze(2), key[0:EP, :].rearrange("(p n) c -> p n c", p=HP)[0:HP - 1, 2 * P - 1:2 * P, :], allow_slow_non_contiguous=True).then_inc(keys_in_rows, 16)
            sp.wait_ge(run_step, ROW_STEPS["link"])
            sp.dma_start(new_key.rearrange("(p n) -> p n", p=HP), link2[:, :]).then_inc(links_stored, 16)


        def prep_vector(dve):
            dve.memset(cnt_m1, -1.0)
            dve.memset(zeros[:, :], 0.0).then_inc(zeroed, 1)
            dve.memset(onesj[:, :], 1.0)
            dve.memset(ones_b[:, :], 1.0)
            dve.memset(M[:, :, :, :], 0.0)
            dve.memset(G[:, :, :, :], 0.0)
            dve.memset(MC[:, :, :, :], 0.0)
            dve.memset(MF[:, :, :], 0.0)
            dve.memset(MK[:, :, :], 0.0)
            dve.memset(keys2[:, :, :], -1.0).then_inc(zeroed, 1)
            dve.memset(YO[:, :, :, :], 0.0)
            dve.wait_ge(loaded, 64)
            dve.tensor_tensor(w[:, :], w[:, :], XG_w, ALU.mult).then_inc(setup_done["dve"], 1)
            dve.tensor_copy(ident_b[:, :], ident).then_inc(setup_done["dve"], 1)
            dve.wait_ge(setup_done["dve"], 2)
            for name, c0, c1, factor in (("o2s", 0, S, 3), ("o2s", S, S + V, 6), ("o2s", S + V, 160, 3), ("o2v", 0, V3, 4), ("o2v", V3, 192, 5)):
                dve.tensor_scalar(W(name, c0=c0, c1=c1), W(name, c0=c0, c1=c1), col(factor, V3), None, ALU.mult).then_inc(setup_done["dve"], 1)
            dve.wait_ge(setup_done["pe"], 1)
            dve.tensor_copy(W("oab0", r1=S, c0=P, c1=P + V), F[0][0:S, 0:V]).then_inc(setup_done["dve"], 1)
            dve.tensor_copy(W("of0", c0=P, c1=P + V), F[0][:, V:2 * V]).then_inc(setup_done["dve"], 1)
            shift, mask = ALU.arith_shift_right, ALU.bitwise_and
            for k, (op, n) in enumerate(((shift, 7), (mask, 127), (shift, 8), (mask, 255))):
                ins = dve.tensor_scalar(part_i[:, k, :, :], keys_i[:, :, :], n, None, op)
            ins.then_inc(count_step, 1)
            dve.wait_ge(count_step, SPLIT)
            dve.tensor_copy(key_f[:, :, :], keys_i[:, :, :])
            dve.tensor_copy(hi_f[:, :, :], part_i[:, 0, :, :])
            dve.tensor_copy(lo_f[:, :, :], part_i[:, 1, :, :])
            dve.tensor_copy(byte_f[:, 1, :, :], part_i[:, 3, :, :])
            dve.tensor_copy(byte_f[:, 2, :, :], part_i[:, 1, :, :])
            dve.tensor_scalar(byte_f[:, 0, :, :], part_i[:, 2, :, :], 256.0, None, ALU.mult).then_inc(count_step, 1)
            dve.wait_ge(count_step, CAST)

            def one_hots(t, u, done):
                for r in range(2):
                    dve.tensor_scalar(oh_hi[:, u, r, :], iota, hi_f[:, r, bass.ds(t, 1)], None, ALU.is_equal)
                    ins = dve.tensor_scalar(oh_lo[:, u, r, :], con[:, K_IOTA:K_IOTA + P], lo_f[:, r, bass.ds(t, 1)], None, ALU.is_equal)
                ins.then_inc(done, 1)

            def count(i, u):
                wait(dve, c_cnt, i * 2 + (u - 1))
                one_hots(i * 2 + u, u, c_hot)
            loop(dve, HT, count)

            dve.wait_ge(c_cnt, ET)
            for r in range(2):
                dve.tensor_copy(cnt[:, r, :], F[r][:, 0:NJ]).then_inc(count_step, 1)
            dve.wait_ge(count_step, COPY)
            for r in range(2):
                dve.tensor_tensor_scan(inc[:, r, :], onesj[:, :], cnt[:, r, :], 0.0, ALU.mult, ALU.add).then_inc(count_step, 1)
            dve.wait_ge(c_base, 1)
            dve.tensor_copy(bcol[:, :], F[2][:, 0:2]).then_inc(count_step, 1)
            dve.wait_ge(count_step, SCAN)
            for r in range(2):
                dve.tensor_tensor(offi[:, r, :], inc[:, r, :], cnt[:, r, :], ALU.subtract).then_inc(count_step, 1)
            dve.wait_ge(count_step, EXCL)
            for r in range(2):
                dve.tensor_scalar(off[:, 1, r, :], offi[:, r, :], bcol[:, r:r + 1], None, ALU.add).then_inc(count_step, 1)

            def ranks(i, u):
                t = i * 2 + u
                rows = F[2 + u]
                dve.wait_ge(c_row, t + 1)
                wait(dve, c_g, t - 1)
                dve.tensor_scalar(oht[:, u, :, :].rearrange("p r n -> p (r n)"), rows[:, 2 * P:4 * P], con[:, K_PIDX:K_PIDX + 1], None, ALU.is_equal).then_inc(c_oht, 1)
                wait(dve, c_rank, t)
                wait(dve, c_posi, t - 1)
                for r in range(2):
                    ins = dve.scalar_tensor_tensor(gt[:, r, :], rows[:, r * P:(r + 1) * P], key_f[:, r, bass.ds(t, 1)],
                                                   con[:, K_TRI:K_TRI + P], ALU.is_equal, ALU.mult, accum_out=pos[:, u, r, 0:1])
                ins.then_inc(c_rank, 1)

            def places(i, u):
                t = i * 2 + u
                dve.wait_ge(c_g, t + 1)
                wait(dve, c_pick, t)
                for r in range(2):
                    ins = dve.scalar_tensor_tensor(gj[:, r, :], reached(u, r), 1.0, oh_hi[:, u, r, :], ALU.mult, ALU.mult, accum_out=pos[:, u, r, 1:2])
                ins.then_inc(c_pick, 1)
                wait(dve, row_out[u], i * 32)
                dve.wait_ge(c_pick, t + 1)
                dve.tensor_tensor(pos_i[:, u, :], pos[:, u, :, 0], pos[:, u, :, 1], ALU.add).then_inc(c_posi, 1)

            def place(i, u, first, last):
                ranks(i, u)
                if not first:
                    places(i + (u - 1), 1 - u)
                if not last:
                    wait(dve, c_upd, i * 2 + u)
                    one_hots(i * 2 + (u + 1), 1 - u, c_hot2)
            one_hots(0, 0, c_hot2)
            loop_tiles(dve, place)
            places(HT - 1, 1)

            dve.wait_ge(keys_in_rows, 6 * 16)
            dve.tensor_copy(key2[:, :, :], keys2[:, :, :].bitcast(I32)).then_inc(run_step, 1)
            dve.wait_ge(run_step, ROW_STEPS["cast"])
            here = key2[:, :, 1:2 * P + 1]
            dve.tensor_tensor(next_eq[:, :, :], here, key2[:, :, 2:2 * P + 2], ALU.is_equal).then_inc(run_step, 1)
            dve.tensor_tensor(prev_eq[:, :, :], here, key2[:, :, 0:2 * P], ALU.is_equal).then_inc(run_step, 1)
            dve.memset(carry2[:, :, :], -1.0).then_inc(run_step, 1)
            dve.wait_ge(run_step, ROW_STEPS["equal"])
            dve.scalar_tensor_tensor(row_to2[:, :, :], next_eq[:, :, :], BIG, here, ALU.mult, ALU.add).then_inc(run_step, 1)
            dve.memset(same_tile[:, :, :], 0.0).then_inc(run_step, 1)
            dve.wait_ge(run_step, ROW_STEPS["equal"] + 2)
            halves = next_eq[:, :, :].rearrange("p r (h n) -> p r h n", h=2)
            same4 = same_tile[:, :, :].rearrange("p r (h n) -> p r h n", h=2)
            dve.tensor_copy(same4[:, :, :, 0:P - 1], halves[:, :, :, 0:P - 1]).then_inc(run_step, 1)
            dve.wait_ge(run_step, ROW_STEPS["equal"] + 3)
            place4 = place2[:, :, :].rearrange("p r (h n) -> p (r h) n", h=2)
            dve.scalar_tensor_tensor(place4, same_tile[:, :, :].rearrange("p r (h n) -> p (r h) n", h=2), 1.0,
                                     con[0:HP, K_IOTA:K_IOTA + P].unsqueeze(1).broadcast_to([HP, 4, P]), ALU.subtract, ALU.mult).then_inc(run_step, 1)
            dve.wait_ge(run_step, ROW_STEPS["parts"])
            for r in range(2):
                dve.tensor_tensor_scan(last2[:, r, 2 * P - 1::-1], same_tile[:, r, 2 * P - 1::-1], place2[:, r, 2 * P - 1::-1],
                                       0.0, ALU.mult, ALU.add).then_inc(run_step, 1)
            dve.wait_ge(run_step, ROW_STEPS["scan"])
            last4 = last2[:, :, :].rearrange("p r (h n) -> p r h n", h=2)
            prev4 = prev_eq[:, :, :].rearrange("p r (h n) -> p r h n", h=2)
            carry4 = carry2[:, :, :].rearrange("p r (h n) -> p r h n", h=2)
            dve.scalar_tensor_tensor(carry4[:, :, :, P - 1:P], last4[:, :, :, 0:1], -1.0, prev4[:, :, :, 0:1], ALU.add, ALU.mult).then_inc(run_step, 1)
            dve.tensor_scalar(link2[:, :], prev_eq[:, 0, :], 1.0, -NEG, ALU.subtract, ALU.mult).then_inc(run_step, 1)
            dve.wait_ge(run_step, ROW_STEPS["link"])
            dve.tensor_scalar(carry4[:, :, :, P - 1:P], carry4[:, :, :, P - 1:P], -1.0, -1.0, ALU.mult, ALU.add).then_inc(run_step, 1)
            dve.wait_ge(turned, 1)
            for r in range(2):
                pairs = F[r][:, 0:4 * HP].rearrange("p (k h t) -> p k t h", k=2, h=2)
                dve.tensor_scalar(LAST[:, r, :].rearrange("p (t h) -> p t h", h=2), pairs[:, 0, :, :], -1.0, None, ALU.mult).then_inc(tables_ready, 1)
                dve.tensor_copy(CARRY[:, r, :].rearrange("p (t h) -> p t h", h=2), pairs[:, 1, :, :])
                dve.tensor_copy(ROW_TO[:, r, :].rearrange("p (t h) -> p t h", h=2),
                                F[2][:, r * 2 * HP:(r + 1) * 2 * HP].rearrange("p (h t) -> p t h", h=2)).then_inc(tables_ready, 1)

        def prep_tensor(pe):
            pe.wait_ge(setup_done["dve"], 2)
            pe.matmul(F[0][0:S, 0:V], W("vst"), W("wg"), start=True, stop=True)
            pe.matmul(F[0][:, V:2 * V], W("vst2"), W("wg"), start=True, stop=True).then_inc(setup_done["pe"], 1)
            pe.wait_ge(setup_done["dve"], 9)
            pe.wait_ge(zeroed, 1)
            for r in range(2):
                pe.matmul(F[r][:, 0:NJ], ident_b[:, :], zeros_b[:, 0:NJ], start=True, stop=False, skip_group_check=True)

            def count(i, u):
                pe.wait_ge(c_hot, i * 2 + (u + 1))
                for r in range(2):
                    ins = pe.matmul(F[r][:, 0:NJ], oh_lo[:, u, r, :], oh_hi[:, u, r, :], start=False, stop=False, skip_group_check=True)
                ins.then_inc(c_cnt, 1)
            loop(pe, HT, count)

            pe.wait_ge(count_step, SCAN)
            for r in range(2):
                ins = pe.matmul(F[2][:, r:r + 1], con[:, K_TRIU:K_TRIU + P], inc[:, r, NJ - 1:NJ], start=True, stop=True)
            ins.then_inc(c_base, 1)
            pe.wait_ge(count_step, FIRST_PLACE)
            for r in range(2):
                ins = pe.matmul(O[:, r, 0:NJ], ident, off[:, 1, r, :], start=True, stop=False, skip_group_check=True)
            ins.then_inc(c_seed, 1)

            def key_rows(t, u):
                pe.wait_ge(c_dg, t + 1)
                wait(pe, c_rank, t - 1)
                for k, at in ((0, 0), (1, 0), (2, 2 * P)):
                    ins = pe.matmul(F[2 + u][:, at:at + 2 * P], ones_b[:, :], dg[:, u, k, :, :].rearrange("p r n -> p (r n)"),
                                    start=k != 1, stop=k > 0, skip_group_check=True)
                ins.then_inc(c_row, 1)

            def place(i, u, first, last):
                t = i * 2 + u
                pe.wait_ge(c_hot2, t + 1)
                pe.wait_ge(c_offs, t + 1)
                for r in range(2):
                    ins = pe.matmul(O[:, r, 0:NJ], oh_lo[:, u, r, :], oh_hi[:, u, r, :], start=False, stop=False, skip_group_check=True)
                ins.then_inc(c_upd, 1)
                if not last:
                    key_rows(t + 1, 1 - u)
                pe.wait_ge(c_oht, t + 1)
                wait(pe, c_pick, t - 1)
                for r in range(2):
                    ins = pe.matmul(reached(u, r), oht[:, u, r, :], off[:, u, r, :], start=True, stop=True)
                ins.then_inc(c_g, 1)
            key_rows(0, 0)
            loop_tiles(pe, place)

            pe.wait_ge(run_step, ROW_STEPS["link"] + 1)
            pe.sem_inc(gate, 1)
            for r in range(2):
                for h in range(2):
                    n = slice(h * P, (h + 1) * P)
                    for k, src in enumerate((last2, carry2)):
                        at = (k * 2 + h) * HP
                        pe.transpose(F[r][:, at:at + HP], src[:, r, n], ident[0:HP, 0:HP])
                    at = (r * 2 + h) * HP
                    ins = pe.transpose(F[2][:, at:at + HP], row_to2[:, r, n], ident[0:HP, 0:HP])
            ins.then_inc(turned, 1)

        zeros_b = zeros[:, 0:NJ].bitcast(BF16)

        def prep_scalar(act):
            def diagonals(t, u):
                wait(act, c_row, t - 1)
                act.sem_inc(gate, 1)
                for k in range(3):
                    for r in range(2):
                        ins = act.activation(dg[:, u, k, r, :], ident, ACT.Copy, scale=byte_f[:, k, r, bass.ds(t, 1)])
                ins.then_inc(c_dg, 1)

            def offsets(i, u):
                wait(act, c_upd, i * 2 + u)
                for r in range(2):
                    ins = act.copy(off[:, u, r, :], O[:, r, 0:NJ])
                ins.then_inc(c_offs, 1)

            def place(i, u, first, last):
                offsets(i, u)
                if not last:
                    diagonals(i * 2 + (u + 1), 1 - u)
            act.wait_ge(count_step, CAST)
            diagonals(0, 0)
            act.wait_ge(c_seed, 1)
            loop_tiles(act, place)

        def prep_pool(pool):
            pool.wait_ge(tables_zero, 16 * (2 * (NJ // ZJ) + 2))

            def scatter(i, u):
                pool.wait_ge(row_in[u], i * 16 + 16)
                pool.wait_ge(c_posi, i * 2 + (u + 1))
                pool.sem_inc(gate, 1)
                for r, table in enumerate((by_dst, by_src)):
                    pool.indirect_dma_start(out=table[0:EP, :], out_offset=bass.IndirectOffsetOnAxis(ap=pos_i[:, u, r:r + 1], axis=0),
                                            in_=rowt[:, u, :], in_offset=None).then_inc(row_out[u], 16)

            def place(i, u, first, last):
                if not first:
                    scatter(i + (u - 1), 1 - u)
            loop_tiles(pool, place)
            scatter(HT - 1, 1)
            for u in range(2):
                pool.wait_ge(row_out[u], 32 * HT)

        HALF = EG // 2

        def two_before(eng, name, L, i, u, per=1):
            before(eng, name, L, i, u - 1, per)

        def loop_edges(eng, body):
            for u in range(2):
                body(0, u, True, True)
            with eng.Fori(1, HALF - 1) as i:
                for u in range(2):
                    body(i, u, True, True)
            for u in range(2):
                body(HALF - 1, u, u == 0, False)

        def edge_sync(sp, L):
            if L == 0:
                stores_before(sp, 0)
            rows = A_OF[L][0:EP, :].rearrange("(g q p) c -> g p q c", q=Q, p=P)
            links = new_key.rearrange("(g n) -> g n", n=GRP)

            def load(i, u):
                if not isinstance(i, int) or i > 0:
                    if L == 0:
                        on(sp, "d_xn", L, i - 1, u)
                        on(sp, "l_rb", L, i - 1, u)
                    else:
                        on(sp, "p_at", L, i - 1, u)
                sp.dma_start(A[:, u, :, :], rows[i * 2 + u]).then_inc(row_ready[u], 16)
                if L == 0:
                    two_before(sp, "d_mb", L, i, u)
                    sp.dma_start(MK[:, u, 0:GRP], links[bass.ds(i * 2 + u, 1), :].broadcast_to([H, GRP])).then_inc(link_ready[u], 16)
            if L:
                for v in range(2):
                    if L == 1:
                        on(sp, "d_xn", 0, HALF - 1, v)
                        on(sp, "l_rb", 0, HALF - 1, v)
                    else:
                        on(sp, "p_at", L - 1, HALF - 1, v)
            loop(sp, HALF, load)

        def gathered_base(L):
            return 16 * Q * HALF * (L + 1 if L else 0)

        def edge_pool(pool, L):
            stores_before(pool, L)

            def gather(i, u):
                pool.wait_ge(row_ready[u], i * 16 + 16 * (HALF * L + 1))
                pool.sem_inc(gate, 1)
                for q in range(Q):
                    idx = A[:, u, q, OTHER[L]:OTHER[L] + 1].bitcast(I32)
                    pool.indirect_dma_start(out=XG[:, u, q, S:S + XW], out_offset=None, in_=X_OF[L],
                                            in_offset=bass.IndirectOffsetOnAxis(ap=idx, axis=0)).then_inc(gathered[u], 16)
                    if L == 0:
                        idx = A[:, u, q, KEY[L]:KEY[L] + 1].bitcast(I32)
                        pool.indirect_dma_start(out=XD[:, u, q, :], out_offset=None, in_=X_OF[L],
                                                in_offset=bass.IndirectOffsetOnAxis(ap=idx, axis=0)).then_inc(gathered[u], 16)

            def cross(i, u, k):
                on(pool, f"a_dx{k}", L, i, u)
                pool.tensor_tensor(xd(C1[:, u, :, :]), xd(DX[:, u, :, V:4 * V]), bd(ER[:, u, :, 2:5]), ALU.mult)
                pool.tensor_tensor(xd(C2[:, u, :, :]), xd(DX[:, u, :, 2 * V:5 * V]), bd(ER[:, u, :, 1:4]), ALU.mult).then_inc(sems[f"l_c{k}"], 1)

            def dot(src, dst, i, u, wait, name):
                on(pool, wait, L, i, u)
                pool.tensor_tensor(dst.rearrange("p q (d x) -> p q d x", x=3), src.rearrange("p q (d x) -> p q d x", x=3),
                                   ER[:, u, :, 0:3].unsqueeze(2).broadcast_to([P, Q, V, 3]), ALU.mult).then_inc(sems[name], 1)

            def prepare(i, u):
                if L == 0:
                    on(pool, "d_er", L, i, u)
                    before(pool, "p_at", L, i, u)
                    pool.tensor_tensor(RB[:, u, :, 0:16], A[:, u, :, A16:A16 + 16], ER[:, u, :, 5:6].to_broadcast([P, Q, 16]), ALU.mult)
                    pool.tensor_copy(RB[:, u, :, 16:32], A[:, u, :, A16:A16 + 16]).then_inc(sems["l_rb"], 1)
                    dot(XN[:, :, P:P + V3], DOT[:, :, 0:V3], i, u, "d_xn", "l_dot")
                    dot(XN[:, :, 2 * P:2 * P + V3], DOT[:, :, V3:2 * V3], i, u, "d_xn", "l_dot2")
                    return
                if L == 3:
                    on(pool, "d_sq", L, i, u)
                    pool.tensor_tensor(KN[:, u, :], SM3[:, u, :, 0], con[:, K_HALF:K_HALF + Q], ALU.pow).then_inc(sems["l_rn"], 1)
                before(pool, "d_dt", L, i, u)
                dot(XG[:, u, :, 2 * S:2 * S + V3], DOT[:, :, 0:V3], i, u, "d_er", "l_dot")
                if L in L12:
                    pool.tensor_tensor(XG[:, u, :, 0:S], XG[:, u, :, S:2 * S],
                                       ER[:, u, :, 5:6].to_broadcast([P, Q, S]), ALU.mult).then_inc(sems["l_se"], 1)

            def deviations(i, u):
                on(pool, "d_var", L, i, u)
                pool.tensor_tensor(RST[:, u, :, :, :].rearrange("p a q r -> p (a q r)"),
                                   STAT[:, u, :, :, :].rearrange("p a q r -> p (a q r)"),
                                   con[:, K_HALF:K_HALF + 16], ALU.pow).then_inc(sems["l_rstd"], 1)

            def attention(i, u):
                cross(i, u, 1)
                on(pool, "a_tanh", L, i, u)
                pool.sem_inc(gate, 1)
                pool.tensor_scalar(SG[:, :, :], SG[:, :, :], 0.5, 0.5, ALU.mult, ALU.add).then_inc(sems["l_sg"], 1)
                on(pool, "d_la", L, i, u)
                pool.tensor_tensor(LA[:, :, :], LA[:, :, :], W("adot").unsqueeze(1).broadcast_to([P, Q, S]), ALU.mult).then_inc(sems["l_la"], 1)

            def body(i, u, more, more2):
                if L in CONV:
                    if L in CROSS:
                        cross(i, u, 1)
                    if not (isinstance(i, int) and i == u == 0):
                        scatter(i + (u - 1), 1 - u)
                    if more2:
                        gather(i + 1, u)
                        prepare(i + 1, u)
                else:
                    if more2:
                        gather(i + 1, u)
                    cross(i, u, 2)
                    if more2:
                        deviations(i + 1, u)
                        prepare(i + 1, u)
                    if more:
                        attention(i + u, 1 - u)
                    scatter(i, u)

            def scatter(i, u):
                on(pool, "d_car", L, i, u)
                on(pool, "a_sum", L, i, u, per=Q, k=Q - 1)
                if L == 0:
                    on(pool, "a_g", L, i, u)
                pool.sem_inc(gate, 1)
                for q in range(Q):
                    src = (M if L else G)[:, u, q, :]
                    pool.indirect_dma_start(out=TABLE[L], out_offset=bass.IndirectOffsetOnAxis(ap=IDX[:, u, q:q + 1], axis=0),
                                            in_=src, in_offset=None, bounds_check=NP - 1, oob_is_err=False).then_inc(scattered[u], 16)
            for u in range(2):
                gather(0, u)
            for u in range(2):
                if L == 0:
                    deviations(0, u)
                prepare(0, u)
            if L == 0:
                attention(0, 0)
            loop_edges(pool, body)
            if L:
                scatter(HALF - 1, 1)

        def edge_tensor(pe, L):
            stores_before(pe, L)
            k_at = ATR[L]

            def flip(bank, rows, src, name):
                pe.sem_inc(gate, 1)
                for q in range(Q):
                    ins = pe.transpose(bank[0:rows, q * P:(q + 1) * P], src(q), ident)
                ins.then_inc(sems[name], 1)

            def product(bank, name, lhsT, rhs):
                pe.matmul(bank[0:lhsT.shape[1], :], lhsT, rhs, start=True, stop=True).then_inc(sems[name], 1)

            def turn(i, u):
                xs = XG[:, u, :, :]
                if L == 0:
                    on(pe, "d_dt", L, i, u)
                    two_before(pe, "a_fv", L, i, u)
                    flip(F[0], P, lambda q: XN[:, q, 0:P], "p_xts")
                    two_before(pe, "a_g", L, i, u)
                    before(pe, "d_p5", L, i, u)
                    flip(F[1], P, lambda q: XN[:, q, P:2 * P], "p_xtv")
                    two_before(pe, "a_fs", L, i, u)
                    flip(F[2], P, lambda q: XN[:, q, 2 * P:3 * P], "p_xtd")
                    on(pe, "l_rb", L, i, u)
                    flip(F[3], k_at, lambda q: RB[:, u, q, :], "p_at")
                    return
                on(pe, "d_dt", L, i, u)
                if L in L12:
                    on(pe, "l_se", L, i, u)
                before(pe, "d_p3", L, i, u)
                flip(F[0], HSK[L], (lambda q: xs[:, q, 0:P]) if L < 3 else (lambda q: xs[:, q, S:2 * S]), "p_xts")
                before(pe, "d_p5" if L != 2 else "a_v", L, i, u)
                flip(F[1], P, lambda q: xs[:, q, 2 * S:2 * S + P], "p_xtv")
                before(pe, "d_p1", L, i, u)
                flip(F[2], k_at, lambda q: A[:, u, q, ATC[L]:ATC[L] + k_at], "p_at")

            def scalars(i, u):
                if L:
                    on(pe, "a_at", L, i, u)
                    before(pe, "a_hid", L, i, u)
                    pe.sem_inc(gate, 1)
                    product(F[3], "p_hid", W(f"fc{L}"), AT[0:k_at, u, :])
                on(pe, "a_xts", L, i, u)
                product(F[0], "p_hs", W(f"hs{L}"), XTs[0:HSK[L], u, :])

            def hidden(u):
                return HID[0:HIDK[L], u, :] if L else AT[0:k_at, u, :]

            def vectors(i, u):
                on(pe, "a_xtv", L, i, u)
                if L:
                    product(F[1], "p_hv", W(f"hv{L}"), XTv[:, u, :])
                else:
                    on(pe, "a_xtd", L, i, u)
                    pe.matmul(F[1][:, :], W("hv0"), XTv[:, u, :], start=True, stop=False)
                    pe.matmul(F[1][:, :], W("hvd0"), XTd[:, :], start=False, stop=True).then_inc(sems["p_hv"], 1)

            def scalar_weights(i, u):
                on(pe, ("a_at", "d_hid", "a_hid", "a_hid")[L], L, i, u)
                product(F[2], "p_wab", W(f"wab{L}"), hidden(u))

            def vector_weights(i, u):
                on(pe, "a_s2", L, i, u)
                product(F[0], "p_w3", W(f"w34{L}"), hidden(u))

            def cross_weights(i, u):
                if L in CROSS:
                    on(pe, "a_v", L, i, u)
                    product(F[1], "p_w5", W(f"w5{L}"), hidden(u))

            def outputs(i, u):
                before(pe, "a_sum", L, i, u, per=Q)
                on(pe, "d_p1", L, i, u)
                sw = PLAN[f"of{L}"][2]
                for q in range(Q):
                    e = slice(q * P, (q + 1) * P)
                    pe.matmul(O[:, q, 0:sw + V], P1[:, u, e], W(f"oab{L}"), start=True, stop=False, skip_group_check=True)
                on(pe, "d_p3", L, i, u)
                for q in range(Q):
                    e = slice(q * P, (q + 1) * P)
                    pe.matmul(O[:, q, 0:sw], P3[:, u, e], W(f"of{L}"), start=False, stop=True, skip_group_check=True)
                    ins = pe.matmul(O[:, q, sw + V:sw + V + V3], P3[:, u, e], W(f"oc{L}"), start=True, stop=True, skip_group_check=True)
                if L in CROSS:
                    on(pe, "d_p5", L, i, u)
                    for q in range(Q):
                        e = slice(q * P, (q + 1) * P)
                        ins = pe.matmul(O[:, q, sw + V + V3:sw + V + 2 * V3], P5[0:V3, u, e], W(f"od{L}"), start=True, stop=True, skip_group_check=True)
                ins.then_inc(sems["p_out"], 1)

            def sum_rows(i, u, q):
                to = O[:, q, MAT[L]:MAT[L] + MW[L]]
                pe.matmul(to, SEL[:, u, q, :], MSG[:, u, q, 0:MW[L]], start=True, stop=False, skip_group_check=True)
                if q:
                    on(pe, "a_sum", L, i, u, per=Q, k=q - 1)
                    prev = M[:, u, q - 1, 0:MW[L]]
                else:
                    prev = M[:, 1 - u, Q - 1, 0:MW[L]] if L else MPS[:, 0:MW[L]]
                pe.matmul(to, CAR[:, u, q, :], prev, start=False, stop=True, skip_group_check=True).then_inc(sems["p_sum"], 1)

            def first(i, u):
                turn(i, u)
                scalars(i, u)
                vectors(i, u)
                scalar_weights(i, u)
                vector_weights(i, u)
                cross_weights(i, u)

            def body(i, u, more, more2):
                j, v = i + u, 1 - u
                outputs(i, u)
                if more:
                    turn(j, v)
                    scalars(j, v)
                    vectors(j, v)
                on(pe, "d_car", L, i, u)
                on(pe, "d_v1", L, i, u)
                on(pe, "a_msg_s", L, i, u)
                for q, piece in enumerate((scalar_weights, vector_weights, cross_weights, None)):
                    sum_rows(i, u, q)
                    if more and piece:
                        piece(j, v)

            def attention_body(i, u, more, more2):
                j, v = i + u, 1 - u
                if more:
                    turn(j, v)
                    scalars(j, v)
                    vectors(j, v)
                    on(pe, "a_at", 0, j, v)
                else:
                    before(pe, "a_g", 0, i, u)
                on(pe, "d_ae", 0, i, u)
                flip(F[3], H, lambda q: AE[:, q, :], "p_ae")
                if more:
                    scalar_weights(j, v)
                    vector_weights(j, v)
                on(pe, "d_mb", 0, i, u)
                pe.sem_inc(gate, 1)
                for q in range(Q):
                    pe.matmul(F[3][:, q * H:(q + 1) * H], MB[:, q * P:(q + 1) * P], con[0:H, K_ID:K_ID + H], start=True, stop=True)
                pe.matmul(F[3][:, 16:16 + H], MB[:, 0:1].to_broadcast([H, P]), con[0:H, K_ID:K_ID + H], start=True, stop=True).then_inc(sems["p_mc"], 1)
                if more:
                    cross_weights(j, v)
                on(pe, "d_dot", 0, i, u)
                if more:
                    on(pe, "d_p1", 0, j, v)
                    on(pe, "d_p3", 0, j, v)
                flip(F[2], V3, lambda q: SG[:, q, :], "p_ta")
                flip(F[0], V3, lambda q: VV[:, q, :], "p_tv")
                on(pe, "a_ta", 0, i, u)
                on(pe, "a_tv", 0, i, u)
                for q in range(Q):
                    e = slice(q * P, (q + 1) * P)
                    pe.matmul(O[:, q, 0:160], TA[0:V3, e], W("o2s"), start=True, stop=True, skip_group_check=True)
                    ins = pe.matmul(O[:, q, 160:352], TV[0:V3, e], W("o2v"), start=True, stop=True, skip_group_check=True)
                ins.then_inc(sems["p_out2"], 1)
                on(pe, "d_car", 0, i, u)
                on(pe, "d_msg", 0, i, u)
                on(pe, "d_mps", 0, i, u)
                for q in range(Q):
                    sum_rows(i, u, q)
                if more:
                    outputs(j, v)
                on(pe, "d_mn", 0, i, u)
                flip(F[2], S, lambda q: MN[:, q, 0:S], "p_fs")
                flip(F[0], V3, lambda q: MN[:, q, S:C], "p_fv")
                on(pe, "a_fs", 0, i, u)
                on(pe, "a_fv", 0, i, u)
                for q in range(Q):
                    e = slice(q * P, (q + 1) * P)
                    bank, at = F[1 + 2 * (q // 2)], q % 2 * C
                    pe.matmul(bank[:, at:at + S], TA[0:S, e], W("fs"), start=True, stop=True, skip_group_check=True)
                    ins = pe.matmul(bank[:, at + S:at + C], TV[0:V3, e], W("fv"), start=True, stop=True, skip_group_check=True)
                ins.then_inc(sems["p_g"], 1)
            first(0, 0)
            if L == 0:
                outputs(0, 0)
            loop_edges(pe, body if L else attention_body)

        def edge_scalar(act, L):
            stores_before(act, L)

            def move(dst, src, name, wait, i, u, **kw):
                on(act, wait, L, i, u)
                if kw:
                    act.activation(dst, src, **kw).then_inc(sems[name], 1)
                else:
                    act.copy(dst, src).then_inc(sems[name], 1)

            def spread_d(i, u, k, at):
                act.copy(DX[:, u, :, 0:V3], O[:, :, at:at + V3])
                act.copy(DX[:, u, :, V3:160], O[:, :, at:at + 2 * V]).then_inc(sems[f"a_dx{k}"], 1)

            def squares(i, u):
                on(act, "d_cent", L, i, u)
                act.activation(XSQ[:, :, :, 0:S], XN[:, :, 0:P].rearrange("p q (r c) -> p q r c", r=2), ACT.Square)
                act.activation(XSQ[:, :, 0, S:C], XG[:, u, :, 2 * S:2 * S + V3], ACT.Square)
                act.activation(XSQ[:, :, 1, S:C], XD[:, u, :, S:C], ACT.Square).then_inc(sems["a_sq"], 1)

            def turned(i, u):
                if L == 0:
                    move(XTs[:, u, :], F[0][:, :], "a_xts", "p_xts", i, u, func=ACT.Identity, scale=col(0), bias=col(1))
                    move(XTv[:, u, :], F[1][:, :], "a_xtv", "p_xtv", i, u, func=ACT.Identity, scale=col(2))
                    move(XTd[:, :], F[2][:, :], "a_xtd", "p_xtd", i, u, func=ACT.Identity, scale=col(2))
                    move(AT[0:ATR[L], u, :], F[3][0:ATR[L], :], "a_at", "p_at", i, u)
                else:
                    move(XTs[0:HSK[L], u, :], F[0][0:HSK[L], :], "a_xts", "p_xts", i, u)
                    move(XTv[:, u, :], F[1][:, :], "a_xtv", "p_xtv", i, u)
                    move(AT[0:ATR[L], u, :], F[2][0:ATR[L], :], "a_at", "p_at", i, u)

            def scalars(i, u):
                if L == 1:
                    move(HSG[0:S, :], F[3][0:S, :], "a_sig", "p_hid", i, u, func=ACT.Tanh, scale=0.5)
                    act.copy(HID[0:S, u, :], F[3][0:S, :]).then_inc(sems["a_hid"], 1)
                elif L:
                    move(HID[0:HIDK[L], u, :], F[3][0:HIDK[L], :], "a_hid", "p_hid", i, u, func=ACT.Relu)
                move(S2[:, u, :], F[0][:, :], "a_s2", "p_hs", i, u)

            def vectors(i, u):
                move(VT[:, u, :], F[1][:, :], "a_v", "p_hv", i, u)

            def sum_rows(i, u, q):
                on(act, "p_sum", L, i, u, per=Q, k=q)
                act.copy(M[:, u, q, 0:MW[L]], O[:, q, MAT[L]:MAT[L] + MW[L]]).then_inc(sems["a_sum"], 1)

            def first(i, u):
                turned(i, u)
                scalars(i, u)
                vectors(i, u)

            def body(i, u, more, more2):
                j, v = i + u, 1 - u
                on(act, "p_out", L, i, u)
                if L in CROSS:
                    spread_d(i, u, 1, 224)
                act.copy(MSG[:, u, :, 0:SW[L]], O[:, :, 0:SW[L]]).then_inc(sems["a_msg_s"], 1)
                if more:
                    turned(j, v)
                    scalars(j, v)
                    vectors(j, v)
                wait(act, scattered[u], i * (16 * Q) + 16 * Q * (HALF * L))
                for q in range(Q):
                    sum_rows(i, u, q)

            def outputs(i, u):
                on(act, "p_out", L, i, u)
                spread_d(i, u, 1, 288)
                act.activation(SG[:, :, :], O[:, :, S:160], ACT.Tanh, scale=0.5).then_inc(sems["a_tanh"], 1)
                act.activation(LA[:, :, :], O[:, :, 0:S], ACT.Copy, scale=0.2).then_inc(sems["a_la"], 1)

            def attention_body(i, u, more, more2):
                j, v = i + u, 1 - u
                if more:
                    turned(j, v)
                    scalars(j, v)
                    vectors(j, v)
                move(AET[:, :], F[3][0:H, :], "a_ae", "p_ae", i, u)
                on(act, "p_mc", L, i, u)
                act.copy(MC[:, u, :, :].rearrange("p q h -> p (q h)"), F[3][:, 0:16]).then_inc(sems["a_mc"], 1)
                on(act, "d_sub", L, i, u)
                act.activation(MSG[:, u, :, C:C + H], AE[:, :, :], ACT.Exp).then_inc(sems["a_exp"], 1)
                on(act, "d_res", L, i, u)
                act.activation(RES[:, :], RES[:, :], ACT.Exp).then_inc(sems["a_res"], 1)
                move(TA[0:V3, :], F[2][0:V3, :], "a_ta", "p_ta", i, u)
                move(TV[0:V3, :], F[0][0:V3, :], "a_tv", "p_tv", i, u)
                if more2:
                    squares(i + 1, u)
                on(act, "p_out2", L, i, u)
                spread_d(i, u, 2, 256)
                act.copy(HS1[:, :, :], O[:, :, V3:160]).then_inc(sems["a_hs"], 1)
                for q in range(Q):
                    sum_rows(i, u, q)
                if more:
                    outputs(j, v)
                move(TA[0:S, :], F[2][0:S, :], "a_fs", "p_fs", i, u)
                move(TV[0:V3, :], F[0][0:V3, :], "a_fv", "p_fv", i, u)
                on(act, "p_g", L, i, u)
                wait(act, scattered[u], i * (16 * Q))
                for k in range(2):
                    ins = act.copy(G[:, u, 2 * k:2 * k + 2, 0:C], F[1 + 2 * k][:, 0:2 * C].rearrange("p (q c) -> p q c", q=2))
                ins.then_inc(sems["a_g"], 1)
            if L == 0:
                squares(0, 0)
            first(0, 0)
            if L == 0:
                squares(0, 1)
                outputs(0, 0)
            loop_edges(act, body if L else attention_body)

        def edge_vector(dve, L):
            stores_before(dve, L)
            DVE_GATHER = 16 * Q * (2 if L == 0 else 1)
            tables = 1 if L == 3 else 0

            def direction(i, u):
                dve.wait_ge(gathered[u], i * DVE_GATHER + gathered_base(L) + DVE_GATHER)
                at = A4 + 1
                if L in L12:
                    e4 = A[:, u, :, A4:A4 + 4]
                    dve.tensor_tensor(e4, e4, XG[:, u, :, S + C:S + C + 1].to_broadcast([P, Q, 4]), ALU.mult).then_inc(sems["d_kc"], 1)
                    on(dve, "d_kc", L, i, u)
                elif L == 3:
                    a3 = A[:, u, :, A3:A3 + 3]
                    dve.tensor_tensor(U[:, u, :, 0:3], a3, a3, ALU.mult).then_inc(sems["d_kc"], 1)
                    on(dve, "d_kc", L, i, u)
                    dve.tensor_reduce(SM3[:, u, :, 0:1], U[:, u, :, 0:3], AX.X, ALU.add).then_inc(sems["d_sq"], 1)
                    on(dve, "l_rn", L, i, u)
                    dve.tensor_tensor(A[:, u, :, A4:A4 + 3], a3, KN[:, u, :].unsqueeze(2).broadcast_to([P, Q, 3]), ALU.mult).then_inc(sems["d_rhat"], 1)
                    on(dve, "d_rhat", L, i, u)
                    at = A4
                if L != 3:
                    dve.tensor_copy(ER[:, u, :, 5:6], A[:, u, :, A4:A4 + 1])
                dve.tensor_copy(ER[:, u, :, 0:3], A[:, u, :, at:at + 3])
                dve.tensor_copy(ER[:, u, :, 3:5], A[:, u, :, at:at + 2]).then_inc(sems["d_er"], 1)

            def dot(i, u):
                on(dve, "l_dot", L, i, u)
                dve.tensor_reduce(XG[:, u, :, 2 * S + V3:2 * S + P].unsqueeze(3),
                                  DOT[:, :, 0:V3].rearrange("p q (d x) -> p q d x", x=3), AX.X, ALU.add).then_inc(sems["d_dt"], 1)

            def dots(i, u):
                for r, name in enumerate(("l_dot", "l_dot2")):
                    on(dve, name, L, i, u)
                    ins = dve.tensor_reduce(XN[:, :, P + r * P + V3:2 * P + r * P].unsqueeze(3),
                                            DOT[:, :, r * V3:(r + 1) * V3].rearrange("p q (d x) -> p q d x", x=3), AX.X, ALU.add)
                ins.then_inc(sems["d_dt"], 1)

            def selectors(i, u):
                tiles = bass.ds((i * 2 + u) * Q, Q)
                two_before(dve, "p_sum", L, i, u, per=Q)
                wait(dve, scattered[u], i * (16 * Q) + 16 * Q * (HALF * L))
                cols = con[:, K_IOTA:K_IOTA + P].unsqueeze(1).broadcast_to([P, Q, P])
                dve.tensor_copy(IDX[:, u, :], ROW_TO[:, tables, tiles])
                dve.tensor_tensor(SEL[:, u, :, :], cols, LAST[:, tables, tiles].unsqueeze(2).broadcast_to([P, Q, P]), ALU.is_equal)
                dve.tensor_tensor(CAR[:, u, :, :], cols, CARRY[:, tables, tiles].unsqueeze(2).broadcast_to([P, Q, P]), ALU.is_equal).then_inc(sems["d_car"], 1)

            def mult(dst, bank, src, rows, wait, name, i, u):
                on(dve, wait, L, i, u)
                dve.tensor_tensor(dst[0:rows, u, :], bank[0:rows, :], src[0:rows, u, :], ALU.mult).then_inc(sems[name], 1)

            def scalar_products(i, u):
                on(dve, "a_s2", L, i, u)
                mult(P1, F[2], S2, P, "p_wab", "d_p1", i, u)
                on(dve, "a_v", L, i, u)
                mult(P3, F[0], VT, P, "p_w3", "d_p3", i, u)

            def cross_products(i, u):
                if L in CROSS:
                    mult(P5, F[1], VT, V3, "p_w5", "d_p5", i, u)

            def vectors(dst, i, u, k, b, c, e0, cross):
                last = f"d_v{k}"
                out4 = xd(dst)
                ins = dve.tensor_tensor(out4, bx(O[:, :, b:b + V]), bd(ER[:, u, :, 0:3]), ALU.mult)
                if not e0:
                    ins.then_inc(sems[f"d_tb{k}"], 1)
                if e0:
                    dve.tensor_tensor(U[:, u, :, :], O[:, :, c:c + V3], ER[:, u, :, 5:6].to_broadcast([P, Q, V3]), ALU.mult).then_inc(sems[f"d_tb{k}"], 1)
                    add = U[:, u, :, :]
                else:
                    add = O[:, :, c:c + V3]
                on(dve, f"d_tb{k}", L, i, u)
                ins = dve.tensor_tensor(dst, dst, add, ALU.add)
                if not cross:
                    ins.then_inc(sems[last], 1)
                if cross:
                    on(dve, f"l_c{k}", L, i, u)
                    dve.tensor_tensor(C1[:, u, :, :], C1[:, u, :, :], C2[:, u, :, :], ALU.subtract).then_inc(sems[f"d_w{k}"], 1)
                    on(dve, f"d_w{k}", L, i, u)
                    dve.tensor_tensor(dst, dst, C1[:, u, :, :], ALU.add).then_inc(sems[last], 1)

            def variances(i, u):
                both = (XG[:, u, :, S:S + C], XD[:, u, :, 0:C])
                dve.wait_ge(gathered[u], i * DVE_GATHER + gathered_base(L) + DVE_GATHER)
                for r in range(2):
                    ins = dve.tensor_reduce(STAT[:, u, 0, :, r:r + 1], both[r][:, :, 0:S], AX.X, ALU.add)
                ins.then_inc(sems["d_mean"], 1)
                on(dve, "d_mean", L, i, u)
                before(dve, "p_xtd", L, i, u)
                for r in range(2):
                    mean = STAT[:, u, 0, :, r:r + 1].to_broadcast([P, Q, S])
                    ins = dve.scalar_tensor_tensor(XN[:, :, r * S:(r + 1) * S], both[r][:, :, 0:S], float(S), mean, ALU.mult, ALU.subtract)
                ins.then_inc(sems["d_cent"], 1)
                on(dve, "a_sq", L, i, u)
                dve.tensor_reduce(STAT[:, u, 0, :, :].unsqueeze(3), XSQ[:, :, :, 0:S], AX.X, ALU.add)
                dve.tensor_reduce(STAT[:, u, 1, :, :].unsqueeze(3), XSQ[:, :, :, S:C], AX.X, ALU.add).then_inc(sems["d_st"], 1)
                on(dve, "d_st", L, i, u)
                dve.tensor_scalar(STAT[:, u, 0, :, :], STAT[:, u, 0, :, :], 1.0 / S, float(S * S) * EPS, ALU.mult, ALU.add)
                dve.tensor_scalar(STAT[:, u, 1, :, :], STAT[:, u, 1, :, :], 1.0 / V, EPS, ALU.mult, ALU.add).then_inc(sems["d_var"], 1)

            def normalise(i, u):
                both = (XG[:, u, :, S:S + C], XD[:, u, :, 0:C])
                on(dve, "l_rstd", L, i, u)
                for r in range(2):
                    sc = slice(r * S, (r + 1) * S)
                    dve.tensor_tensor(XN[:, :, sc], XN[:, :, sc], RST[:, u, 0, :, r:r + 1].to_broadcast([P, Q, S]), ALU.mult)
                    vc = slice(P + r * P, P + r * P + V3)
                    ins = dve.tensor_tensor(XN[:, :, vc], both[r][:, :, S:C], RST[:, u, 1, :, r:r + 1].to_broadcast([P, Q, V3]), ALU.mult)
                ins.then_inc(sems["d_xn"], 1)

            def silu(i, u):
                if L == 1:
                    on(dve, "a_sig", L, i, u)
                    dve.tensor_scalar(HSG[0:S, :], HSG[0:S, :], 0.5, 0.5, ALU.mult, ALU.add).then_inc(sems["d_hsg"], 1)
                    on(dve, "d_hsg", L, i, u)
                    on(dve, "a_hid", L, i, u)
                    dve.tensor_tensor(HID[0:S, u, :], HID[0:S, u, :], HSG[0:S, :], ALU.mult).then_inc(sems["d_hid"], 1)

            def body(i, u, more, more2):
                on(dve, "a_msg_s", L, i, u)
                sw = SW[L]
                vectors(MSG[:, u, :, sw:sw + V3], i, u, 1, sw, sw + V, L in L12, L in CROSS)
                if more:
                    j, v = i + u, 1 - u
                    silu(j, v)
                    scalar_products(j, v)
                    cross_products(j, v)
                    selectors(j, v)
                if more2:
                    direction(i + 1, u)
                    dot(i + 1, u)

            def attention_body(i, u, more, more2):
                j, v = i + u, 1 - u
                on(dve, "a_la", L, i, u)
                dve.tensor_tensor(LA[:, :, :], LA[:, :, :], O[:, :, 0:S], ALU.max).then_inc(sems["d_la"], 1)
                vectors(VV[:, :, :], i, u, 1, 160, 192, False, True)
                on(dve, "l_la", L, i, u)
                dve.tensor_reduce(AE[:, :, :].unsqueeze(3), LA[:, :, :].rearrange("p q (h c) -> p q h c", h=H), AX.X, ALU.add).then_inc(sems["d_ae"], 1)
                on(dve, "l_sg", L, i, u)
                on(dve, "d_v1", L, i, u)
                dve.tensor_tensor(xd(VV[:, :, :]), xd(VV[:, :, :]), bx(SG[:, :, S:V3]), ALU.mult).then_inc(sems["d_gate"], 1)
                on(dve, "d_gate", L, i, u)
                dve.tensor_tensor(xd(U[:, u, :, :]), xd(VV[:, :, :]), bd(ER[:, u, :, 0:3]), ALU.mult).then_inc(sems["d_link"], 1)
                on(dve, "d_link", L, i, u, per=4, k=LINK["vy"])
                dve.tensor_reduce(SG[:, :, S:V3].unsqueeze(3), U[:, u, :, :].rearrange("p q (x d) -> p q d x", x=3), AX.X, ALU.add).then_inc(sems["d_dot"], 1)
                if more:
                    selectors(j, v)
                on(dve, "a_ae", L, i, u)
                dve.wait_ge(link_ready[u], i * 16 + 16)
                before(dve, "d_mf", L, i, u)
                dve.tensor_tensor_scan(MF[:, u, :], MK[:, u, 0:GRP], AET[:, :], MF[:, 1 - u, GRP - 1:GRP], ALU.add, ALU.max).then_inc(sems["d_mf"], 1)
                on(dve, "d_mf", L, i, u)
                dve.tensor_tensor_scan(MB[:, GRP - 1::-1], MK[:, u, GRP:0:-1], MF[:, u, GRP - 1::-1], NEG, ALU.add, ALU.max).then_inc(sems["d_mb"], 1)
                if more:
                    scalar_products(j, v)
                on(dve, "a_mc", L, i, u)
                dve.tensor_tensor(AE[:, :, :].rearrange("p q h -> p (q h)"), AE[:, :, :].rearrange("p q h -> p (q h)"), F[3][:, 0:16], ALU.subtract).then_inc(sems["d_sub"], 1)
                dve.tensor_tensor(RES[:, :], MC[:, 1 - u, Q - 1, :], F[3][:, 16:16 + H], ALU.subtract).then_inc(sems["d_link"], 1)
                on(dve, "d_link", L, i, u, per=4, k=LINK["res"])
                dve.tensor_scalar(RES[:, :], RES[:, :], 0.0, None, ALU.min).then_inc(sems["d_res"], 1)
                if more:
                    cross_products(j, v)
                on(dve, "a_res", L, i, u)
                before(dve, "a_sum", L, i, u, per=Q)
                old = M[:, 1 - u, Q - 1, :]
                heads(MPS[:, 0:S], old[:, 0:S], RES[:, :], HS)
                for k in range(3):
                    heads(MPS[:, S + k * V:S + (k + 1) * V], old[:, S + k * V:S + (k + 1) * V], RES[:, :], HV)
                dve.tensor_tensor(MPS[:, C:C + H], old[:, C:C + H], RES[:, :], ALU.mult).then_inc(sems["d_mps"], 1)
                if more2:
                    variances(i + 1, u)
                on(dve, "a_exp", L, i, u)
                on(dve, "a_hs", L, i, u)
                dve.tensor_tensor(U[:, u, :, 0:S], O[:, :, 0:S], ER[:, u, :, 5:6].to_broadcast([P, Q, S]), ALU.mult).then_inc(sems["d_link"], 1)
                on(dve, "d_link", L, i, u, per=4, k=LINK["hs"])
                dve.tensor_tensor(HS1[:, :, :], HS1[:, :, :], U[:, u, :, 0:S], ALU.add).then_inc(sems["d_hs"], 1)
                on(dve, "d_hs", L, i, u)
                ex = MSG[:, u, :, C:C + H]
                dve.tensor_tensor(MSG[:, u, :, 0:S].rearrange("p q (h c) -> p q h c", h=H), HS1[:, :, :].rearrange("p q (h c) -> p q h c", h=H),
                                  bd(ex, HS), ALU.mult)
                vectors(VV[:, :, :], i, u, 2, 64, 160, True, True)
                on(dve, "d_v2", L, i, u)
                for k in range(3):
                    c = slice(S + k * V, S + (k + 1) * V)
                    ins = dve.tensor_tensor(MSG[:, u, :, c].rearrange("p q (h c) -> p q h c", h=H),
                                            VV[:, :, k * V:(k + 1) * V].rearrange("p q (h c) -> p q h c", h=H), bd(ex, HV), ALU.mult)
                ins.then_inc(sems["d_msg"], 1)
                if more2:
                    direction(i + 1, u)
                    normalise(i + 1, u)
                on(dve, "a_sum", L, i, u, per=Q, k=Q - 1)
                dve.tensor_scalar(DEN[:, :, :], M[:, u, :, C:C + H], 1e-16, None, ALU.add).then_inc(sems["d_link"], 1)
                on(dve, "d_link", L, i, u, per=4, k=LINK["den"])
                dve.reciprocal(DEN[:, :, :], DEN[:, :, :]).then_inc(sems["d_rden"], 1)
                on(dve, "d_rden", L, i, u)
                dve.tensor_tensor(MN[:, :, 0:S].rearrange("p q (h c) -> p q h c", h=H), M[:, u, :, 0:S].rearrange("p q (h c) -> p q h c", h=H),
                                  bd(DEN[:, :, :], HS), ALU.mult)
                for k in range(3):
                    c = slice(S + k * V, S + (k + 1) * V)
                    ins = dve.tensor_tensor(MN[:, :, c].rearrange("p q (h c) -> p q h c", h=H), M[:, u, :, c].rearrange("p q (h c) -> p q h c", h=H),
                                            bd(DEN[:, :, :], HV), ALU.mult)
                ins.then_inc(sems["d_mn"], 1)
                if more2:
                    dots(i + 1, u)

            def heads(dst, src, factor, n):
                dve.tensor_tensor(dst.rearrange("p (h c) -> p h c", h=H), src.rearrange("p (h c) -> p h c", h=H),
                                  factor.unsqueeze(2).broadcast_to([P, H, n]), ALU.mult)

            def prepare_attention(i, u):
                variances(i, u)
                direction(i, u)
                normalise(i, u)
                dots(i, u)

            if L:
                for u in range(2):
                    direction(0, u)
                    dot(0, u)
            else:
                prepare_attention(0, 0)
            silu(0, 0)
            selectors(0, 0)
            scalar_products(0, 0)
            cross_products(0, 0)
            if L == 0:
                prepare_attention(0, 1)
            loop_edges(dve, body if L else attention_body)

        LINK = {"vy": 0, "res": 1, "hs": 2, "den": 3}

        PASSES = NG // DEPTH

        def loop_nodes(eng, body):
            for v in range(DEPTH):
                body(0, v, True, False)
            with eng.Fori(1, PASSES - 1) as i:
                for v in range(DEPTH):
                    body(i, v, False, False)
            for v in range(DEPTH):
                body(PASSES - 1, v, False, True)

        def after(i, v, n=1):
            return i + (v + n) // DEPTH, (v + n) % DEPTH

        def node_loaded(eng, L, i, v):
            turns = DEPTH // BUFS
            eng.wait_ge(node_in[v % BUFS], i * (32 * turns) + 32 * (PASSES * turns * L + v // BUFS + 1))

        def node_sync(sp, L):
            scatters_before(sp, L)
            stores_before(sp, L)
            xv = X_OF[L].rearrange("(p g q) c -> g p q c", g=NG, q=Q)
            tv = TABLE[L].rearrange("(p g q) c -> g p q c", g=NG, q=Q)
            ov = X_TO[L].rearrange("(p g q) c -> g p q c", g=NG, q=Q)
            gw = MW[L] if L else C
            width = XW if L < 3 else C

            def load(i, v):
                sp.dma_start(XI[:, v % BUFS, :, :], xv[i * DEPTH + v]).then_inc(node_in[v % BUFS], 16)
                sp.dma_start(GN[:, v % BUFS, :, 0:gw], tv[i * DEPTH + v][:, :, 0:gw]).then_inc(node_in[v % BUFS], 16)

            def store(i, v):
                onn(sp, "n_out", L, i, v)
                sp.dma_start(ov[i * DEPTH + v], YO[:, v % 2, :, 0:width]).then_inc(stored[v % 2], 16)

            def body(i, v, first, last):
                if not last or v + BUFS < DEPTH:
                    onn(sp, "n_y", L, i, v)
                    load(*after(i, v, BUFS))
                if not (first and v == 0):
                    store(*after(i, v, -1))
            for v in range(BUFS):
                load(0, v)
            loop_nodes(sp, body)
            store(PASSES - 1, DEPTH - 1)

        def node_tensor(pe, L):
            scatters_before(pe, L)
            if L == 0:
                return
            sw = PLAN[f"ns{L}"][2]

            def turn(i, v):
                s_bank, v_bank = F[2 * (v % 2)], F[2 * (v % 2) + 1]
                node_loaded(pe, L, i, v)
                onn(pe, "n_extv", L - 1, i, v, back=2)
                pe.sem_inc(gate, 1)
                for q in range(Q):
                    ins = pe.transpose(s_bank[0:S, q * P:(q + 1) * P], XI[:, v % BUFS, q, 0:S], ident)
                ins.then_inc(sems["n_xts"], 1)
                for q in range(Q):
                    ins = pe.transpose(v_bank[0:V3, q * P:(q + 1) * P], XI[:, v % BUFS, q, S:C], ident)
                ins.then_inc(sems["n_xtv"], 1)

            def body(i, v, first, last):
                if not (last and v == DEPTH - 1):
                    turn(*after(i, v))
                onn(pe, "n_t", L - 1, i, v, back=2)
                onn(pe, "n_exts", L - 1, i, v)
                onn(pe, "n_extv", L - 1, i, v)
                for q in range(Q):
                    e = slice(q * P, (q + 1) * P)
                    bank, at = 2 * (v % 2) + q // 2, q % 2 * (sw + V3)
                    pe.matmul(O[:, bank, at:at + sw], NTs[0:S, v % 2, e], W(f"ns{L}"), start=True, stop=True, skip_group_check=True)
                    ins = pe.matmul(O[:, bank, at + sw:at + sw + V3], NTv[0:V3, v % 2, e], W(f"nv{L}"), start=True, stop=True, skip_group_check=True)
                ins.then_inc(sems["n_lin"], 1)
            turn(0, 0)
            loop_nodes(pe, body)

        def node_scalar(act, L):
            scatters_before(act, L)

            def turned(i, v):
                onn(act, "n_lin", L - 1, i, v, back=2)
                onn(act, "n_xts", L - 1, i, v)
                act.copy(NTs[0:S, v % 2, :], F[2 * (v % 2)][0:S, :]).then_inc(sems["n_exts"], 1)
                onn(act, "n_xtv", L - 1, i, v)
                act.copy(NTv[0:V3, v % 2, :], F[2 * (v % 2) + 1][0:V3, :]).then_inc(sems["n_extv"], 1)

            def gates(i, v):
                onn(act, "n_ta" if L == 1 else "n_t", 0 if L == 1 else 2, i, v)
                act.activation(SIG[:, v % 2, :, :], T1[:, v % 2, :, 0:V3], ACT.Tanh, scale=0.5).then_inc(sems["n_sig"], 1)

            def write(i, v):
                u = v % 2
                onn(act, "n_nm", L, i, v)
                wait(act, stored[u], i * 16 * (DEPTH // 2) + 16 * (NG // 2 * L + v // 2))
                for q in range(Q):
                    ins = act.activation(YO[:, u, q, 0:C], Y[:, u, q, 0:C], ACT.Identity, scale=RS[:, u, q:q + 1], bias=NM[:, u, q:q + 1])
                if L < 3:
                    ins = act.copy(YO[:, u, :, C:C + 1], Y[:, u, :, C:C + 1])
                ins.then_inc(sems["n_out"], 1)

            def body(i, v, first, last):
                if L and not (last and v == DEPTH - 1):
                    turned(*after(i, v))
                if not (first and v < 2):
                    write(*after(i, v, -2))
                if L in (1, 3):
                    gates(i, v)
            if L:
                turned(0, 0)
            loop_nodes(act, body)
            for v in (DEPTH - 2, DEPTH - 1):
                write(PASSES - 1, v)

        def node_pool(pool, L):
            scatters_before(pool, L)

            def scale(i, v):
                u = v % 2
                if L in (1, 2):
                    onn(pool, "n_t", L - 1, i, v)
                    pool.tensor_tensor(T1[:, u, :, 0:MW[L]], T1[:, u, :, 0:MW[L]], XI[:, v % BUFS, :, C:C + 1].to_broadcast([P, Q, MW[L]]), ALU.mult).then_inc(sems["n_ta"], 1)
                if L in (1, 3):
                    onn(pool, "n_sig", 0 if L == 1 else 1, i, v)
                    pool.sem_inc(gate, 1)
                    pool.tensor_scalar(SIG[:, u, :, :], SIG[:, u, :, :], 0.5, 0.5, ALU.mult, ALU.add).then_inc(sems["n_sg2"], 1)

            def deviation(i, v):
                u = v % 2
                onn(pool, "n_mv", L, i, v)
                pool.sem_inc(gate, 1)
                pool.tensor_scalar(RS[:, u, :].unsqueeze(2), MV[:, u, :, 1:2], 1.0, EPS, ALU.mult, ALU.add).then_inc(sems["n_rs0"], 1)
                onn(pool, "n_rs0", L, i, v)
                pool.tensor_tensor(RS[:, u, :], RS[:, u, :], con[:, K_HALF:K_HALF + Q], ALU.pow).then_inc(sems["n_rs"], 1)

            def body(i, v, first, last):
                scale(i, v)
                if not (first and v < 1):
                    deviation(*after(i, v, -1))
            loop_nodes(pool, body)
            deviation(PASSES - 1, DEPTH - 1)

        def node_vector(dve, L):
            scatters_before(dve, L)

            def perm(ap):
                return ap.rearrange("p q (x d) -> p q d x", x=3)

            def chan(ap):
                return ap.rearrange("p q (d x) -> p q d x", x=3)

            def linear(i, v):
                if L:
                    sw = PLAN[f"ns{L}"][2]
                    node_loaded(dve, L, i, v)
                    onn(dve, "n_lin", L - 1, i, v)
                    n = sw + V3

                    def pairs(ap):
                        return ap.rearrange("p (b t) c -> p b t c", b=2)
                    bank = 2 * (v % 2)
                    dve.tensor_tensor(pairs(T1[:, v % 2, :, 0:n]), O[:, bank:bank + 2, 0:2 * n].rearrange("p b (t c) -> p b t c", t=2),
                                      pairs(GN[:, v % BUFS, :, 0:n]), ALU.add).then_inc(sems["n_t"], 1)

            def residual(i, v):
                u = v % 2
                xin = XI[:, v % BUFS, :, :]
                y = Y[:, u, :, 0:C]
                t = T1[:, u, :, :]
                onn(dve, "n_out", L, i, v, back=2)
                if L in (1, 2):
                    dve.tensor_copy(Y[:, u, :, C:C + 1], xin[:, :, C:C + 1])
                if L == 0:
                    g = GN[:, v % BUFS, :, :]
                    node_loaded(dve, L, i, v)
                    dve.tensor_copy(Y[:, u, :, C:C + 1], xin[:, :, C:C + 1])
                    dve.scalar_tensor_tensor(y[:, :, 0:S], xin[:, :, 0:S], 2.0, g[:, :, 0:S], ALU.mult, ALU.add)
                    for x in range(3):
                        ins = dve.scalar_tensor_tensor(y[:, :, S + x:C:3], xin[:, :, S + x:C:3], 2.0, g[:, :, S + x * V:S + (x + 1) * V], ALU.mult, ALU.add)
                    ins.then_inc(sems["n_y"], 1)
                elif L == 2:
                    onn(dve, "n_ta", 1, i, v)
                    dve.tensor_tensor(y[:, :, 0:S], t[:, :, 0:S], xin[:, :, 0:S], ALU.add)
                    dve.tensor_tensor(chan(y[:, :, S:C]), perm(t[:, :, S:C]), chan(xin[:, :, S:C]), ALU.add).then_inc(sems["n_y"], 1)
                else:
                    k = 0 if L == 1 else 1
                    onn(dve, "n_sg2", k, i, v)
                    if L == 1:
                        onn(dve, "n_ta", 0, i, v)
                    dve.tensor_tensor(y[:, :, 0:S], t[:, :, 0:S], SIG[:, u, :, 0:S], ALU.mult)
                    dve.tensor_tensor(chan(y[:, :, S:C]), perm(t[:, :, V3:2 * V3]), bd(SIG[:, u, :, S:V3], 3), ALU.mult).then_inc(sems["n_yv"], 1)
                    onn(dve, "n_yv", k, i, v)
                    dve.tensor_tensor(y, y, xin[:, :, 0:C], ALU.add).then_inc(sems["n_y"], 1)

            def moments(i, v):
                u = v % 2
                onn(dve, "n_y", L, i, v)
                for q in range(Q):
                    ins = dve.bn_stats(BN[:, u, q, :], Y[:, u, q, 0:C])
                ins.then_inc(sems["n_bn"], 1)
                onn(dve, "n_bn", L, i, v)
                dve.sem_inc(gate, 1)
                for q in range(Q):
                    ins = dve.bn_aggr(MV[:, u, q, :], BN[:, u, q, :])
                ins.then_inc(sems["n_mv"], 1)

            def shift(i, v):
                u = v % 2
                onn(dve, "n_rs", L, i, v)
                dve.scalar_tensor_tensor(NM[:, u, :], MV[:, u, :, 0], -1.0, RS[:, u, :], ALU.mult, ALU.mult).then_inc(sems["n_nm"], 1)

            def body(i, v, first, last):
                if not (last and v == DEPTH - 1):
                    linear(*after(i, v))
                if not (first and v == 0):
                    shift(*after(i, v, -1))
                residual(i, v)
                moments(i, v)
            linear(0, 0)
            loop_nodes(dve, body)
            shift(PASSES - 1, DEPTH - 1)

        block = ctx.enter_context(nc.Block())
        LAYERS = range(stop_after)

        @block.sync
        def _(sp):
            prep_sync(sp)
            for L in LAYERS:
                edge_sync(sp, L)
                node_sync(sp, L)
            for u in range(2):
                sp.wait_ge(stored[u], 16 * (NG // 2) * len(LAYERS))

        @block.gpsimd
        def _(pool):
            prep_pool(pool)
            for L in LAYERS:
                edge_pool(pool, L)
                node_pool(pool, L)

        @block.tensor
        def _(pe):
            prep_tensor(pe)
            for L in LAYERS:
                edge_tensor(pe, L)
                node_tensor(pe, L)

        @block.scalar
        def _(act):
            prep_scalar(act)
            for L in LAYERS:
                edge_scalar(act, L)
                node_scalar(act, L)

        @block.vector
        def _(dve):
            prep_vector(dve)
            for L in LAYERS:
                edge_vector(dve, L)
                node_vector(dve, L)


def pack(inputs):
    import numpy as np
    get = {k: np.asarray(v) for k, v in inputs.items()}
    wt, sc = np.zeros((P, WW), np.float32), np.ones((P, WW), np.float32)

    def put(name, r0, c0, matrix, scale=1.0):
        at = PLAN[name][1] + c0
        wt[r0:r0 + matrix.shape[0], at:at + matrix.shape[1]] = matrix
        sc[r0:r0 + matrix.shape[0], at:at + matrix.shape[1]] = scale

    def put3(name, matrix, scale=1.0, c0=0, inner=False):
        if inner and PLAN[name][0] == P:
            put(name, V3, c0 + V3, matrix, scale)
        at = PLAN[name][1] + c0
        for x in range(3):
            rows = slice(x, V3, 3) if inner else slice(x * V, (x + 1) * V)
            wt[rows, at + x * V:at + (x + 1) * V] = matrix
            sc[rows, at + x * V:at + (x + 1) * V] = scale

    def rep(matrix):
        return np.concatenate([matrix] * 3, axis=1)

    r2, r3 = 2.0 ** 0.5, 3.0 ** 0.5
    g = {k[7:]: v for k, v in get.items() if k.startswith("L0_gnn_")}
    for c0 in (0, S):
        put("hs0", 0, c0, g["Ws_src"])
        put("hs0", S, c0, g["Ws_dst"])
    put3("hv0", g["Wv_src"], inner=True)
    put3("hvd0", g["Wv_dst"], inner=True)
    rbf = g["W_rbf"]
    put("wab0", 0, 0, rbf[:, 0:S])
    put("wab0", 16, S, rbf[:, S:2 * S])
    put("w340", 0, 0, rep(rbf[:, 2 * S:2 * S + V]))
    put("w340", 16, V3, rbf[:, 2 * S + V:2 * S + 2 * V])
    put("w50", 16, 0, rep(rbf[:, 2 * S + 2 * V:]))
    put("oab0", 0, 0, g["W_alpha"][0:S])
    put("oab0", 0, S, g["Ws_val"][0:S])
    put("oab0", S, 160, g["Wv_val"][0:S])
    put("of0", V3, 0, g["W_alpha"][S:], 1 / r3)
    put("of0", V3, S, g["Ws_val"][S:], 1 / r3)
    put3("oc0", g["Wv_val"][S:S + V])
    put3("od0", g["Wv_val"][S + V:], 1 / r2)
    put("vst", 0, 0, g["Ws_val"][0:S].T)
    put("vst2", 0, V3, g["Ws_val"][S:].T, 1 / r3)
    put("wg", 0, 0, g["Wg"])
    put("o2s", 0, 0, g["Ws_vlin"][0:S])
    put("o2s", 0, S, g["Wv_vlin"][0:S])
    put("o2s", S, S + V, g["Ws_vlin"][S:], 1 / r3)
    put3("o2v", g["Wv_vlin"][S:S + V])
    put3("o2v", g["Wv_vlin"][S + V:], 1 / r2, c0=V3)
    put("fs", 0, 0, g["Wps"])
    put3("fv", g["Wpv"])
    put("adot", 0, 0, np.broadcast_to(g["alpha_dot"].reshape(1, S), (P, S)))
    for r0 in (0, S):
        put("cols", r0, 0, g["gamma_s"][:, None])
        put("cols", r0, 1, g["beta_s"][:, None])
    put("cols", 0, 2, np.concatenate([np.repeat(g["gamma_v"], 3), g["gamma_v"]])[:, None])
    put("cols", 0, 3, np.concatenate([g["w2_ss"], g["w2_vv0"]])[:, None])
    put("cols", 0, 4, np.concatenate([g["w2_vs"]] * 3)[:, None])
    put("cols", 0, 5, np.concatenate([g["w2_vv1"]] * 3)[:, None])
    put("cols", 0, 6, g["w2_sv"][:, None])

    def conv(L, ls, lv, fc1, fc2, os_, ov, ns, nv, c_h, c_hv, c_fc1, c_fc2, c_s, c_dot, c_b, c_v, c_x, c_ns, c_nv):
        if L == 3:
            put("hs3", 0, 0, ls, c_h)
            put("hs3", 0, S, ls, c_h)
        else:
            put(f"hs{L}", 0, 0, ls, c_h)
            put(f"hs{L}", S, S, ls, c_h)
        put3(f"hv{L}", lv, c_hv, inner=True)
        put(f"fc{L}", 0, 0, fc1, c_fc1)
        put(f"wab{L}", 0, 0, fc2[:, 0:2 * S], c_fc2)
        put(f"w34{L}", 0, 0, rep(fc2[:, 2 * S:2 * S + V]), c_fc2)
        put(f"w34{L}", 0, V3, fc2[:, 2 * S + V:2 * S + 2 * V], c_fc2)
        if L != 2:
            put(f"w5{L}", 0, 0, rep(fc2[:, 2 * S + 2 * V:]), c_fc2)
        put(f"oab{L}", 0, 0, os_[0], c_s)
        put(f"oab{L}", S, os_[0].shape[1], ov[0], c_b)
        put(f"of{L}", V3, 0, os_[1], c_dot)
        put3(f"oc{L}", ov[1], c_v)
        if L != 2:
            put3(f"od{L}", ov[2], c_x)
        put(f"ns{L}", 0, 0, ns, c_ns)
        put3(f"nv{L}", nv, c_nv, inner=True)

    g = {k[7:]: v for k, v in get.items() if k.startswith("L1_gnn_")}
    s96, s128 = 96.0 ** -0.5 / 4, 128.0 ** -0.5 / 4
    conv(1, g["lin1_ws"], g["lin1_wv"], g["fc_w1"], g["fc_w2"], (g["lin2_ws"][0:S], g["lin2_ws"][S:]),
         (g["lin2_wv"][0:S], g["lin2_wv"][S:S + V], g["lin2_wv"][S + V:]), g["sc_ws"], g["sc_wv"],
         1 / 8, 32.0 ** -0.5, 1 / 8, 1 / 8, s96, s96 / r3, s128, s128, s128 / r2, 1 / 8, 32.0 ** -0.5)
    g = {k[7:]: v for k, v in get.items() if k.startswith("L2_gnn_")}
    o = 0.5 / 4 * 96.0 ** -0.5
    conv(2, g["W_l1_0"], g["W_l1_1"], g["W_fc1"], g["W_fc2"], (g["W_l2_00"], g["W_l2_10"]), (g["W_l2_01"], g["W_l2_11"]),
         g["W_si0"], g["W_si1"], 1 / 8, 32.0 ** -0.5, 10.0 ** -0.5, r2 / 10, o, o / r3, o, o, o, 1 / 8, 32.0 ** -0.5)
    g = {k[7:]: v for k, v in get.items() if k.startswith("L3_gnn_")}
    conv(3, g["W_nl0"], g["W_nl1"], g["W_fc1"], g["W_fc2"], (g["W_out_s"][0:S], g["W_out_s"][S:]),
         (g["W_out_v"][0:S], g["W_out_v"][S:S + V], g["W_out_v"][S + V:]), g["W_skip0"], g["W_skip1"],
         1.0, 1.0, 1.0, 1.0, 1 / 32, 1 / 32, r3 / 32, 1 / 32, r3 / r2 / 32, 1.0, 1.0)
    return wt, sc


def constants():
    import numpy as np
    k = np.zeros((P, KW), np.float32)
    k[:, K_ID:K_ID + P] = np.eye(P)
    k[:, K_TRI:K_TRI + P] = np.tri(P, P, -1)
    k[:, K_TRIU:K_TRIU + P] = np.tri(P, P, -1).T
    k[:, K_ONE:K_ONE + P] = 1.0
    k[:, K_IOTA:K_IOTA + NJ] = np.arange(NJ)
    k[:, K_PIDX] = np.arange(P)
    k[P - 1, K_LAST] = 1.0
    k[:, K_HALF:K_HALF + 16] = -0.5
    return k


def kernel(**inputs):
    import numpy as np
    import concourse.bacc as bacc
    from concourse.bass_utils import run_bass_kernel_spmd

    get = {k: np.asarray(inputs[k]) for k in ("x", "src", "dst", "edge_attr_10", "edge_attr_16", "edge_attr_3",
                                              "edge_attr_4", "edge_attr_64", "node_vec1")}
    x = np.zeros((NP, XW), np.float32)
    x[0:N, 0:C] = get["x"]
    x[0:N, C:C + 1] = get["node_vec1"]
    attr = np.zeros((EP, AW), np.float32)
    attr[:, A3:A3 + 3] = 1.0
    for at, name in ((A64, "edge_attr_64"), (A4, "edge_attr_4"), (A10, "edge_attr_10"), (A16, "edge_attr_16"), (A3, "edge_attr_3")):
        attr[0:E, at:at + get[name].shape[1]] = get[name]
    ends = attr.view(np.int32)
    ends[:, ASRC] = ends[:, ADST] = N
    ends[0:E, ASRC], ends[0:E, ADST] = get["src"], get["dst"]
    keys = np.full((2, EP), N, np.int32)
    keys[0, 0:E], keys[1, 0:E] = get["dst"], get["src"]
    keys = np.ascontiguousarray(keys.reshape(2, ET, P).transpose(2, 0, 1))
    wt, sc = pack(inputs)

    nc = bacc.Bacc("TRN2", target_bir_lowering=False, num_devices=1)
    arrays = {"x_in": x, "attr_in": attr, "keys_in": keys, "w_in": wt, "wscale_in": sc, "const_in": constants()}
    args = [nc.dram_tensor(k, a.shape, mybir.dt.from_np(a.dtype), kind="ExternalInput").ap() for k, a in arrays.items()]
    out = nc.dram_tensor("out", (NP, C), F32, kind="ExternalOutput").ap()
    build(nc, *args, out)
    r = run_bass_kernel_spmd(nc, [arrays], core_ids=[0])
    return r.results[0]["out"][0:N]
```
